# Optimizing a Trainium2 kernel written in Bass

```python
import numpy as np
import jax
import jax.numpy as jnp

def _softmax(x, axis=-1):
    return jax.nn.softmax(x, axis=axis)

def _gelu(x):
    return jax.nn.gelu(x, approximate=True)

def _silu(x):
    return jax.nn.silu(x)

def _sigmoid(x):
    return jax.nn.sigmoid(x)

def _layernorm(x, axis=-1, eps=1e-05):
    m = jnp.mean(x, axis=axis, keepdims=True)
    v = jnp.var(x, axis=axis, keepdims=True)
    return (x - m) / jnp.sqrt(v + eps)

def _scatter_add(tgt, idx, src, axis=0):
    return tgt.at[idx].add(src)

def _segment_sum(src, seg, n):
    return jax.ops.segment_sum(src, seg, n)
kernel_name = 'mk_flamingo_gated_d4_seqx_r8_c0e18e'

def setup_inputs(seed: int=0):
    np.random.seed(seed)
    _w = jnp.asarray

    def _rec_inputs():
        import jax
        import jax.numpy as jnp
        _rk = jax.random.key(seed)
        x = 7.22e-05 + 1 * jax.random.normal(jax.random.fold_in(_rk, 1), (16, 128, 128), jnp.float32)
        _lenS = 128 - jax.random.randint(jax.random.fold_in(_rk, 7), (16,), 0, max(1, 128 // 4) + 1, jnp.int32)
        _lenS2 = 77 - jax.random.randint(jax.random.fold_in(_rk, 8), (16,), 0, max(1, 77 // 4) + 1, jnp.int32)
        _ctx_1024P = jax.random.normal(jax.random.fold_in(_rk, 11), (16, 16, 128), jnp.float32)
        _ctx_1024c = jax.random.dirichlet(jax.random.fold_in(_rk, 511), 0.3 * jnp.ones((16,), jnp.float32), (16, 77))
        _ctx_1024t = jnp.einsum('bsk,bkd->bsd', _ctx_1024c, _ctx_1024P)
        _ctx_1024t = _ctx_1024t * jax.lax.rsqrt(jnp.mean(jnp.square(_ctx_1024t)) + 1e-12) * 0.953939
        ctx_1024 = 4.13588e-05 + 0.999923 * (_ctx_1024t + 0.3 * jax.random.normal(jax.random.fold_in(_rk, 611), (16, 77, 128), jnp.float32))
        fside_SxS2_0 = 0.000675642 + 1.00031 * jax.random.normal(jax.random.fold_in(_rk, 12), (128, 77), jnp.float32)
        _g = jax.random.normal(jax.random.fold_in(_rk, 9001), (2, 4), jnp.float32)
        _g = jnp.sign(_g) * jnp.maximum(jnp.abs(_g), 1.0) + (_g == 0) * 1.0
        g_xattn = _g[0]
        g_ffn = _g[1]
        return (x, ctx_1024, fside_SxS2_0, g_xattn, g_ffn)
    x, ctx_1024, fside_SxS2_0, g_xattn, g_ffn = _rec_inputs()

    def _L0_xattn_setup():
        import jax, jax.numpy as jnp
        import numpy as np
        key = jax.random.key(seed)
        k1, k2, k3, k4, k5 = jax.random.split(key, 5)
        b, t, e, h = (4, 256, 128, 16)
        d = e // h
        return {'queries': jax.random.normal(k1, (b, t, e), dtype=jnp.float32), 'keys': jax.random.normal(k2, (b, t, e), dtype=jnp.float32), 'values': jax.random.normal(k3, (b, t, e), dtype=jnp.float32), 'W1': jax.random.normal(k4, (d, d), dtype=jnp.float32) * (1.0 / np.sqrt(d)), 'W2': jax.random.normal(k5, (e, e), dtype=jnp.float32) * (1.0 / np.sqrt(e)), 'num_heads': 16}
    _L0_xattn_all = _L0_xattn_setup()
    _L0_xattn_in = {k: v for k, v in _L0_xattn_all.items() if k in ('W1', 'W2')}
    del _L0_xattn_all

    def _L0_ffn_setup():
        import jax, jax.numpy as jnp
        import numpy as np
        DIM = 128
        DEPTH = 6
        HEADS = 16
        DIM_HEAD = 64
        WINDOW = 32
        INNER = HEADS * DIM_HEAD
        DIM_INNER = int(DIM * 4 * 2 / 3)
        QK_SCALE = 8.0

        def shift_tokens(t):
            a, s = jnp.split(t, 2, -1)
            s = jnp.pad(s, ((0, 0), (1, 0), (0, 0)))[:, :-1]
            return jnp.concatenate([a, s], -1)

        def l2norm(t):
            return t / jnp.maximum(jnp.linalg.norm(t, axis=-1, keepdims=True), 1e-12)

        def rotate_half(x):
            x1, x2 = jnp.split(x, 2, -1)
            return jnp.concatenate([-x2, x1], -1)

        def rotary_tables(n):
            half = jnp.arange(0, DIM_HEAD, 2, dtype=jnp.float32)
            inv_freq = 1.0 / 10000.0 ** (half / DIM_HEAD)
            t = jnp.arange(n, dtype=jnp.float32)
            freqs = t[:, None] * inv_freq[None, :]
            freqs = jnp.concatenate([freqs, freqs], -1)
            base_scale = (half + 0.4 * DIM_HEAD) / (1.4 * DIM_HEAD)
            power = (t - n // 2) / (WINDOW // 2)
            scale = base_scale[None, :] ** power[:, None]
            scale = jnp.concatenate([scale, scale], -1)
            return (freqs, scale)

        def local_attention(q, k, v):
            b, h, n, d = q.shape
            w = WINDOW
            nw = n // w
            bq = q.reshape(b, h, nw, w, d)
            bk = k.reshape(b, h, nw, w, d)
            bv = v.reshape(b, h, nw, w, d)

            def look(t):
                p = jnp.pad(t, ((0, 0), (0, 0), (1, 0), (0, 0), (0, 0)))
                return jnp.concatenate([p[:, :, :nw], p[:, :, 1:]], axis=3)
            bk2, bv2 = (look(bk), look(bv))
            seq = jnp.arange(n).reshape(nw, w)
            seq_p = jnp.pad(seq, ((1, 0), (0, 0)), constant_values=-1)
            jt = jnp.concatenate([seq_p[:nw], seq_p[1:]], axis=1)
            it = seq[:, :, None]
            jb = jt[:, None, :]
            mask = (it < jb) | (it > jb + w) | (jb == -1)
            sim = jnp.einsum('bhwie,bhwje->bhwij', bq, bk2) * QK_SCALE
            sim = jnp.where(mask, -jnp.finfo(sim.dtype).max, sim)
            attn = jax.nn.softmax(sim, -1)
            out = jnp.einsum('bhwij,bhwje->bhwie', attn, bv2)
            return out.reshape(b, h, n, d)

        def attn_layer(x, Wqkv, qs, ksc, Wo):
            b, n, _ = x.shape
            qkv = x @ Wqkv
            q, k, v = jnp.split(qkv, 3, -1)
            sh = lambda t: t.reshape(b, n, HEADS, DIM_HEAD).transpose(0, 2, 1, 3)
            q, k, v = (sh(q), sh(k), sh(v))
            q = l2norm(q) * qs
            k = l2norm(k) * ksc
            freqs, scale = rotary_tables(n)
            cos, sin = (jnp.cos(freqs), jnp.sin(freqs))
            q = q * cos * scale + rotate_half(q) * sin * scale
            inv = 1.0 / scale
            k = k * cos * inv + rotate_half(k) * sin * inv
            out = local_attention(q, k, v)
            out = out.transpose(0, 2, 1, 3).reshape(b, n, INNER)
            return out @ Wo

        def ffn_layer(x, g, bln, W1, b1, W2, b2):
            mu = x.mean(-1, keepdims=True)
            var = ((x - mu) ** 2).mean(-1, keepdims=True)
            xn = (x - mu) / jnp.sqrt(var + 1e-05) * g + bln
            hg = xn @ W1 + b1
            a, gate = jnp.split(hg, 2, -1)
            return a * jax.nn.gelu(gate, approximate=False) @ W2 + b2
        key = jax.random.key(seed)
        ks = jax.random.split(key, 8)
        B, N = (2, 256)
        init = lambda k, shape: jax.random.normal(k, shape, jnp.float32) * 0.02
        return {'x': jax.random.normal(ks[0], (B, N, DIM), jnp.float32), 'Wqkv': init(ks[1], (DEPTH, DIM, 3 * INNER)), 'q_scale': jnp.ones((DEPTH, DIM_HEAD), jnp.float32), 'k_scale': jnp.ones((DEPTH, DIM_HEAD), jnp.float32), 'Wo': init(ks[2], (DEPTH, INNER, DIM)), 'ln_g': jnp.ones((DEPTH, DIM), jnp.float32), 'ln_b': jnp.zeros((DEPTH, DIM), jnp.float32), 'W1': init(ks[3], (DEPTH, DIM, 2 * DIM_INNER)), 'b1': jnp.zeros((DEPTH, 2 * DIM_INNER), jnp.float32), 'W2': init(ks[4], (DEPTH, DIM_INNER, DIM)), 'b2': jnp.zeros((DEPTH, DIM), jnp.float32)}
    _L0_ffn_all = _L0_ffn_setup()
    _L0_ffn_in = {k: v for k, v in _L0_ffn_all.items() if k in ('Wqkv', 'q_scale', 'k_scale', 'Wo', 'ln_g', 'ln_b', 'W1', 'b1', 'W2', 'b2')}
    del _L0_ffn_all

    def _L1_xattn_setup():
        import jax, jax.numpy as jnp
        import numpy as np
        DIM = 128
        DIM_VISUAL = 128
        DIM_HEAD = 64
        HEADS = 8
        INNER = DIM_HEAD * HEADS

        def _layer_norm(x, scale, bias, eps=1e-05):
            mu = jnp.mean(x, axis=-1, keepdims=True)
            var = jnp.mean(jnp.square(x - mu), axis=-1, keepdims=True)
            return (x - mu) * jax.lax.rsqrt(var + eps) * scale + bias
        key = jax.random.key(seed)
        ks = jax.random.split(key, 7)
        B, Ttxt, Timg = (4, 256, 256)
        x = jax.random.normal(ks[0], (B, Ttxt, DIM), dtype=jnp.float32)
        y = jax.random.normal(ks[1], (B, Timg, DIM_VISUAL), dtype=jnp.float32)
        ln_scale = jnp.ones((DIM,), dtype=jnp.float32)
        ln_bias = jnp.zeros((DIM,), dtype=jnp.float32)
        Wq = jax.random.normal(ks[2], (DIM, INNER), dtype=jnp.float32) / np.sqrt(DIM)
        Wkv = jax.random.normal(ks[3], (DIM_VISUAL, 2 * INNER), dtype=jnp.float32) / np.sqrt(DIM_VISUAL)
        Wo = jax.random.normal(ks[4], (INNER, DIM), dtype=jnp.float32) / np.sqrt(INNER)
        return {'x': x, 'y': y, 'ln_scale': ln_scale, 'ln_bias': ln_bias, 'Wq': Wq, 'Wkv': Wkv, 'Wo': Wo}
    _L1_xattn_all = _L1_xattn_setup()
    _L1_xattn_in = {k: v for k, v in _L1_xattn_all.items() if k in ('ln_scale', 'ln_bias', 'Wq', 'Wkv', 'Wo')}
    del _L1_xattn_all

    def _L1_ffn_setup():
        import jax, jax.numpy as jnp
        import numpy as np
        EPS = 1e-09
        key = jax.random.key(seed)
        k1, k2, k3, k4 = jax.random.split(key, 4)
        B, T, H, D, E = (2, 256, 128, 128, 8)
        x = jax.random.normal(k1, (B, T, H), dtype=jnp.float32)
        gate_w = jax.random.normal(k2, (E, H), dtype=jnp.float32) * 0.02
        gate_up_proj = jax.random.normal(k3, (E, H, 2 * D), dtype=jnp.float32) * 0.02
        down_proj = jax.random.normal(k4, (E, D, H), dtype=jnp.float32) * 0.02
        return {'x': x, 'gate_w': gate_w, 'gate_up_proj': gate_up_proj, 'down_proj': down_proj}
    _L1_ffn_all = _L1_ffn_setup()
    _L1_ffn_in = {k: v for k, v in _L1_ffn_all.items() if k in ('gate_w', 'gate_up_proj', 'down_proj')}
    del _L1_ffn_all

    def _L2_xattn_setup():
        import jax, jax.numpy as jnp
        import numpy as np
        E = 128
        H = 16
        D = E // H
        SCALING = float(D * 1.0) ** (-0.5)
        key = jax.random.key(seed)
        ks = jax.random.split(key, 10)
        B, L, S = (4, 256, 256)
        query = jax.random.normal(ks[0], (B, L, E), dtype=jnp.float32)
        k_in = jax.random.normal(ks[1], (B, S, E), dtype=jnp.float32)
        v_in = jax.random.normal(ks[2], (B, S, E), dtype=jnp.float32)
        attn_bias = jax.random.normal(ks[3], (L, S), dtype=jnp.float32)
        attn_mask = jax.random.normal(ks[4], (L, S), dtype=jnp.float32)
        lim_in = np.sqrt(6.0 / (E + 3 * E))
        Wqkv = jax.random.uniform(ks[5], (3 * E, E), minval=-lim_in, maxval=lim_in, dtype=jnp.float32)
        bqkv = jnp.zeros((3 * E,), dtype=jnp.float32)
        lim_out = np.sqrt(1.0 / E)
        Wo = jax.random.uniform(ks[6], (E, E), minval=-lim_out, maxval=lim_out, dtype=jnp.float32)
        bo = jnp.zeros((E,), dtype=jnp.float32)
        return {'query': query, 'key': k_in, 'value': v_in, 'attn_bias': attn_bias, 'attn_mask': attn_mask, 'Wqkv': Wqkv, 'bqkv': bqkv, 'Wo': Wo, 'bo': bo}
    _L2_xattn_all = _L2_xattn_setup()
    _L2_xattn_in = {k: v for k, v in _L2_xattn_all.items() if k in ('Wqkv', 'bqkv', 'Wo', 'bo')}
    del _L2_xattn_all

    def _L2_ffn_setup():
        import jax, jax.numpy as jnp
        import numpy as np
        B, S, H, I, E_ROUTED, TOP_K = (8, 256, 128, 256, 8, 2)

        def _expert(x, Wg, Wu, Wd):
            return jax.nn.silu(x @ Wg.T) * (x @ Wu.T) @ Wd.T
        key = jax.random.key(seed)
        ks = jax.random.split(key, 9)
        s = 0.02
        return {'x': jax.random.normal(ks[0], (B, S, H), dtype=jnp.float32), 'Wg_s': jax.random.normal(ks[1], (I, H), dtype=jnp.float32) * s, 'Wu_s': jax.random.normal(ks[2], (I, H), dtype=jnp.float32) * s, 'Wd_s': jax.random.normal(ks[3], (H, I), dtype=jnp.float32) * s, 'Wg': jax.random.normal(ks[4], (E_ROUTED, I, H), dtype=jnp.float32) * s, 'Wu': jax.random.normal(ks[5], (E_ROUTED, I, H), dtype=jnp.float32) * s, 'Wd': jax.random.normal(ks[6], (E_ROUTED, H, I), dtype=jnp.float32) * s, 'Wr': jax.random.normal(ks[7], (E_ROUTED, H), dtype=jnp.float32) * s, 'rb': jnp.zeros((E_ROUTED,), dtype=jnp.float32)}
    _L2_ffn_all = _L2_ffn_setup()
    _L2_ffn_in = {k: v for k, v in _L2_ffn_all.items() if k in ('Wg_s', 'Wu_s', 'Wd_s', 'Wg', 'Wu', 'Wd', 'Wr', 'rb')}
    del _L2_ffn_all

    def _L3_xattn_setup():
        import jax, jax.numpy as jnp
        import numpy as np
        HEADS = 8
        DIM_HEAD = 64
        SCALE = 8.0
        EPS = 1e-05

        def layer_norm(x, g, b):
            mu = jnp.mean(x, axis=-1, keepdims=True)
            var = jnp.mean((x - mu) ** 2, axis=-1, keepdims=True)
            return (x - mu) * jax.lax.rsqrt(var + EPS) * g + b
        key = jax.random.key(seed)
        ks = jax.random.split(key, 6)
        b, n, dim = (4, 512, 128)
        inner = HEADS * DIM_HEAD
        return {'x': jax.random.normal(ks[0], (b, n, dim), jnp.float32), 'context': jax.random.normal(ks[1], (b, n, dim), jnp.float32), 'Wq': jax.random.normal(ks[2], (dim, inner), jnp.float32) * 0.03, 'Wkv': jax.random.normal(ks[3], (dim, 2 * inner), jnp.float32) * 0.03, 'null_kv': jax.random.normal(ks[4], (2, DIM_HEAD), jnp.float32), 'ln_q_g': jnp.ones((inner,), jnp.float32), 'ln_q_b': jnp.zeros((inner,), jnp.float32), 'ln_out_g': jnp.ones((inner,), jnp.float32), 'ln_out_b': jnp.zeros((inner,), jnp.float32), 'Wout': jax.random.normal(ks[5], (inner, dim), jnp.float32) * 0.03}
    _L3_xattn_all = _L3_xattn_setup()
    _L3_xattn_in = {k: v for k, v in _L3_xattn_all.items() if k in ('Wq', 'Wkv', 'null_kv', 'ln_q_g', 'ln_q_b', 'ln_out_g', 'ln_out_b', 'Wout')}
    del _L3_xattn_all

    def _L3_ffn_setup():
        import jax, jax.numpy as jnp
        import numpy as np
        D_MODEL = 128
        D_FF = 512
        NUM_EXPERTS = 8
        B, N = (16, 128)
        key = jax.random.key(seed)
        ks = jax.random.split(key, 7)
        s_in = 1.0 / np.sqrt(D_MODEL)
        s_ff = 1.0 / np.sqrt(D_FF)
        return {'x': jax.random.normal(ks[0], (B, N, D_MODEL), dtype=jnp.float32), 'Wr': jax.random.uniform(ks[1], (D_MODEL, NUM_EXPERTS), jnp.float32, -s_in, s_in), 'br': jax.random.uniform(ks[2], (NUM_EXPERTS,), jnp.float32, -s_in, s_in), 'W1': jax.random.uniform(ks[3], (NUM_EXPERTS, D_MODEL, D_FF), jnp.float32, -s_in, s_in), 'b1': jax.random.uniform(ks[4], (NUM_EXPERTS, D_FF), jnp.float32, -s_in, s_in), 'W2': jax.random.uniform(ks[5], (NUM_EXPERTS, D_FF, D_MODEL), jnp.float32, -s_ff, s_ff), 'b2': jax.random.uniform(ks[6], (NUM_EXPERTS, D_MODEL), jnp.float32, -s_ff, s_ff)}
    _L3_ffn_all = _L3_ffn_setup()
    _L3_ffn_in = {k: v for k, v in _L3_ffn_all.items() if k in ('Wr', 'br', 'W1', 'b1', 'W2', 'b2')}
    del _L3_ffn_all
    return {'x': x, 'ctx_1024': ctx_1024, 'fside_SxS2_0': fside_SxS2_0, 'g_xattn': g_xattn, 'g_ffn': g_ffn, 'L0_xattn_W1': _L0_xattn_in['W1'], 'L0_xattn_W2': _L0_xattn_in['W2'], 'L0_ffn_Wqkv': _L0_ffn_in['Wqkv'], 'L0_ffn_q_scale': _L0_ffn_in['q_scale'], 'L0_ffn_k_scale': _L0_ffn_in['k_scale'], 'L0_ffn_Wo': _L0_ffn_in['Wo'], 'L0_ffn_ln_g': _L0_ffn_in['ln_g'], 'L0_ffn_ln_b': _L0_ffn_in['ln_b'], 'L0_ffn_W1': _L0_ffn_in['W1'], 'L0_ffn_b1': _L0_ffn_in['b1'], 'L0_ffn_W2': _L0_ffn_in['W2'], 'L0_ffn_b2': _L0_ffn_in['b2'], 'L1_xattn_ln_scale': _L1_xattn_in['ln_scale'], 'L1_xattn_ln_bias': _L1_xattn_in['ln_bias'], 'L1_xattn_Wq': _L1_xattn_in['Wq'], 'L1_xattn_Wkv': _L1_xattn_in['Wkv'], 'L1_xattn_Wo': _L1_xattn_in['Wo'], 'L1_ffn_gate_w': _L1_ffn_in['gate_w'], 'L1_ffn_gate_up_proj': _L1_ffn_in['gate_up_proj'], 'L1_ffn_down_proj': _L1_ffn_in['down_proj'], 'L2_xattn_Wqkv': _L2_xattn_in['Wqkv'], 'L2_xattn_bqkv': _L2_xattn_in['bqkv'], 'L2_xattn_Wo': _L2_xattn_in['Wo'], 'L2_xattn_bo': _L2_xattn_in['bo'], 'L2_ffn_Wg_s': _L2_ffn_in['Wg_s'], 'L2_ffn_Wu_s': _L2_ffn_in['Wu_s'], 'L2_ffn_Wd_s': _L2_ffn_in['Wd_s'], 'L2_ffn_Wg': _L2_ffn_in['Wg'], 'L2_ffn_Wu': _L2_ffn_in['Wu'], 'L2_ffn_Wd': _L2_ffn_in['Wd'], 'L2_ffn_Wr': _L2_ffn_in['Wr'], 'L2_ffn_rb': _L2_ffn_in['rb'], 'L3_xattn_Wq': _L3_xattn_in['Wq'], 'L3_xattn_Wkv': _L3_xattn_in['Wkv'], 'L3_xattn_null_kv': _L3_xattn_in['null_kv'], 'L3_xattn_ln_q_g': _L3_xattn_in['ln_q_g'], 'L3_xattn_ln_q_b': _L3_xattn_in['ln_q_b'], 'L3_xattn_ln_out_g': _L3_xattn_in['ln_out_g'], 'L3_xattn_ln_out_b': _L3_xattn_in['ln_out_b'], 'L3_xattn_Wout': _L3_xattn_in['Wout'], 'L3_ffn_Wr': _L3_ffn_in['Wr'], 'L3_ffn_br': _L3_ffn_in['br'], 'L3_ffn_W1': _L3_ffn_in['W1'], 'L3_ffn_b1': _L3_ffn_in['b1'], 'L3_ffn_W2': _L3_ffn_in['W2'], 'L3_ffn_b2': _L3_ffn_in['b2']}

def reference(x, ctx_1024, fside_SxS2_0, g_xattn, g_ffn, L0_xattn_W1, L0_xattn_W2, L0_ffn_Wqkv, L0_ffn_q_scale, L0_ffn_k_scale, L0_ffn_Wo, L0_ffn_ln_g, L0_ffn_ln_b, L0_ffn_W1, L0_ffn_b1, L0_ffn_W2, L0_ffn_b2, L1_xattn_ln_scale, L1_xattn_ln_bias, L1_xattn_Wq, L1_xattn_Wkv, L1_xattn_Wo, L1_ffn_gate_w, L1_ffn_gate_up_proj, L1_ffn_down_proj, L2_xattn_Wqkv, L2_xattn_bqkv, L2_xattn_Wo, L2_xattn_bo, L2_ffn_Wg_s, L2_ffn_Wu_s, L2_ffn_Wd_s, L2_ffn_Wg, L2_ffn_Wu, L2_ffn_Wd, L2_ffn_Wr, L2_ffn_rb, L3_xattn_Wq, L3_xattn_Wkv, L3_xattn_null_kv, L3_xattn_ln_q_g, L3_xattn_ln_q_b, L3_xattn_ln_out_g, L3_xattn_ln_out_b, L3_xattn_Wout, L3_ffn_Wr, L3_ffn_br, L3_ffn_W1, L3_ffn_b1, L3_ffn_W2, L3_ffn_b2):
    import jax
    import jax.numpy as jnp

    def _L0_xattn_ref(queries, keys, values, W1, W2, num_heads):
        import jax, jax.numpy as jnp
        import numpy as np
        b, t2, e = queries.shape
        t = values.shape[1]
        h = num_heads
        d = e // h
        qh = jnp.einsum('bqhd,ed->bqhe', queries.reshape(b, t2, h, d), W1)
        kh = jnp.einsum('bkhd,ed->bkhe', keys.reshape(b, t, h, d), W1)
        vh = jnp.einsum('bkhd,ed->bkhe', values.reshape(b, t, h, d), W1)
        scores = jnp.einsum('bqhd,bkhd->bhqk', qh, kh) / jnp.sqrt(jnp.asarray(d, dtype=qh.dtype))
        causal = jnp.arange(t)[None, :] > jnp.arange(t2)[:, None]
        scores = jnp.where(causal[None, None, :, :], -jnp.inf, scores)
        soft = jax.nn.softmax(scores, axis=-1)
        ctx = jnp.einsum('bhqk,bkhd->bqhd', soft, vh).reshape(b, t2, e)
        return ctx @ W2.T

    def _L0_ffn_ref(x, Wqkv, q_scale, k_scale, Wo, ln_g, ln_b, W1, b1, W2, b2):
        import jax, jax.numpy as jnp
        import numpy as np
        DIM = 128
        DEPTH = 6
        HEADS = 16
        DIM_HEAD = 64
        WINDOW = 32
        INNER = HEADS * DIM_HEAD
        DIM_INNER = int(DIM * 4 * 2 / 3)
        QK_SCALE = 8.0

        def shift_tokens(t):
            a, s = jnp.split(t, 2, -1)
            s = jnp.pad(s, ((0, 0), (1, 0), (0, 0)))[:, :-1]
            return jnp.concatenate([a, s], -1)

        def l2norm(t):
            return t / jnp.maximum(jnp.linalg.norm(t, axis=-1, keepdims=True), 1e-12)

        def rotate_half(x):
            x1, x2 = jnp.split(x, 2, -1)
            return jnp.concatenate([-x2, x1], -1)

        def rotary_tables(n):
            half = jnp.arange(0, DIM_HEAD, 2, dtype=jnp.float32)
            inv_freq = 1.0 / 10000.0 ** (half / DIM_HEAD)
            t = jnp.arange(n, dtype=jnp.float32)
            freqs = t[:, None] * inv_freq[None, :]
            freqs = jnp.concatenate([freqs, freqs], -1)
            base_scale = (half + 0.4 * DIM_HEAD) / (1.4 * DIM_HEAD)
            power = (t - n // 2) / (WINDOW // 2)
            scale = base_scale[None, :] ** power[:, None]
            scale = jnp.concatenate([scale, scale], -1)
            return (freqs, scale)

        def local_attention(q, k, v):
            b, h, n, d = q.shape
            w = WINDOW
            nw = n // w
            bq = q.reshape(b, h, nw, w, d)
            bk = k.reshape(b, h, nw, w, d)
            bv = v.reshape(b, h, nw, w, d)

            def look(t):
                p = jnp.pad(t, ((0, 0), (0, 0), (1, 0), (0, 0), (0, 0)))
                return jnp.concatenate([p[:, :, :nw], p[:, :, 1:]], axis=3)
            bk2, bv2 = (look(bk), look(bv))
            seq = jnp.arange(n).reshape(nw, w)
            seq_p = jnp.pad(seq, ((1, 0), (0, 0)), constant_values=-1)
            jt = jnp.concatenate([seq_p[:nw], seq_p[1:]], axis=1)
            it = seq[:, :, None]
            jb = jt[:, None, :]
            mask = (it < jb) | (it > jb + w) | (jb == -1)
            sim = jnp.einsum('bhwie,bhwje->bhwij', bq, bk2) * QK_SCALE
            sim = jnp.where(mask, -jnp.finfo(sim.dtype).max, sim)
            attn = jax.nn.softmax(sim, -1)
            out = jnp.einsum('bhwij,bhwje->bhwie', attn, bv2)
            return out.reshape(b, h, n, d)

        def attn_layer(x, Wqkv, qs, ksc, Wo):
            b, n, _ = x.shape
            qkv = x @ Wqkv
            q, k, v = jnp.split(qkv, 3, -1)
            sh = lambda t: t.reshape(b, n, HEADS, DIM_HEAD).transpose(0, 2, 1, 3)
            q, k, v = (sh(q), sh(k), sh(v))
            q = l2norm(q) * qs
            k = l2norm(k) * ksc
            freqs, scale = rotary_tables(n)
            cos, sin = (jnp.cos(freqs), jnp.sin(freqs))
            q = q * cos * scale + rotate_half(q) * sin * scale
            inv = 1.0 / scale
            k = k * cos * inv + rotate_half(k) * sin * inv
            out = local_attention(q, k, v)
            out = out.transpose(0, 2, 1, 3).reshape(b, n, INNER)
            return out @ Wo

        def ffn_layer(x, g, bln, W1, b1, W2, b2):
            mu = x.mean(-1, keepdims=True)
            var = ((x - mu) ** 2).mean(-1, keepdims=True)
            xn = (x - mu) / jnp.sqrt(var + 1e-05) * g + bln
            hg = xn @ W1 + b1
            a, gate = jnp.split(hg, 2, -1)
            return a * jax.nn.gelu(gate, approximate=False) @ W2 + b2
        for i in range(DEPTH):
            x = attn_layer(shift_tokens(x), Wqkv[i], q_scale[i], k_scale[i], Wo[i]) + x
            x = ffn_layer(shift_tokens(x), ln_g[i], ln_b[i], W1[i], b1[i], W2[i], b2[i]) + x
        return x

    def _L1_xattn_ref(x, y, ln_scale, ln_bias, Wq, Wkv, Wo):
        import jax, jax.numpy as jnp
        import numpy as np
        DIM = 128
        DIM_VISUAL = 128
        DIM_HEAD = 64
        HEADS = 8
        INNER = DIM_HEAD * HEADS

        def _layer_norm(x, scale, bias, eps=1e-05):
            mu = jnp.mean(x, axis=-1, keepdims=True)
            var = jnp.mean(jnp.square(x - mu), axis=-1, keepdims=True)
            return (x - mu) * jax.lax.rsqrt(var + eps) * scale + bias
        B, Ttxt, _ = x.shape
        _, Timg, _ = y.shape
        h, d = (HEADS, DIM_HEAD)
        scale = d ** (-0.5)
        xn = _layer_norm(x, ln_scale, ln_bias)
        q = xn @ Wq
        kv = y @ Wkv
        k, v = jnp.split(kv, 2, axis=-1)
        q = q.reshape(B, Ttxt, h, d).transpose(0, 2, 1, 3) * scale
        k = k.reshape(B, Timg, h, d).transpose(0, 2, 1, 3)
        v = v.reshape(B, Timg, h, d).transpose(0, 2, 1, 3)
        sim = jnp.einsum('bhid,bhjd->bhij', q, k)
        sim = sim - jax.lax.stop_gradient(jnp.max(sim, axis=-1, keepdims=True))
        attn = jax.nn.softmax(sim, axis=-1)
        out = jnp.einsum('bhij,bhjd->bhid', attn, v)
        out = out.transpose(0, 2, 1, 3).reshape(B, Ttxt, h * d)
        return out @ Wo

    def _L1_ffn_ref(x, gate_w, gate_up_proj, down_proj):
        import jax, jax.numpy as jnp
        import numpy as np
        EPS = 1e-09
        B, T, H = x.shape
        E = gate_w.shape[0]
        top_k = 2
        hidden = x.reshape(-1, H)
        router_logits = hidden @ gate_w.T
        routing_weights = jax.nn.softmax(router_logits.astype(jnp.float32), axis=-1)
        topk_weights, topk_indices = jax.lax.top_k(routing_weights, top_k)
        topk_weights = topk_weights / (jnp.sum(topk_weights, axis=-1, keepdims=True) + EPS)
        N = hidden.shape[0]
        routed = jnp.zeros((N, E), dtype=router_logits.dtype)
        rows = jnp.arange(N)[:, None]
        routed = routed.at[rows, topk_indices].set(topk_weights.astype(router_logits.dtype))
        routed = routed / (jnp.sum(routed, axis=-1, keepdims=True) + EPS)
        routed = routed.astype(hidden.dtype)
        gate_up = jnp.einsum('th,ehq->teq', hidden, gate_up_proj)
        gate, up = jnp.split(gate_up, 2, axis=-1)
        expert_outputs = jnp.einsum('teq,eqh->teh', jax.nn.silu(gate) * up, down_proj)
        out = jnp.sum(expert_outputs * routed[:, :, None], axis=1)
        return out.reshape(B, T, H)

    def _L2_xattn_ref(query, key, value, attn_bias, attn_mask, Wqkv, bqkv, Wo, bo):
        import jax, jax.numpy as jnp
        import numpy as np
        E = 128
        H = 16
        D = E // H
        SCALING = float(D * 1.0) ** (-0.5)
        B, L, _ = query.shape
        S = key.shape[1]
        q = query @ Wqkv[:E].T + bqkv[:E]
        k = key @ Wqkv[E:2 * E].T + bqkv[E:2 * E]
        v = value @ Wqkv[2 * E:].T + bqkv[2 * E:]
        q = q * SCALING
        q = q.reshape(B, L, H, D)
        k = k.reshape(B, S, H, D)
        v = v.reshape(B, S, H, D)
        scores = jnp.einsum('blhd,bshd->bhls', q, k)
        scores = scores + attn_mask[None, None] + attn_bias[None, None]
        weights = jax.nn.softmax(scores, axis=-1)
        out = jnp.einsum('bhls,bshd->blhd', weights, v).reshape(B, L, E)
        return out @ Wo.T + bo

    def _L2_ffn_ref(x, Wg_s, Wu_s, Wd_s, Wg, Wu, Wd, Wr, rb):
        import jax, jax.numpy as jnp
        import numpy as np
        B, S, H, I, E_ROUTED, TOP_K = (8, 256, 128, 256, 8, 2)

        def _expert(x, Wg, Wu, Wd):
            return jax.nn.silu(x @ Wg.T) * (x @ Wu.T) @ Wd.T
        shared = _expert(x, Wg_s, Wu_s, Wd_s)
        logits = jnp.einsum('bsh,eh->bse', x, Wr) + rb
        probs = jax.nn.sigmoid(logits)
        scores, idx = jax.lax.top_k(probs, TOP_K)
        cw = (jax.nn.one_hot(idx, E_ROUTED, dtype=x.dtype) * scores[..., None]).sum(-2)
        out = shared
        for e in range(E_ROUTED):
            out = out + cw[..., e:e + 1] * _expert(x, Wg[e], Wu[e], Wd[e])
        return out

    def _L3_xattn_ref(x, context, Wq, Wkv, null_kv, ln_q_g, ln_q_b, ln_out_g, ln_out_b, Wout):
        import jax, jax.numpy as jnp
        import numpy as np
        HEADS = 8
        DIM_HEAD = 64
        SCALE = 8.0
        EPS = 1e-05

        def layer_norm(x, g, b):
            mu = jnp.mean(x, axis=-1, keepdims=True)
            var = jnp.mean((x - mu) ** 2, axis=-1, keepdims=True)
            return (x - mu) * jax.lax.rsqrt(var + EPS) * g + b
        b, n, _ = x.shape
        m = context.shape[1]
        h, d = (HEADS, DIM_HEAD)
        q = x @ Wq
        kv = context @ Wkv
        k, v = jnp.split(kv, 2, axis=-1)
        q = layer_norm(q, ln_q_g, ln_q_b)
        split = lambda t: t.reshape(t.shape[0], t.shape[1], h, d).transpose(0, 2, 1, 3)
        q, k, v = (split(q), split(k), split(v))
        nk = jnp.broadcast_to(null_kv[0], (b, h, 1, d))
        nv = jnp.broadcast_to(null_kv[1], (b, h, 1, d))
        k = jnp.concatenate([nk, k], axis=2)
        v = jnp.concatenate([nv, v], axis=2)
        q = jax.nn.softmax(q, axis=-1) * SCALE
        k = jax.nn.softmax(k, axis=2)
        ctx = jnp.einsum('bhnd,bhne->bhde', k, v)
        out = jnp.einsum('bhnd,bhde->bhne', q, ctx)
        out = out.transpose(0, 2, 1, 3).reshape(b, n, h * d)
        out = layer_norm(out, ln_out_g, ln_out_b)
        return out @ Wout

    def _L3_ffn_ref(x, Wr, br, W1, b1, W2, b2):
        import jax, jax.numpy as jnp
        import numpy as np
        D_MODEL = 128
        D_FF = 512
        NUM_EXPERTS = 8
        B, N = (16, 128)
        scores = jnp.einsum('bh,he->be', x.mean(axis=1), Wr) + br
        top1 = jnp.argmax(scores, axis=-1)
        w1 = W1[top1]
        c1 = b1[top1]
        w2 = W2[top1]
        c2 = b2[top1]
        h = jax.nn.relu(jnp.einsum('bnh,bhf->bnf', x, w1) + c1[:, None, :])
        out = jnp.einsum('bnf,bfh->bnh', h, w2) + c2[:, None, :]
        return out
    x = x + jnp.tanh(g_xattn[0]) * _L0_xattn_ref(_layernorm(x, axis=-1), ctx_1024, ctx_1024, L0_xattn_W1, L0_xattn_W2, 16)
    x = x + jnp.tanh(g_ffn[0]) * _L0_ffn_ref(_layernorm(x, axis=-1), L0_ffn_Wqkv, L0_ffn_q_scale, L0_ffn_k_scale, L0_ffn_Wo, L0_ffn_ln_g, L0_ffn_ln_b, L0_ffn_W1, L0_ffn_b1, L0_ffn_W2, L0_ffn_b2)
    x = x + jnp.tanh(g_xattn[1]) * _L1_xattn_ref(_layernorm(x, axis=-1), ctx_1024, L1_xattn_ln_scale, L1_xattn_ln_bias, L1_xattn_Wq, L1_xattn_Wkv, L1_xattn_Wo)
    x = x + jnp.tanh(g_ffn[1]) * _L1_ffn_ref(_layernorm(x, axis=-1), L1_ffn_gate_w, L1_ffn_gate_up_proj, L1_ffn_down_proj)
    x = x + jnp.tanh(g_xattn[2]) * _L2_xattn_ref(_layernorm(x, axis=-1), ctx_1024, ctx_1024, fside_SxS2_0, fside_SxS2_0, L2_xattn_Wqkv, L2_xattn_bqkv, L2_xattn_Wo, L2_xattn_bo)
    x = x + jnp.tanh(g_ffn[2]) * _L2_ffn_ref(_layernorm(x, axis=-1), L2_ffn_Wg_s, L2_ffn_Wu_s, L2_ffn_Wd_s, L2_ffn_Wg, L2_ffn_Wu, L2_ffn_Wd, L2_ffn_Wr, L2_ffn_rb)
    x = x + jnp.tanh(g_xattn[3]) * _L3_xattn_ref(_layernorm(x, axis=-1), ctx_1024, L3_xattn_Wq, L3_xattn_Wkv, L3_xattn_null_kv, L3_xattn_ln_q_g, L3_xattn_ln_q_b, L3_xattn_ln_out_g, L3_xattn_ln_out_b, L3_xattn_Wout)
    x = x + jnp.tanh(g_ffn[3]) * _L3_ffn_ref(_layernorm(x, axis=-1), L3_ffn_Wr, L3_ffn_br, L3_ffn_W1, L3_ffn_b1, L3_ffn_W2, L3_ffn_b2)
    return x

_drawn_inputs = setup_inputs


def setup_inputs(seed=0):
    import zlib

    import numpy as np

    out = dict(_drawn_inputs(seed))
    spreads = {'L0_ffn_q_scale': (1.0, 0.6),
     'L0_ffn_k_scale': (1.0, 0.6),
     'L0_ffn_ln_g': (1.0, 0.6),
     'L0_ffn_ln_b': (0.0, 0.8),
     'L0_ffn_b1': (0.0, 0.551),
     'L0_ffn_b2': (0.0, 0.1),
     'L1_xattn_ln_scale': (1.0, 0.2),
     'L1_xattn_ln_bias': (0.0, 0.336),
     'L2_xattn_bqkv': (0.0, 0.1),
     'L2_xattn_bo': (0.0, 0.1),
     'L2_ffn_rb': (0.0, 0.8),
     'L3_xattn_ln_q_g': (1.0, 0.6),
     'L3_xattn_ln_q_b': (0.0, 2.0),
     'L3_xattn_ln_out_g': (1.0, 0.6),
     'L3_xattn_ln_out_b': (0.0, 0.8)}
    factors = {'g_ffn': 6.631,
     'L1_ffn_gate_w': 8.0,
     'L1_ffn_gate_up_proj': 8.0,
     'L1_ffn_down_proj': 8.0,
     'L2_ffn_Wg_s': 8.0,
     'L2_ffn_Wu_s': 8.0,
     'L2_ffn_Wd_s': 8.0,
     'L2_ffn_Wg': 8.0,
     'L2_ffn_Wu': 8.0,
     'L2_ffn_Wd': 8.0,
     'L2_ffn_Wr': 8.0,
     'L3_xattn_Wq': 28.016,
     'L3_ffn_b1': 25.656,
     'L3_xattn_null_kv': 7.956,
     'L3_ffn_br': 4.36,
     'L3_ffn_W1': 2.705,
     'L3_ffn_b2': 8.0,
     'L3_xattn_Wkv': 8.0}
    for name, (base, spread) in spreads.items():
        noise = np.random.default_rng([zlib.crc32(name.encode()), seed]).standard_normal(out[name].shape)
        drawn = base * np.exp(spread * noise) if base else spread * noise
        out[name] = jnp.asarray(drawn.astype(out[name].dtype))
    for name, factor in factors.items():
        out[name] = (out[name] * factor).astype(out[name].dtype)
    return out
```

```python
from contextlib import ExitStack

import numpy as np

import concourse.bass as bass
from concourse import mybir

F32 = mybir.dt.float32
BF16 = mybir.dt.bfloat16
U32 = mybir.dt.uint32
ALU = mybir.AluOpType
ACT = mybir.ActivationFunctionType
AX = mybir.AxisListType

B, S, D, M = 16, 128, 128, 77
G = 2
IT = B // G
DEPTH, LH, LD = 6, 16, 64
INNER = LH * LD
HID = int(D * 4 * 2 / 3)
HC = [(0, 128), (128, 256), (256, HID)]
WINDOW = 32
EPS = 1e-5
NEG = -1e30
E1, E2, E3 = 8, 9, 8
EH2 = 256
FF3 = 512
H3, D3 = 8, 64
ND = D // 128 * 4
KEYS3 = M + 1


def constants():
    t = np.arange(S)
    shift = np.zeros((S, S), np.float32)
    shift[t[:-1], t[1:]] = 1
    i, j = t[:, None], t[None, :]
    first = (i // WINDOW - 1) * WINDOW
    seen = (j <= i) & (j + WINDOW >= i) & (j >= first)
    half = np.arange(0, LD, 2, dtype=np.float32)
    inv = (np.float32(1) / np.float32(10000) ** (half / np.float32(LD))).astype(np.float32)
    f = t[:, None].astype(np.float32) * inv[None]
    base = ((half + np.float32(0.4 * LD)) / np.float32(1.4 * LD)).astype(np.float32)
    power = ((t.astype(np.float32) - S // 2) / np.float32(WINDOW // 2)).astype(np.float32)
    scale = (base[None] ** power[:, None]).astype(np.float32)
    two = lambda a: np.concatenate([a, a], 1)
    cos, sin, scale = two(np.cos(f)), two(np.sin(f)), two(scale)
    sin[:, :LD // 2] *= -1
    rot = np.stack([cos * scale, sin * scale, cos / scale, sin / scale], 1)
    d = np.arange(D)
    return {
        "ident": np.eye(S, dtype=np.float32),
        "shift": shift,
        "band": np.where(seen, 0, NEG).astype(np.float32),
        "causal": np.where(np.arange(M)[None] > t[:, None], NEG, 0).astype(np.float32),
        "heads16": (d[:, None] // 8 == np.arange(16)[None]).astype(np.float32),
        "heads2": (d[:, None] // 64 == np.arange(2)[None]).astype(np.float32),
        "pair": (d[:, None] // 64 == d[None] // 64).astype(np.float32),
        "rot": np.ascontiguousarray(rot, np.float32),
        "iota": np.tile(np.arange(8, dtype=np.float32)[None], (S, 1)),
    }


def program(nc, dram, out):
    ctx = ExitStack()
    with ctx:
        def sb(name, shape, dt=F32):
            return ctx.enter_context(nc.sbuf_tensor(name, list(shape), dt))

        def sem(name):
            return ctx.enter_context(nc.semaphore(name))

        def pair(name, shape, dt=F32):
            return [sb(f"{name}{s}", shape, dt) for s in range(G)]

        X = sb("X", [S, B, D])
        Y = sb("Y", [S, B, D])
        ident, shift = sb("ident", [S, S]), sb("shift", [S, S])
        band_f = sb("band_f", [S, S])
        ident_b, band_b = sb("ident_b", [S, S], BF16), sb("band_b", [S, S], BF16)
        causal = sb("causal", [S, M])
        heads16, heads2 = sb("heads16", [D, 16]), sb("heads2", [D, 2])
        blockpair = sb("blockpair", [D, D])
        iota = sb("iota", [S, 8])
        rot = sb("rot", [S, 4, LD])
        qk_scale = pair("qk_scale", [S, 2, LD])
        table = pair("table", [S, 2, 2, LD])
        gates = sb("gates", [S, 2, 4])
        eps_col, neghalf = sb("eps_col", [S, 1]), sb("neghalf", [S, 2 * LH])
        seed = sb("seed", [S, 1])
        w0 = sb("w0", [D, 2, D])
        w1 = sb("w1", [D, 4, 4 * D])
        aff1 = sb("aff1", [D, 2])
        moe1_r = sb("moe1_r", [D, E1])
        moe1_gu = sb("moe1_gu", [D, E1, 2 * D])
        moe1_d = sb("moe1_d", [D, E1, D])
        LW = 3 * INNER + INNER + 2 * HID + 3 * D + D
        lw = [sb(f"lw{p}", [D, LW]) for p in range(2)]
        lcol = [sb(f"lcol{p}", [D, 8]) for p in range(2)]
        wqkv = [t[:, 0:3 * INNER] for t in lw]
        o_ = 3 * INNER
        wout = [t[:, o_:o_ + INNER].rearrange("p (c n) -> p c n", n=D) for t in lw]
        o_ += INNER
        wff1 = [t[:, o_:o_ + 2 * HID] for t in lw]
        o_ += 2 * HID
        wff2 = [t[:, o_:o_ + 3 * D].rearrange("p (c n) -> p c n", n=D) for t in lw]
        o_ += 3 * D
        bff2 = [t[:, o_:o_ + D] for t in lw]
        moe2_g = lw[0][:, 0:E2 * EH2].rearrange("p (e n) -> p e n", n=EH2)
        moe2_u = lw[0][:, E2 * EH2:2 * E2 * EH2].rearrange("p (e n) -> p e n", n=EH2)
        o_ = 2 * E2 * EH2
        w2 = lw[0][:, o_:o_ + 4 * D].rearrange("p (k n) -> p k n", n=D)
        moe2_d = lw[1][:, 0:E2 * EH2].rearrange("p (e c n) -> p e c n", e=E2, n=D)
        o_ = E2 * EH2
        w3 = lw[1][:, o_:o_ + 3 * 512].rearrange("p (k n) -> p k n", n=512)
        o_ += 3 * 512
        w3o = lw[1][:, o_:o_ + 512].rearrange("p (c n) -> p c n", n=D)
        o_ += 512
        small = sb("small", [D, 1100])
        qg, qb = small[:, 0:512], small[:, 512:1024]
        og, ob = small[:, 1024:1028], small[:, 1028:1032]
        bqkv, bq_s = small[:, 1032:1035], small[:, 1035:1036]
        nullk = small[:, 1036:1037]
        moe2_r, moe2_rb = small[:, 1040:1048], small[:, 1048:1056]
        moe3_r, moe3_rb = small[:, 1056:1064], small[:, 1064:1072]
        bo2 = sb("bo2", [S, D])
        xw = pair("xw", [S, D])
        xn = pair("xn", [S, D])
        xnT = pair("xnT", [D, S])
        st, mv, ve, rs = (pair(n, [S, k]) for n, k in (("st", 12), ("mv", 2), ("ve", 1), ("rs", 1)))
        ctxT = pair("ctxT", [D, M])
        area = pair("area", [128, 5 * 2 * INNER + LH * (LD + 1) + 12 * 128])
        K2 = 2 * INNER

        def part(s, at, n, p=128):
            return area[s][0:p, at:at + n]

        bufs = range(G)
        QN = [part(s, 0, K2) for s in bufs]
        SQ = [part(s, K2, K2) for s in bufs]
        QR = [part(s, 2 * K2, K2) for s in bufs]
        RA = [part(s, 3 * K2, K2) for s in bufs]
        QKT = [part(s, 4 * K2, K2) for s in bufs]
        LV = [part(s, 5 * K2, LH * (LD + 1)).rearrange("p (h e) -> p h e", e=LD + 1) for s in bufs]
        at_ = 5 * K2 + LH * (LD + 1)
        hidT = [part(s, at_, 384).rearrange("p (c n) -> p c n", n=S) for s in bufs]
        geluT = [part(s, at_ + 384, 384).rearrange("p (c n) -> p c n", n=S) for s in bufs]
        xsT = [part(s, at_ + 768, S) for s in bufs]
        y1 = [part(s, at_ + 896, D) for s in bufs]
        yb = [part(s, at_ + 1024, D) for s in bufs]
        LP, LPT = SQ, RA
        LO = [part(s, 0, INNER) for s in bufs]
        LOT = [part(s, INNER, INNER).rearrange("p (c n) -> p c n", n=S) for s in bufs]
        XQT = [part(s, 0, 512) for s in bufs]
        XKT = [part(s, 512, 4 * M) for s in bufs]
        XKX = [part(s, 1024, 16 * M) for s in bufs]
        XP = [part(s, K2 + 512, 16 * M) for s in bufs]
        XPT = [part(s, 2 * K2, K2, M) for s in bufs]
        XV = [part(s, 3 * K2, 8 * 65, M) for s in bufs]
        XO = [part(s, 3 * K2 + 1024, 512) for s in bufs]
        XOT = [part(s, 4 * K2, 512) for s in bufs]
        xt = [part(s, 4 * K2 + 512, D) for s in bufs]
        SG = [part(s, 0, 512) for s in bufs]
        AT = [part(s, 512, 512) for s in bufs]
        acc = [part(s, 1024, D) for s in bufs]
        Q3 = [part(s, 0, 512) for s in bufs]
        Q3T = [part(s, 512, 512).rearrange("p (c n) -> p c n", n=S) for s in bufs]
        K3 = [part(s, 1024, 4 * KEYS3).rearrange("p (c n) -> p c n", n=KEYS3) for s in bufs]
        K3T = [part(s, 1536, 512, KEYS3) for s in bufs]
        V3 = [part(s, 2048, 512, KEYS3) for s in bufs]
        C3 = [part(s, 2560, 512).rearrange("p (c n) -> p c n", n=D) for s in bufs]
        O3 = [part(s, 3072, 512) for s in bufs]
        O3T = [part(s, 3584, 512).rearrange("p (c n) -> p c n", n=S) for s in bufs]
        K3E = [part(s, 4096, 4 * KEYS3).rearrange("p (c n) -> p c n", n=KEYS3) for s in bufs]
        F1 = [part(s, 5000, FF3) for s in bufs]
        F2 = [part(s, 5512, FF3).rearrange("p (c n) -> p c n", n=D) for s in bufs]
        FB1 = [part(s, 6024, 4) for s in bufs]
        FB2 = [part(s, 6028, D) for s in bufs]
        F1T = [part(s, 6200, FF3).rearrange("p (c n) -> p c n", n=S) for s in bufs]
        ssq, rnq = pair("ssq", [S, 2 * LH]), pair("rnq", [S, 2 * LH])
        mx = pair("mx", [S, 16])
        rc = pair("rc", [S, 16])
        lg, pr, top8 = pair("lg", [S, 8]), pair("pr", [S, 8]), pair("top8", [S, 8])
        idx, idxf = pair("idx", [S, 8], U32), pair("idxf", [S, 8])
        sel, rw, col = pair("sel", [S, 8]), pair("rw", [S, 8]), pair("col", [S, 4])
        tokmean = pair("tokmean", [D, 1])

        ps = [ctx.enter_context(nc.psum_tensor(f"ps{s}", [128, 4, 512], F32)) for s in range(G)]

        x_loaded, w0_loaded, w1_loaded = sem("x_loaded"), sem("w0_loaded"), sem("w1_loaded")
        lw_loaded = [sem("lw_loaded0"), sem("lw_loaded1")]
        late_loaded = sem("late_loaded")
        ctx_loaded = [sem("ctx_loaded0"), sem("ctx_loaded1")]
        expert_loaded = [sem("expert_loaded0"), sem("expert_loaded1")]
        stored = sem("stored")
        consts_cast, tables_ready, gates_ready = sem("consts_cast"), sem("tables_ready"), sem("gates_ready")
        table_link, late_prep = sem("table_link"), sem("late_prep")
        v_ones = sem("v_ones")
        x_updated, ffn_done, ffn_gated = sem("x_updated"), sem("ffn_done"), sem("ffn_gated")
        xw_ready, ln_stats, ln_mean, ln_var, ln_rstd = (sem(n) for n in ("xw_ready", "ln_stats", "ln_mean", "ln_var", "ln_rstd"))
        x_normed, xnT_ps, xnT_ready = sem("x_normed"), sem("xnT_ps"), sem("xnT_ready")
        ln2_stats, ln2_mean, ln2_var, ln2_rstd, x_normed2 = (sem(n) for n in ("ln2_stats", "ln2_mean", "ln2_var", "ln2_rstd", "x_normed2"))
        k_ps, v_ps, q_ps, kT_ready, v_ready, kx_ready, qT_ready = (sem(n) for n in ("k_ps", "v_ps", "q_ps", "kT_ready", "v_ready", "kx_ready", "qT_ready"))
        sc_ps, sc_masked, sc_max, sc_shifted, sc_exp = (sem(n) for n in ("sc_ps", "sc_masked", "sc_max", "sc_shifted", "sc_exp"))
        pT_ps, pT_act, pT_dve, o_ps, o_recip, o_ready, oT_ps, oT_ready, y_ps, y_biased = (
            sem(n) for n in ("pT_ps", "pT_act", "pT_dve", "o_ps", "o_recip", "o_ready", "oT_ps", "oT_ready", "y_ps", "y_biased"))
        l_y, l_xsT_ps, l_xsT, l_qk_ps, l_sq, l_ss, l_ssf, l_rn, l_qn, l_ra, l_rb, l_rot = (
            sem("l_" + n) for n in ("y", "xsT_ps", "xsT", "qk_ps", "sq", "ss", "ssf", "rn", "qn", "ra", "rb", "rot"))
        l_qkT_ps, l_qkT, l_v_ps, l_v, l_sc_ps, l_max, l_shift, l_exp, l_pT_ps, l_pT, l_pv_ps, l_rc, l_o = (
            sem("l_" + n) for n in ("qkT_ps", "qkT", "v_ps", "v", "sc_ps", "max", "shift", "exp", "pT_ps", "pT", "pv_ps", "rc", "o"))
        l_oT_ps, l_oT, l_att_ps, l_y1, l_yb, l_sh_ps, l_st, l_mv, l_ve, l_rs, l_xn, l_xnT_ps, l_xnT = (
            sem("l_" + n) for n in ("oT_ps", "oT", "att_ps", "y1", "yb", "sh_ps", "st", "mv", "ve", "rs", "xn", "xnT_ps", "xnT"))
        l_gate_ps, l_gelu, l_hid, l_ff_ps = (sem("l_" + n) for n in ("gate_ps", "gelu", "hid", "ff_ps"))
        m_lg_ps, m_link, m_shift, m_prob, m_route, m_gu_ps, m_silu, m_act, m_dn_ps, m_part, m_acc = (
            sem("m_" + n) for n in ("lg_ps", "link", "shift", "prob", "route", "gu_ps", "silu", "act", "dn_ps", "part", "acc"))
        e_xT = sem("e_xT")
        t_v, t_k, t_klink, t_kshift, t_kexp, t_kT_ps, t_kT, t_c_ps, t_c = (
            sem("t_" + n) for n in ("v", "k", "klink", "kshift", "kexp", "kT_ps", "kT", "c_ps", "c"))
        t_qlink, t_qvar, t_qrs, t_qg, t_qshift, t_qexp, t_qT_ps, t_qT, t_o_ps, t_olink, t_ovar, t_ors, t_o, t_oT_ps, t_oT, t_y_ps = (
            sem("t_" + n) for n in ("qlink", "qvar", "qrs", "qg", "qshift", "qexp", "qT_ps", "qT", "o_ps", "olink", "ovar", "ors", "o", "oT_ps", "oT", "y_ps"))

        LN0, LNY, LN1, LN1F, LN2, LN2F, LN3, LN3F = (16 * i for i in range(8))
        NO = {LN0: 0, LN1: 16, LN1F: 32, LN2: 48, LN2F: 64, LN3: 80, LN3F: 96}

        def nth(base, it, s, per=1, k=0):
            return base * per + (it * G + s) * per + k + 1

        def nth_group(base, it, s, per, g):
            return base + it * (G * per) + g * G + s + 1

        def heads4(ap, m=M):
            return ap.rearrange("p (h m) -> p h m", m=m)

        XA = [
            dict(ln=LN0, H=16, dv=8, C=1, scale=8 ** -0.5, mask=causal, hm=heads16, wq=w0[:, 0, :], wk=w0[:, 0, :],
                 wv=w0[:, 0, :], wo=w0[:, 1:2, :], gate=gates[:, 0, 0:1]),
            dict(ln=LN1, H=8, dv=64, C=4, scale=64 ** -0.5, mask=None, hm=heads2, wq=w1[:, 0, :], wk=w1[:, 1, :],
                 wv=w1[:, 2, :], wo=w1[:, 3, :].rearrange("p (c n) -> p c n", n=D), gate=gates[:, 0, 1:2]),
            dict(ln=LN2, H=16, dv=8, C=1, scale=1.0, mask=None, hm=heads16, wq=w2[:, 0, :], wk=w2[:, 1, :],
                 wv=w2[:, 2, :], wo=w2[:, 3:4, :], gate=gates[:, 0, 2:3]),
        ]
        side = sb("side", [S, M])
        XA[2]["mask"] = side
        for a in XA:
            a["HB"] = a["H"] // 4
            a["OB"] = 4 if a["dv"] == 64 else 16

        def gu1(e):
            return [(moe1_gu[:, e, 0:D], moe1_gu[:, e, D:2 * D])]

        def gu2(e):
            return [(moe2_g[:, e, c * 128:(c + 1) * 128], moe2_u[:, e, c * 128:(c + 1) * 128]) for c in range(2)]

        MOE = [
            dict(ln=LN1F, groups=[[0, 1, 2, 3], [4, 5, 6, 7]], gu=gu1, down=lambda e: [moe1_d[:, e, :]], r=moe1_r[:, :],
                 base=0, part0=0, parts=6, link0=0, links=17, gate=gates[:, 1, 1:2]),
            dict(ln=LN2F, groups=[[0, 1], [2, 3], [4, 5], [6, 7], [8]], gu=gu2,
                 down=lambda e: [moe2_d[:, e, c, :] for c in range(2)], r=moe2_r, base=32, part0=96, parts=4, link0=16 * 17, links=5, gate=gates[:, 1, 2:3]),
        ]

        block = ctx.enter_context(nc.Block())

        @block.sync
        def _(sp):
            def load(dst, name, done):
                sp.dma_start(dst, dram[name]).then_inc(done, 16)

            def context(a, s, b):
                sp.dma_start(ctxT[s][:, :], dram["ctxT"][:, b, :]).then_inc(ctx_loaded[s], 16)

            load(X[:, :, :], "x", x_loaded)
            for dst, name in ((ident, "ident"), (heads16, "heads16"), (causal, "causal")):
                load(dst[:, :], name, w0_loaded)
            load(w0[:, :, :], "w0", w0_loaded)
            for s in range(G):
                context(0, s, s)
            for i, name in enumerate(("g_xattn", "g_ffn")):
                sp.dma_start(gates[:, i, :], dram[name].partition_broadcast(S)).then_inc(w0_loaded, 16)
            for dst, name in ((shift, "shift"), (band_f, "band")):
                load(dst[:, :], name, w1_loaded)
            load(rot[:, :, :], "rot", w1_loaded)
            for dst, name in ((heads2, "heads2"), (blockpair, "pair"), (iota, "iota"), (aff1, "aff1"), (moe1_r, "moe1_r")):
                load(dst[:, :], name, w1_loaded)
            for dst, name in ((w1, "w1"), (moe1_gu, "moe1_gu"), (moe1_d, "moe1_d")):
                load(dst[:, :, :], name, w1_loaded)

            def layer(p, l):
                for dst, src in (
                    (wqkv[p], dram["wqkv"][l, :, :]), (wout[p], dram["wout"][l, :, :, :]), (wff1[p], dram["wff1"][l, :, :]),
                    (wff2[p][:, 0:2, :], dram["wff2"][l, 0:256, :].rearrange("(c p) n -> p c n", p=128)),
                    (wff2[p][0:HID - 256, 2, :], dram["wff2"][l, 256:HID, :]),
                    (lcol[p][:, :], dram["lcol"][l, :, :]), (bff2[p], dram["bff2"][bass.ds(l, 1), :].partition_broadcast(S)),
                    (qk_scale[p][:, 0, :], dram["q_scale"][bass.ds(l, 1), :].partition_broadcast(S)),
                    (qk_scale[p][:, 1, :], dram["k_scale"][bass.ds(l, 1), :].partition_broadcast(S)),
                ):
                    sp.dma_start(dst, src).then_inc(lw_loaded[p], 16)

            for p in range(2):
                layer(p, p)

            def contexts(a):
                if a:
                    for s in range(G):
                        sp.wait_ge(v_ps, 16 * a)
                        context(a, s, s)
                with sp.Fori(0, IT - 1) as it:
                    for s in range(G):
                        sp.wait_ge(v_ps, nth(16 * a, it, s))
                        context(a, s, it * G + s + G)

            contexts(0)
            with sp.Fori(0, DEPTH // 2 - 1) as lp:
                for p in range(2):
                    sp.wait_ge(ffn_done, G + (lp * 2 + p + 1) * B)
                    layer(p, lp * 2 + p + 2)
            sp.wait_ge(ffn_done, G + DEPTH * B)
            for dst, name in ((moe2_g, "moe2_g"), (moe2_u, "moe2_u"), (w2, "w2"), (w3, "w3"), (w3o, "w3o")):
                load(dst, name, late_loaded)
            load(moe2_d, "moe2_d", late_loaded)
            load(side[:, :], "side", late_loaded)
            for dst, name in ((og, "og"), (ob, "ob"), (bqkv, "bqkv"), (nullk, "nullk"), (moe2_r, "moe2_r"), (moe3_r, "moe3_r")):
                load(dst, name, late_loaded)
            for dst, name in ((qg, "qg"), (qb, "qb"), (moe2_rb, "moe2_rb"), (moe3_rb, "moe3_rb"), (bo2[:, :], "bo2")):
                sp.dma_start(dst, dram[name].partition_broadcast(128)).then_inc(late_loaded, 16)
            contexts(1)
            contexts(2)
            for s in range(G):
                sp.wait_ge(x_updated, G + LN3)
                sp.dma_start(V3[s][M:KEYS3, :], dram["nullv"]).then_inc(expert_loaded[s], 16)
            for s in range(G):
                sp.wait_ge(v_ps, 48)
                context(3, s, s)
            with sp.Fori(0, IT - 1) as it:
                for s in range(G):
                    sp.wait_ge(v_ps, nth(48, it, s))
                    context(3, s, it * G + s + G)
            with sp.Fori(0, IT) as it:
                for s in range(G):
                    sp.compute_val(nth(32, it, s))
                    sp.wait_ge(x_loaded, 16)
                    sp.wait_ge(m_route, nth(32, it, s))
                    e = sp.value_load(idx[s][0:1, 0:1], min_val=0, max_val=E3 - 1)
                    for dst, src in (
                        (F1[s], dram["moe3_w1"][bass.ds(e, 1), :, :].rearrange("a p n -> (a p) n")),
                        (F2[s], dram["moe3_w2"][bass.ds(e, 1), :, :, :].rearrange("a p c n -> (a p) c n")),
                        (FB1[s], dram["moe3_b1"][bass.ds(e, 1), :, :].rearrange("a p n -> (a p) n")),
                        (FB2[s], dram["moe3_b2"][bass.ds(e, 1), :].partition_broadcast(S)),
                    ):
                        sp.dma_start(dst, src).then_inc(expert_loaded[s], 16)
            sp.wait_ge(x_updated, G + LN3F + 16)
            sp.wait_ge(ffn_gated, 1)
            sp.dma_start(out, X[:, :, :]).then_inc(stored, 16)
            sp.wait_ge(stored, 16)

        @block.tensor
        def _(pe):
            def transpose_x(k, it, s, ready, n):
                pe.wait_ge(ready, n)
                nc.tensor.transpose(ps[s][:, 0, 0:S], xn[s][:, :], ident[:, :]).then_inc(xnT_ps, 1)

            def attention(a, i):
                H, dv, C, HB, OB = a["H"], a["dv"], a["C"], a["HB"], a["OB"]
                no = NO[a["ln"]]
                with pe.Fori(0, IT) as it:
                    for s in range(G):
                        pe.wait_ge(ctx_loaded[s], 16 * (IT * i + it + 1))
                        pe.wait_ge(x_updated, nth(a["ln"], it, s))
                        for c in range(C):
                            last = nc.tensor.matmul(ps[s][:, 2, c * M:(c + 1) * M], a["wk"][:, c * 128:(c + 1) * 128],
                                                    ctxT[s][:, :], start=True, stop=True)
                        last.then_inc(k_ps, 1)
                        nc.tensor.matmul(ps[s][0:M, 3, 0:H * dv], ctxT[s][:, :], a["wv"],
                                         start=True, stop=True).then_inc(v_ps, 1)
                    for s in range(G):
                        if i == 1:
                            transpose_x(no, it, s, x_normed2, nth(0, it, s))
                        else:
                            transpose_x(no, it, s, x_normed, nth(no, it, s))
                    for s in range(G):
                        pe.wait_ge(xnT_ready, nth(no, it, s))
                        for c in range(C):
                            last = nc.tensor.matmul(ps[s][:, 1, c * S:(c + 1) * S], a["wq"][:, c * 128:(c + 1) * 128],
                                                    xnT[s][:, :], start=True, stop=True)
                        last.then_inc(q_ps, 1)
                    for s in range(G):
                        pe.wait_ge(kx_ready, nth(16 * i, it, s))
                        pe.wait_ge(v_ready, nth(16 * i, it, s))
                        pe.wait_ge(qT_ready, nth(16 * i, it, s))
                        for j in range(4):
                            c = j if C == 4 else 0
                            last = nc.tensor.matmul(ps[s][:, j, 0:HB * M], XQT[s][:, c * S:(c + 1) * S],
                                                    XKX[s][:, j * HB * M:(j + 1) * HB * M], start=True, stop=True)
                        last.then_inc(sc_ps, 1)
                    for s in range(G):
                        pe.wait_ge(sc_exp, nth(16 * i, it, s))
                        for h in range(H):
                            last = nc.tensor.transpose(ps[s][0:M, h // 4, (h % 4) * S:(h % 4 + 1) * S],
                                                       XP[s][:, h * M:(h + 1) * M], ident[:, :])
                        last.then_inc(pT_ps, 1)
                    for s in range(G):
                        pe.wait_ge(pT_act, nth(16 * i, it, s))
                        pe.wait_ge(pT_dve, nth(16 * i, it, s))
                        for h in range(H):
                            w = dv + 1
                            last = nc.tensor.matmul(ps[s][:, h // OB, (h % OB) * w:(h % OB + 1) * w],
                                                    XPT[s][:, h * S:(h + 1) * S], XV[s][:, h * w:(h + 1) * w],
                                                    start=True, stop=True)
                        last.then_inc(o_ps, 1)
                    for s in range(G):
                        pe.wait_ge(o_ready, nth(16 * i, it, s))
                        for c in range(C):
                            last = nc.tensor.transpose(ps[s][:, 2, c * S:(c + 1) * S], XO[s][:, c * 128:(c + 1) * 128],
                                                       ident[:, :])
                        last.then_inc(oT_ps, 1)
                    for s in range(G):
                        pe.wait_ge(oT_ready, nth(16 * i, it, s))
                        for c in range(C):
                            last = nc.tensor.matmul(ps[s][:, 3, 0:D], XOT[s][:, c * S:(c + 1) * S], a["wo"][:, c, :],
                                                    start=(c == 0), stop=(c == C - 1))
                        last.then_inc(y_ps, 1)

            def local_layer(p, lp):
                with pe.Fori(0, IT) as pr_:
                    it = lp * (2 * IT) + p * IT + pr_
                    one = lambda q, s, per=1, k=0: nth(0, it, s, per, k)
                    for s in range(G):
                        pe.wait_ge(l_y, one(0, s))
                        nc.tensor.matmul(ps[s][0:64, 0, 0:S], xw[s][:, 0:64], ident[:, :], start=True, stop=True)
                        nc.tensor.matmul(ps[s][64:128, 0, 0:S], xw[s][:, 64:128], shift[:, :],
                                         start=True, stop=True).then_inc(l_xsT_ps, 1)
                    for s in range(G):
                        pe.wait_ge(lw_loaded[p], 144 * (lp + 1))
                        pe.wait_ge(l_xsT, one(0, s))
                        for j in range(4):
                            nc.tensor.matmul(ps[s][:, j, :], xsT[s], wqkv[p][:, j * 512:(j + 1) * 512],
                                             start=True, stop=True).then_inc(l_qk_ps, 1)
                    for s in range(G):
                        for j in range(4):
                            pe.wait_ge(l_rot, one(0, s, 4, j))
                            for c in range(4):
                                last = nc.tensor.transpose(ps[s][:, j, c * S:(c + 1) * S],
                                                           QR[s][:, j * 512 + c * 128:j * 512 + (c + 1) * 128], ident[:, :])
                            last.then_inc(l_qkT_ps, 1)
                    for s in range(G):
                        pe.wait_ge(l_qkT, one(0, s, 4, 3))
                        for j in range(2):
                            nc.tensor.matmul(ps[s][:, 2 + j, :], xsT[s], wqkv[p][:, K2 + j * 512:K2 + (j + 1) * 512],
                                             start=True, stop=True).then_inc(l_v_ps, 1)
                    for s in range(G):
                        for g in range(4):
                            if g == 2:
                                pe.wait_ge(l_v, one(0, s, 2, 1))
                            odd, c0 = g // 2, (g % 2) * 4
                            nc.tensor.matmul(ps[s][:, g, :].rearrange("p (c n) -> p c n", n=S), ident_b[:, :],
                                             band_b[:, None, :].to_broadcast([S, 4, S]), start=True, stop=False,
                                             skip_group_check=True)
                            for c in range(4):
                                rows = slice(64 * odd, 64 * odd + 64)
                                cols = slice((c0 + c) * S, (c0 + c + 1) * S)
                                last = nc.tensor.matmul(ps[s][:, g, c * S:(c + 1) * S], QKT[s][rows, cols],
                                                        QKT[s][rows, slice(INNER + cols.start, INNER + cols.stop)],
                                                        start=False, stop=(c == 3), skip_group_check=True)
                            last.then_inc(l_sc_ps, 1)
                    for s in range(G):
                        for g in range(4):
                            pe.wait_ge(l_exp, one(0, s, 4, g))
                            for c in range(4):
                                last = nc.tensor.transpose(ps[s][:, g, c * S:(c + 1) * S],
                                                           LP[s][:, g * 512 + c * S:g * 512 + (c + 1) * S], ident[:, :])
                            last.then_inc(l_pT_ps, 1)
                    for s in range(G):
                        for g in range(4):
                            pe.wait_ge(l_pT, one(0, s, 4, g))
                            for c in range(4):
                                h = 2 * ((g % 2) * 4 + c) + g // 2
                                last = nc.tensor.matmul(ps[s][:, g, c * 65:(c + 1) * 65],
                                                        LPT[s][:, g * 512 + c * S:g * 512 + (c + 1) * S], LV[s][:, h, :],
                                                        start=True, stop=True)
                            last.then_inc(l_pv_ps, 1)
                    for s in range(G):
                        pe.wait_ge(l_o, one(0, s, 4, 3))
                        for j in range(2):
                            for c in range(4):
                                last = nc.tensor.transpose(ps[s][:, j, c * S:(c + 1) * S],
                                                           LO[s][:, (4 * j + c) * 128:(4 * j + c + 1) * 128], ident[:, :])
                            last.then_inc(l_oT_ps, 1)
                    for s in range(G):
                        for c in range(8):
                            if c % 4 == 0:
                                pe.wait_ge(l_oT, one(0, s, 2, c // 4))
                            last = nc.tensor.matmul(ps[s][:, 2, 0:D], LOT[s][:, c, :], wout[p][:, c, :],
                                                    start=(c == 0), stop=(c == 7))
                        last.then_inc(l_att_ps, 1)
                    for s in range(G):
                        pe.wait_ge(l_y1, one(0, s))
                        nc.tensor.matmul(ps[s][:, 3, 0:64], shift[:, :], y1[s][:, 64:128],
                                         start=True, stop=True).then_inc(l_sh_ps, 1)
                    for s in range(G):
                        pe.wait_ge(l_xn, one(0, s, 2, 1))
                        nc.tensor.transpose(ps[s][:, 0, 0:S], xn[s][:, :], ident[:, :]).then_inc(l_xnT_ps, 1)
                    for s in range(G):
                        pe.wait_ge(l_xnT, one(0, s))
                        for bank, at in ((1, HID), (2, 0)):
                            for c, (lo, hi) in enumerate(HC):
                                last = nc.tensor.matmul(ps[s][0:hi - lo, bank, c * S:(c + 1) * S],
                                                        wff1[p][:, at + lo:at + hi], xnT[s][:, :], start=True, stop=True)
                            last.then_inc(l_gate_ps, 1)
                    for s in range(G):
                        for c, (lo, hi) in enumerate(HC):
                            pe.wait_ge(l_hid, one(0, s, 3, c))
                            last = nc.tensor.matmul(ps[s][:, 0, 128:256], hidT[s][0:hi - lo, c, :], wff2[p][0:hi - lo, c, :],
                                                    start=(c == 0), stop=(c == 2))
                        last.then_inc(l_ff_ps, 1)

            def mixture(m):
                no, base = NO[m["ln"]], m["base"]
                mi = 16 if base else 0
                NG = len(m["groups"])
                with pe.Fori(0, IT) as it:
                    for s in range(G):
                        transpose_x(no, it, s, x_normed, nth(no, it, s))
                    for s in range(G):
                        pe.wait_ge(xnT_ready, nth(no, it, s))
                        nc.tensor.matmul(ps[s][:, 1, 0:8], xnT[s][:, :], m["r"], start=True, stop=True).then_inc(m_lg_ps, 1)
                    for g, experts in enumerate(m["groups"]):
                        for s in range(G):
                            if g:
                                pe.wait_ge(m_act, nth_group(base, it, s, NG, g - 1))
                            u = 0
                            for e in experts:
                                for wg, wu in m["gu"](e):
                                    nc.tensor.matmul(ps[s][:, 2, u * S:(u + 1) * S], wg, xnT[s][:, :], start=True, stop=True)
                                    last = nc.tensor.matmul(ps[s][:, 3, u * S:(u + 1) * S], wu, xnT[s][:, :], start=True, stop=True)
                                    u += 1
                            last.then_inc(m_gu_ps, 1)
                        for s in range(G):
                            if g == 0:
                                pass
                            elif g == 1:
                                pe.wait_ge(m_shift, nth(mi, it, s))
                            else:
                                pe.wait_ge(m_acc, nth_group(base, it, s, NG, g - 2))
                            pe.wait_ge(m_act, nth_group(base, it, s, NG, g))
                            u = 0
                            for n, e in enumerate(experts):
                                wd = m["down"](e)
                                for c, w in enumerate(wd):
                                    last = nc.tensor.matmul(ps[s][:, g % 2, n * D:(n + 1) * D], AT[s][:, u * S:(u + 1) * S], w,
                                                            start=(c == 0), stop=(c == len(wd) - 1))
                                    u += 1
                            last.then_inc(m_dn_ps, 1)

            def linear_attention():
                no = NO[LN3]
                with pe.Fori(0, IT) as it:
                    for s in range(G):
                        pe.wait_ge(ctx_loaded[s], 16 * (IT * 3 + it + 1))
                        pe.wait_ge(x_updated, nth(LN3, it, s))
                        for c in range(4):
                            last = nc.tensor.matmul(ps[s][:, 2, c * M:(c + 1) * M], w3[:, 1, c * 128:(c + 1) * 128],
                                                    ctxT[s][:, :], start=True, stop=True)
                        last.then_inc(k_ps, 1)
                        nc.tensor.matmul(ps[s][0:M, 3, :], ctxT[s][:, :], w3[:, 2, :], start=True, stop=True).then_inc(v_ps, 1)
                    for s in range(G):
                        transpose_x(no, it, s, x_normed, nth(no, it, s))
                    for s in range(G):
                        pe.wait_ge(xnT_ready, nth(no, it, s))
                        nc.tensor.matmul(ps[s][:, 1, :], xnT[s][:, :], w3[:, 0, :], start=True, stop=True).then_inc(q_ps, 1)
                    for s in range(G):
                        pe.wait_ge(t_kexp, nth(0, it, s))
                        for c in range(4):
                            last = nc.tensor.transpose(ps[s][0:KEYS3, 2, c * 128:(c + 1) * 128], K3E[s][:, c, :], ident[:, :])
                        last.then_inc(t_kT_ps, 1)
                    for s in range(G):
                        pe.wait_ge(t_v, nth(0, it, s))
                        pe.wait_ge(t_kT, nth(0, it, s))
                        for c in range(4):
                            cols = slice(c * 128, (c + 1) * 128)
                            last = nc.tensor.matmul(ps[s][:, 3, cols], K3T[s][:, cols], V3[s][:, cols], start=True, stop=True)
                        last.then_inc(t_c_ps, 1)
                    for s in range(G):
                        pe.wait_ge(t_qexp, nth(0, it, s))
                        for c in range(4):
                            last = nc.tensor.transpose(ps[s][:, 0, c * S:(c + 1) * S], Q3[s][:, c * 128:(c + 1) * 128], ident[:, :])
                        last.then_inc(t_qT_ps, 1)
                    for s in range(G):
                        pe.wait_ge(t_c, nth(0, it, s))
                        pe.wait_ge(t_qT, nth(0, it, s))
                        for c in range(4):
                            last = nc.tensor.matmul(ps[s][:, 1, c * 128:(c + 1) * 128], Q3T[s][:, c, :], C3[s][:, c, :],
                                                    start=True, stop=True)
                        last.then_inc(t_o_ps, 1)
                    for s in range(G):
                        pe.wait_ge(t_o, nth(0, it, s))
                        for c in range(4):
                            last = nc.tensor.transpose(ps[s][:, 2, c * S:(c + 1) * S], O3[s][:, c * 128:(c + 1) * 128], ident[:, :])
                        last.then_inc(t_oT_ps, 1)
                    for s in range(G):
                        pe.wait_ge(t_oT, nth(0, it, s))
                        for c in range(4):
                            last = nc.tensor.matmul(ps[s][:, 3, 0:D], O3T[s][:, c, :], w3o[:, c, :],
                                                    start=(c == 0), stop=(c == 3))
                        last.then_inc(t_y_ps, 1)

            def chosen_expert():
                no = NO[LN3F]
                with pe.Fori(0, IT) as it:
                    for s in range(G):
                        transpose_x(no, it, s, x_normed, nth(no, it, s))
                    for s in range(G):
                        pe.wait_ge(xnT_ready, nth(no, it, s))
                        nc.tensor.matmul(ps[s][0:1, 1, 0:8], tokmean[s][:, :], moe3_r, start=True, stop=True).then_inc(m_lg_ps, 1)
                    for s in range(G):
                        pe.wait_ge(expert_loaded[s], 16 + 64 * (it + 1))
                        for c in range(4):
                            last = nc.tensor.matmul(ps[s][:, 2, c * S:(c + 1) * S], F1[s][:, c * 128:(c + 1) * 128], xnT[s][:, :],
                                                    start=True, stop=True)
                        last.then_inc(m_gu_ps, 1)
                    for s in range(G):
                        pe.wait_ge(m_silu, nth(16 * 7, it, s))
                        for c in range(4):
                            last = nc.tensor.matmul(ps[s][:, 3, 0:D], F1T[s][:, c, :], F2[s][:, c, :],
                                                    start=(c == 0), stop=(c == 3))
                        last.then_inc(m_dn_ps, 1)

            pe.wait_ge(w0_loaded, 96)
            attention(XA[0], 0)
            pe.wait_ge(consts_cast, 2)
            with pe.Fori(0, DEPTH // 2) as lp:
                for p in range(2):
                    local_layer(p, lp)
            pe.wait_ge(ffn_gated, 1)
            pe.wait_ge(w1_loaded, 176)
            attention(XA[1], 1)
            mixture(MOE[0])
            pe.wait_ge(late_loaded, 288)
            attention(XA[2], 2)
            mixture(MOE[1])
            linear_attention()
            chosen_expert()

        @block.scalar
        def _(act):
            def copy(dst, src, **kw):
                return nc.scalar.activation(dst, src, ACT.Identity if kw else ACT.Copy, **kw)

            def attention(a, i):
                H, dv, C, no = a["H"], a["dv"], a["C"], NO[a["ln"]]
                with act.Fori(0, IT) as it:
                    for s in range(G):
                        act.wait_ge(k_ps, nth(16 * i, it, s))
                        kw = dict(bias=bqkv[:, 1:2]) if i == 2 else {}
                        copy(XKT[s][:, 0:C * M], ps[s][:, 2, 0:C * M], **kw).then_inc(kT_ready, 1)
                        act.wait_ge(v_ps, nth(16 * i, it, s))
                        copy(heads4(XV[s][:, 0:H * (dv + 1)], dv + 1)[:, :, 0:dv],
                             ps[s][0:M, 3, 0:H * dv].rearrange("p (h e) -> p h e", e=dv)).then_inc(v_ready, 1)
                    for s in range(G):
                        act.wait_ge(xnT_ps, nth(no, it, s))
                        kw = dict(scale=aff1[:, 0:1], bias=aff1[:, 1:2]) if i == 1 else {}
                        copy(xnT[s][:, :], ps[s][:, 0, 0:S], **kw).then_inc(xnT_ready, 1)
                    for s in range(G):
                        act.wait_ge(q_ps, nth(16 * i, it, s))
                        kw = dict(scale=8 ** -0.5, bias=bq_s) if i == 2 else {}
                        copy(XQT[s][:, 0:C * S], ps[s][:, 1, 0:C * S], **kw).then_inc(qT_ready, 1)
                    for s in range(G):
                        act.wait_ge(sc_shifted, nth(16 * i, it, s))
                        nc.scalar.activation(XP[s][:, 0:H * M], XP[s][:, 0:H * M], ACT.Exp, scale=a["scale"]).then_inc(sc_exp, 1)
                    for s in range(G):
                        act.wait_ge(pT_ps, nth(16 * i, it, s))
                        copy(XPT[s][:, 0:H * S // 2], ps[s][0:M, 0:H // 8, :].rearrange("p j n -> p (j n)")).then_inc(pT_act, 1)
                    for s in range(G):
                        act.wait_ge(oT_ps, nth(16 * i, it, s))
                        kw = dict(bias=bqkv[:, 2:3]) if i == 2 else {}
                        copy(XOT[s][:, 0:C * S], ps[s][:, 2, 0:C * S], **kw).then_inc(oT_ready, 1)

            def local_layer(p, lp):
                with act.Fori(0, IT) as pr_:
                    it = lp * (2 * IT) + p * IT + pr_
                    one = lambda s, per=1, k=0: nth(0, it, s, per, k)
                    for s in range(G):
                        act.wait_ge(l_xsT_ps, one(s))
                        copy(xsT[s], ps[s][:, 0, 0:S]).then_inc(l_xsT, 1)
                    for s in range(G):
                        for j in range(4):
                            act.wait_ge(l_qk_ps, one(s, 4, j))
                            nc.scalar.activation(SQ[s][:, j * 512:(j + 1) * 512], ps[s][:, j, :], ACT.Square).then_inc(l_sq, 1)
                    for s in range(G):
                        for j in range(4):
                            act.wait_ge(l_qkT_ps, one(s, 4, j))
                            copy(QKT[s][:, j * 512:(j + 1) * 512], ps[s][:, j, :]).then_inc(l_qkT, 1)
                    for s in range(G):
                        for j in range(2):
                            act.wait_ge(l_v_ps, one(s, 2, j))
                            copy(LV[s][:, 8 * j:8 * j + 8, 0:LD], ps[s][:, 2 + j, :].rearrange("p (h e) -> p h e", e=LD)).then_inc(l_v, 1)
                    for s in range(G):
                        for g in range(4):
                            act.wait_ge(l_shift, one(s, 4, g))
                            P = LP[s][:, g * 512:(g + 1) * 512]
                            nc.scalar.activation(P, P, ACT.Exp, scale=8.0).then_inc(l_exp, 1)
                    for s in range(G):
                        for g in range(4):
                            act.wait_ge(l_pT_ps, one(s, 4, g))
                            copy(LPT[s][:, g * 512:(g + 1) * 512], ps[s][:, g, :]).then_inc(l_pT, 1)
                    for s in range(G):
                        for j in range(2):
                            act.wait_ge(l_oT_ps, one(s, 2, j))
                            copy(LOT[s][:, 4 * j:4 * j + 4, :].rearrange("p c n -> p (c n)"), ps[s][:, j, :]).then_inc(l_oT, 1)
                    for s in range(G):
                        act.wait_ge(lw_loaded[p], 144 * (lp + 1))
                        act.wait_ge(l_xnT_ps, one(s))
                        copy(xnT[s][:, :], ps[s][:, 0, 0:S], scale=lcol[p][:, 0:1], bias=lcol[p][:, 1:2]).then_inc(l_xnT, 1)
                    for s in range(G):
                        act.wait_ge(l_gate_ps, one(s, 2, 0))
                        for c, (lo, hi) in enumerate(HC):
                            nc.scalar.activation(geluT[s][0:hi - lo, c, :], ps[s][0:hi - lo, 1, c * S:(c + 1) * S], ACT.Gelu,
                                                 bias=lcol[p][0:hi - lo, 5 + c:6 + c]).then_inc(l_gelu, 1)

            def mixture(m):
                no, base, NG = NO[m["ln"]], m["base"], len(m["groups"])
                mi = 16 if base else 0
                with act.Fori(0, IT) as it:
                    for s in range(G):
                        act.wait_ge(xnT_ps, nth(no, it, s))
                        copy(xnT[s][:, :], ps[s][:, 0, 0:S]).then_inc(xnT_ready, 1)
                    for s in range(G):
                        act.wait_ge(m_shift, nth(mi, it, s))
                        nc.scalar.activation(pr[s][:, :], lg[s][:, :], ACT.Sigmoid if base else ACT.Exp).then_inc(m_prob, 1)
                    for g, experts in enumerate(m["groups"]):
                        n = 512 if not base else 256 * len(experts)
                        for s in range(G):
                            act.wait_ge(m_gu_ps, nth_group(base, it, s, NG, g))
                            nc.scalar.activation(SG[s][:, 0:n], ps[s][:, 2, 0:n], ACT.Silu).then_inc(m_silu, 1)

            def linear_attention():
                no = NO[LN3]
                for s in range(G):
                    act.wait_ge(x_updated, LN3 + s + 1)
                    act.wait_ge(late_loaded, 288)
                    copy(K3[s][:, :, M], nullk.to_broadcast([128, 4])).then_inc(t_k, 1)
                with act.Fori(0, IT) as it:
                    for s in range(G):
                        act.wait_ge(k_ps, nth(48, it, s))
                        copy(K3[s][:, :, 0:M], ps[s][:, 2, 0:4 * M].rearrange("p (c n) -> p c n", n=M)).then_inc(t_k, 1)
                        act.wait_ge(v_ps, nth(48, it, s))
                        copy(V3[s][0:M, :], ps[s][0:M, 3, :]).then_inc(t_v, 1)
                    for s in range(G):
                        act.wait_ge(xnT_ps, nth(no, it, s))
                        copy(xnT[s][:, :], ps[s][:, 0, 0:S]).then_inc(xnT_ready, 1)
                    for s in range(G):
                        act.wait_ge(t_kshift, nth(0, it, s))
                        K = K3E[s].rearrange("p c n -> p (c n)")
                        nc.scalar.activation(K, K, ACT.Exp).then_inc(t_kexp, 1)
                    for s in range(G):
                        act.wait_ge(t_kT_ps, nth(0, it, s))
                        copy(K3T[s], ps[s][0:KEYS3, 2, :]).then_inc(t_kT, 1)
                    for s in range(G):
                        act.wait_ge(t_qshift, nth(0, it, s))
                        nc.scalar.activation(Q3[s], Q3[s], ACT.Exp).then_inc(t_qexp, 1)
                    for s in range(G):
                        act.wait_ge(t_qT_ps, nth(0, it, s))
                        copy(Q3T[s].rearrange("p c n -> p (c n)"), ps[s][:, 0, :]).then_inc(t_qT, 1)
                    for s in range(G):
                        act.wait_ge(t_oT_ps, nth(0, it, s))
                        for c in range(4):
                            last = copy(O3T[s][:, c, :], ps[s][:, 2, c * S:(c + 1) * S], scale=og[:, c:c + 1], bias=ob[:, c:c + 1])
                        last.then_inc(t_oT, 1)

            def chosen_expert():
                no = NO[LN3F]
                with act.Fori(0, IT) as it:
                    for s in range(G):
                        act.wait_ge(xnT_ps, nth(no, it, s))
                        copy(xnT[s][:, :], ps[s][:, 0, 0:S]).then_inc(e_xT, 1)
                        act.wait_ge(e_xT, nth(0, it, s))
                        nc.scalar.activation(F1T[s][:, 0, :], xnT[s][:, :], ACT.Copy, scale=1.0 / S,
                                             accum_out=tokmean[s][:, :]).then_inc(xnT_ready, 1)
                    for s in range(G):
                        act.wait_ge(m_gu_ps, nth(16 * 7, it, s))
                        for c in range(4):
                            last = nc.scalar.activation(F1T[s][:, c, :], ps[s][:, 2, c * S:(c + 1) * S], ACT.Relu, bias=FB1[s][:, c:c + 1])
                        last.then_inc(m_silu, 1)

            act.wait_ge(w0_loaded, 96)
            nc.scalar.activation(gates[:, :, :], gates[:, :, :], ACT.Tanh).then_inc(gates_ready, 1)
            act.wait_ge(v_ones, 2)
            attention(XA[0], 0)
            act.wait_ge(v_ones, 4)
            with act.Fori(0, DEPTH // 2) as lp:
                for p in range(2):
                    local_layer(p, lp)
            act.wait_ge(w1_loaded, 176)
            act.wait_ge(v_ones, 6)
            attention(XA[1], 1)
            mixture(MOE[0])
            act.wait_ge(late_prep, 2)
            act.wait_ge(v_ones, 8)
            attention(XA[2], 2)
            mixture(MOE[1])
            linear_attention()
            chosen_expert()

        @block.gpsimd
        def _(pool):
            def layer_norms(base):
                with pool.Fori(0, IT) as it:
                    for s in range(G):
                        pool.wait_ge(ln_mean, nth(base, it, s))
                        pool.tensor_tensor(ve[s][:, :], mv[s][:, 1:2], eps_col[:, :], ALU.add).then_inc(ln_var, 1)
                        pool.wait_ge(ln_var, nth(base, it, s))
                        pool.tensor_tensor(rs[s][:, :], ve[s][:, :], neghalf[:, 0:1], ALU.pow).then_inc(ln_rstd, 1)

            def attention(a, i):
                H, C, hm = a["H"], a["C"], a["hm"]
                with pool.Fori(0, IT) as it:
                    for s in range(G):
                        pool.wait_ge(ln_mean, nth(a["ln"], it, s))
                        pool.tensor_tensor(ve[s][:, :], mv[s][:, 1:2], eps_col[:, :], ALU.add).then_inc(ln_var, 1)
                        pool.wait_ge(ln_var, nth(a["ln"], it, s))
                        pool.tensor_tensor(rs[s][:, :], ve[s][:, :], neghalf[:, 0:1], ALU.pow).then_inc(ln_rstd, 1)
                    if i == 1:
                        for s in range(G):
                            pool.wait_ge(ln2_mean, nth(0, it, s))
                            pool.tensor_tensor(ve[s][:, :], mv[s][:, 1:2], eps_col[:, :], ALU.add).then_inc(ln2_var, 1)
                            pool.wait_ge(ln2_var, nth(0, it, s))
                            pool.tensor_tensor(rs[s][:, :], ve[s][:, :], neghalf[:, 0:1], ALU.pow).then_inc(ln2_rstd, 1)
                    for s in range(G):
                        pool.wait_ge(kT_ready, nth(16 * i, it, s))
                        pool.wait_ge(x_updated, nth(a["ln"], it, s))
                        HQ = H // C
                        for c in range(C):
                            last = pool.tensor_tensor(heads4(XKX[s][:, c * HQ * M:(c + 1) * HQ * M]),
                                                      XKT[s][:, None, c * M:(c + 1) * M].to_broadcast([128, HQ, M]),
                                                      hm[:, :, None].to_broadcast([128, HQ, M]), ALU.mult)
                        last.then_inc(kx_ready, 1)

            def local_layer(p, lp):
                hd = LD // 2
                pool.wait_ge(lw_loaded[p], 144 * (lp + 1))
                for i in range(2):
                    pool.tensor_tensor(table[p][:, i, 0, :], qk_scale[p][:, i, :], rot[:, 2 * i, :], ALU.mult)
                    for lo, other in ((0, hd), (hd, 0)):
                        last = pool.tensor_tensor(table[p][:, i, 1, lo:lo + hd], qk_scale[p][:, i, other:other + hd],
                                                  rot[:, 2 * i + 1, lo:lo + hd], ALU.mult)
                last.then_inc(tables_ready, 1)
                with pool.Fori(0, IT) as pr_:
                    it = lp * (2 * IT) + p * IT + pr_
                    one = lambda s, per=1, k=0: nth(0, it, s, per, k)
                    l = lp * 2 + p
                    for s in range(G):
                        pool.wait_ge(l_ssf, one(s))
                        pool.tensor_tensor(rnq[s][:, :], ssq[s][:, :], neghalf[:, :], ALU.pow).then_inc(l_rn, 1)
                    for s in range(G):
                        for j in range(4):
                            pool.wait_ge(tables_ready, l + 1)
                            pool.wait_ge(l_qn, one(s, 4, j))
                            pool.tensor_tensor(RA[s][:, j * 512:(j + 1) * 512].rearrange("p (h d) -> p h d", d=LD),
                                               QN[s][:, j * 512:(j + 1) * 512].rearrange("p (h d) -> p h d", d=LD),
                                               table[p][:, j // 2, 0:1, :].to_broadcast([S, 8, LD]), ALU.mult).then_inc(l_ra, 1)
                    for s in range(G):
                        pool.wait_ge(lw_loaded[p], 144 * (lp + 1))
                        pool.wait_ge(l_y1, one(s))
                        pool.tensor_tensor(yb[s], y1[s], bff2[p], ALU.add).then_inc(l_yb, 1)
                    for s in range(G):
                        pool.wait_ge(l_mv, one(s))
                        pool.tensor_tensor(ve[s][:, :], mv[s][:, 1:2], eps_col[:, :], ALU.add).then_inc(l_ve, 1)
                        pool.wait_ge(l_ve, one(s))
                        pool.tensor_tensor(rs[s][:, :], ve[s][:, :], neghalf[:, 0:1], ALU.pow).then_inc(l_rs, 1)

            def linear_attention():
                with pool.Fori(0, IT) as it:
                    for s in range(G):
                        pool.wait_ge(ln_mean, nth(LN3, it, s))
                        pool.tensor_tensor(ve[s][:, :], mv[s][:, 1:2], eps_col[:, :], ALU.add).then_inc(ln_var, 1)
                        pool.wait_ge(ln_var, nth(LN3, it, s))
                        pool.tensor_tensor(rs[s][:, :], ve[s][:, :], neghalf[:, 0:1], ALU.pow).then_inc(ln_rstd, 1)
                    for link, var, done in ((t_qlink, t_qvar, t_qrs), (t_olink, t_ovar, t_ors)):
                        for s in range(G):
                            pool.wait_ge(link, nth(0, it, s, 2, 1))
                            pool.tensor_tensor(ve[s][:, :], mv[s][:, 1:2], eps_col[:, :], ALU.add).then_inc(var, 1)
                            pool.wait_ge(var, nth(0, it, s))
                            pool.tensor_tensor(rs[s][:, :], ve[s][:, :], neghalf[:, 0:1], ALU.pow).then_inc(done, 1)

            pool.memset(eps_col[:, :], EPS).then_inc(table_link, 1)
            pool.memset(neghalf[:, :], -0.5).then_inc(table_link, 1)
            for s in range(G):
                pool.memset(XV[s], 1.0).then_inc(v_ones, 1)
            pool.wait_ge(w0_loaded, 96)
            pool.wait_ge(table_link, 2)
            attention(XA[0], 0)
            pool.wait_ge(w1_loaded, 176)
            layer_norms(LNY)
            for s in range(G):
                pool.wait_ge(x_updated, G + LNY)
                pool.memset(LV[s], 1.0).then_inc(v_ones, 1)
            with pool.Fori(0, DEPTH // 2) as lp:
                for p in range(2):
                    local_layer(p, lp)
            for s in range(G):
                pool.wait_ge(ffn_gated, 1)
                pool.memset(XV[s], 1.0).then_inc(v_ones, 1)
            attention(XA[1], 1)
            layer_norms(LN1F)
            for s in range(G):
                pool.wait_ge(x_updated, G + LN2)
                pool.memset(XV[s], 1.0).then_inc(v_ones, 1)
            attention(XA[2], 2)
            layer_norms(LN2F)
            linear_attention()
            layer_norms(LN3F)

        @block.vector
        def _(dve):
            V = nc.vector

            def norm_steps(base, no, it, final):
                for s in range(G):
                    dve.wait_ge(x_updated, nth(base, it, s))
                    V.tensor_scalar(xw[s][:, :], X[:, it * G + s, :], 1.0, None, ALU.mult).then_inc(xw_ready, 1)
                for s in range(G):
                    dve.wait_ge(xw_ready, nth(base, it, s))
                    V.bn_stats(st[s][:, 0:6], xw[s][:, :]).then_inc(ln_stats, 1)
                for s in range(G):
                    dve.wait_ge(x_loaded, 16)
                    dve.wait_ge(ln_stats, nth(base, it, s))
                    V.bn_aggr(mv[s][:, :], st[s][:, 0:6]).then_inc(ln_mean, 1)
                for s in range(G):
                    dve.wait_ge(ln_rstd, nth(base, it, s))
                    final(s)

            def normed(s):
                V.tensor_scalar(xn[s][:, :], xw[s][:, :], mv[s][:, 0:1], rs[s][:, 0:1], ALU.subtract, ALU.mult).then_inc(x_normed, 1)

            def attention(a, i):
                H, dv, C, HB, OB = a["H"], a["dv"], a["C"], a["HB"], a["OB"]
                no = NO[a["ln"]]
                with dve.Fori(0, IT) as it:
                    norm_steps(a["ln"], no, it, normed)
                    if i == 1:
                        for s in range(G):
                            dve.wait_ge(x_normed, nth(no, it, s))
                            V.bn_stats(st[s][:, 0:6], xn[s][:, :]).then_inc(ln2_stats, 1)
                        for s in range(G):
                            dve.compute_val(nth(0, it, s))
                            dve.wait_ge(x_loaded, 16)
                            dve.wait_ge(ln2_stats, nth(0, it, s))
                            V.bn_aggr(mv[s][:, :], st[s][:, 0:6]).then_inc(ln2_mean, 1)
                        for s in range(G):
                            dve.wait_ge(ln2_rstd, nth(0, it, s))
                            V.tensor_scalar(xn[s][:, :], xn[s][:, :], mv[s][:, 0:1], rs[s][:, 0:1],
                                            ALU.subtract, ALU.mult).then_inc(x_normed2, 1)
                    four = lambda ap: ap.rearrange("p (j h m) -> p j h m", j=4, m=M)
                    score = lambda s: ps[s][:, :, 0:HB * M].rearrange("p j (h m) -> p j h m", m=M)
                    P = lambda s: XP[s][:, 0:H * M]
                    if a["mask"] is not None:
                        for s in range(G):
                            dve.wait_ge(sc_ps, nth(16 * i, it, s))
                            mask = a["mask"][:, None, :].to_broadcast([S, HB, M])
                            for j in range(4):
                                last = V.tensor_tensor(four(P(s))[:, j, :, :], score(s)[:, j, :, :], mask, ALU.add)
                            last.then_inc(sc_masked, 1)
                    for s in range(G):
                        if a["mask"] is not None:
                            dve.wait_ge(sc_masked, nth(16 * (i // 2), it, s))
                            V.tensor_reduce(mx[s][:, 0:H], heads4(P(s)), AX.X, ALU.max).then_inc(sc_max, 1)
                        else:
                            dve.wait_ge(sc_ps, nth(16 * i, it, s))
                            V.tensor_reduce(mx[s][:, 0:H].rearrange("p (j h) -> p j h", j=4), score(s), AX.X, ALU.max).then_inc(sc_max, 1)
                    for s in range(G):
                        dve.wait_ge(sc_max, nth(16 * i, it, s))
                        if a["mask"] is not None:
                            V.tensor_tensor(heads4(P(s)), heads4(P(s)), mx[s][:, 0:H, None].to_broadcast([S, H, M]),
                                            ALU.subtract).then_inc(sc_shifted, 1)
                        else:
                            for j in range(4):
                                last = V.tensor_tensor(four(P(s))[:, j, :, :], score(s)[:, j, :, :],
                                                       mx[s][:, j * HB:(j + 1) * HB, None].to_broadcast([S, HB, M]), ALU.subtract)
                            last.then_inc(sc_shifted, 1)
                    for s in range(G):
                        dve.wait_ge(pT_ps, nth(16 * i, it, s))
                        V.tensor_copy(XPT[s][:, H * S // 2:H * S],
                                      ps[s][0:M, H // 8:H // 4, :].rearrange("p j n -> p (j n)")).then_inc(pT_dve, 1)
                    NB = H // OB
                    ov = lambda s: ps[s][:, 0:NB, 0:OB * (dv + 1)].rearrange("p j (h e) -> p j h e", e=dv + 1)
                    for s in range(G):
                        dve.wait_ge(o_ps, nth(16 * i, it, s))
                        V.reciprocal(rc[s][:, 0:H].rearrange("p (j h) -> p j h", j=NB), ov(s)[:, :, :, dv]).then_inc(o_recip, 1)
                    for s in range(G):
                        dve.wait_ge(o_recip, nth(16 * i, it, s))
                        for j in range(NB):
                            last = V.tensor_tensor(XO[s][:, j * OB * dv:(j + 1) * OB * dv].rearrange("p (h e) -> p h e", e=dv),
                                                   ov(s)[:, j, :, 0:dv],
                                                   rc[s][:, j * OB:(j + 1) * OB, None].to_broadcast([S, OB, dv]), ALU.mult)
                        last.then_inc(o_ready, 1)
                    for s in range(G):
                        dve.wait_ge(y_ps, nth(16 * i, it, s))
                        y = ps[s][:, 3, 0:D]
                        if i == 2:
                            V.tensor_tensor(xt[s], y, bo2[:, :], ALU.add).then_inc(y_biased, 1)
                            dve.wait_ge(y_biased, nth(0, it, s))
                            y = xt[s]
                        V.scalar_tensor_tensor(X[:, it * G + s, :], y, a["gate"], xw[s][:, :], ALU.mult, ALU.add).then_inc(x_updated, 1)

            def local_layer(p, lp):
                with dve.Fori(0, IT) as pr_:
                    it = lp * (2 * IT) + p * IT + pr_
                    l = lp * 2 + p
                    one = lambda s, per=1, k=0: nth(0, it, s, per, k)
                    blk = lambda ap, j: ap[:, j * 512:(j + 1) * 512].rearrange("p (h d) -> p h d", d=LD)
                    for s in range(G):
                        dve.wait_ge(ffn_done, one(s))
                        V.tensor_scalar(xw[s][:, :], Y[:, pr_ * G + s, :], 1.0, None, ALU.mult).then_inc(l_y, 1)
                    for s in range(G):
                        for j in range(4):
                            dve.wait_ge(l_sq, one(s, 4, j))
                            V.tensor_reduce(ssq[s][:, 8 * j:8 * j + 8], blk(SQ[s], j), AX.X, ALU.add).then_inc(l_ss, 1)
                        dve.wait_ge(l_ss, one(s, 4, 3))
                        V.tensor_scalar(ssq[s][:, :], ssq[s][:, :], 1e-24, None, ALU.max).then_inc(l_ssf, 1)
                    for s in range(G):
                        dve.wait_ge(l_rn, one(s))
                        for j in range(4):
                            V.tensor_tensor(blk(QN[s], j), ps[s][:, j, :].rearrange("p (h d) -> p h d", d=LD),
                                            rnq[s][:, 8 * j:8 * j + 8, None].to_broadcast([S, 8, LD]), ALU.mult).then_inc(l_qn, 1)
                    hd = LD // 2
                    for s in range(G):
                        dve.wait_ge(tables_ready, l + 1)
                        for j in range(4):
                            dve.wait_ge(l_qn, one(s, 4, j))
                            for lo, other in ((0, hd), (hd, 0)):
                                last = V.tensor_tensor(blk(QR[s], j)[:, :, lo:lo + hd], blk(QN[s], j)[:, :, other:other + hd],
                                                       table[p][:, j // 2, 1:2, lo:lo + hd].to_broadcast([S, 8, hd]), ALU.mult)
                            last.then_inc(l_rb, 1)
                        for j in range(4):
                            dve.wait_ge(l_rb, one(s, 4, j))
                            dve.wait_ge(l_ra, one(s, 4, j))
                            V.tensor_tensor(blk(QR[s], j), blk(QR[s], j), blk(RA[s], j), ALU.add).then_inc(l_rot, 1)
                    for s in range(G):
                        for g in range(4):
                            dve.wait_ge(l_sc_ps, one(s, 4, g))
                            V.tensor_reduce(mx[s][:, 4 * g:4 * g + 4], ps[s][:, g, :].rearrange("p (c n) -> p c n", n=S),
                                            AX.X, ALU.max).then_inc(l_max, 1)
                            dve.wait_ge(l_max, one(s, 4, g))
                            V.tensor_tensor(LP[s][:, g * 512:(g + 1) * 512].rearrange("p (c n) -> p c n", n=S),
                                            ps[s][:, g, :].rearrange("p (c n) -> p c n", n=S),
                                            mx[s][:, 4 * g:4 * g + 4, None].to_broadcast([S, 4, S]), ALU.subtract).then_inc(l_shift, 1)
                    for s in range(G):
                        for g in range(4):
                            dve.wait_ge(l_pv_ps, one(s, 4, g))
                            pv = ps[s][:, g, 0:4 * 65].rearrange("p (c e) -> p c e", e=65)
                            V.reciprocal(rc[s][:, 4 * g:4 * g + 4], pv[:, :, LD]).then_inc(l_rc, 1)
                            dve.wait_ge(l_rc, one(s, 4, g))
                            o = LO[s].rearrange("p (c k e) -> p c k e", k=2, e=LD)
                            V.tensor_tensor(o[:, (g % 2) * 4:(g % 2) * 4 + 4, g // 2, :], pv[:, :, 0:LD],
                                            rc[s][:, 4 * g:4 * g + 4, None].to_broadcast([S, 4, LD]), ALU.mult).then_inc(l_o, 1)
                    for s in range(G):
                        dve.wait_ge(l_att_ps, one(s))
                        V.tensor_tensor(y1[s], ps[s][:, 2, 0:D], xw[s][:, :], ALU.add).then_inc(l_y1, 1)
                    for s in range(G):
                        dve.wait_ge(l_y1, one(s))
                        V.bn_stats(st[s][:, 0:6], y1[s][:, 0:64])
                        dve.wait_ge(l_sh_ps, one(s))
                        V.bn_stats(st[s][:, 6:12], ps[s][:, 3, 0:64]).then_inc(l_st, 1)
                    for s in range(G):
                        dve.wait_ge(x_loaded, 16)
                        dve.wait_ge(l_st, one(s))
                        V.bn_aggr(mv[s][:, :], st[s][:, 0:12]).then_inc(l_mv, 1)
                    for s in range(G):
                        dve.wait_ge(l_rs, one(s))
                        V.tensor_scalar(xn[s][:, 0:64], y1[s][:, 0:64], mv[s][:, 0:1], rs[s][:, 0:1],
                                        ALU.subtract, ALU.mult).then_inc(l_xn, 1)
                        V.tensor_scalar(xn[s][:, 64:128], ps[s][:, 3, 0:64], mv[s][:, 0:1], rs[s][:, 0:1],
                                        ALU.subtract, ALU.mult).then_inc(l_xn, 1)
                    for s in range(G):
                        dve.wait_ge(lw_loaded[p], 144 * (lp + 1))
                        dve.wait_ge(l_gate_ps, one(s, 2, 1))
                        for c, (lo, hi) in enumerate(HC):
                            dve.wait_ge(l_gelu, one(s, 3, c))
                            V.scalar_tensor_tensor(hidT[s][0:hi - lo, c, :], ps[s][0:hi - lo, 2, c * S:(c + 1) * S],
                                                   lcol[p][0:hi - lo, 2 + c:3 + c], geluT[s][0:hi - lo, c, :],
                                                   ALU.add, ALU.mult).then_inc(l_hid, 1)
                    for s in range(G):
                        dve.wait_ge(l_yb, one(s))
                        dve.wait_ge(l_ff_ps, one(s))
                        V.tensor_tensor(Y[:, pr_ * G + s, :], ps[s][:, 0, 128:256], yb[s], ALU.add).then_inc(ffn_done, 1)

            def mixture(m):
                no, base, NG = NO[m["ln"]], m["base"], len(m["groups"])
                mi = 16 if base else 0
                first = 1 if base else 0
                with dve.Fori(0, IT) as it:
                    norm_steps(m["ln"], no, it, normed)

                    def linked(k, s):
                        return m["link0"] + it * (G * m["links"]) + (k - 1) * G + s + 1

                    if base:
                        k, prob = 0, pr
                        for s in range(G):
                            dve.wait_ge(m_lg_ps, nth(mi, it, s))
                            V.tensor_tensor(lg[s][:, :], ps[s][:, 1, 0:8], moe2_rb, ALU.add).then_inc(m_shift, 1)
                    else:
                        k, prob = 4, sel
                        for s in range(G):
                            dve.wait_ge(m_lg_ps, nth(mi, it, s))
                            V.tensor_reduce(col[s][:, 0:1], ps[s][:, 1, 0:8], AX.X, ALU.max).then_inc(m_link, 1)
                        for s in range(G):
                            dve.wait_ge(m_link, linked(1, s))
                            V.tensor_scalar(lg[s][:, :], ps[s][:, 1, 0:8], col[s][:, 0:1], None, ALU.subtract).then_inc(m_shift, 1)
                        for s in range(G):
                            dve.wait_ge(m_prob, nth(mi, it, s))
                            V.tensor_reduce(col[s][:, 1:2], pr[s][:, :], AX.X, ALU.add).then_inc(m_link, 1)
                        for s in range(G):
                            dve.wait_ge(m_link, linked(2, s))
                            V.reciprocal(col[s][:, 2:3], col[s][:, 1:2]).then_inc(m_link, 1)
                        for s in range(G):
                            dve.wait_ge(m_link, linked(3, s))
                            V.tensor_scalar(sel[s][:, :], pr[s][:, :], col[s][:, 2:3], None, ALU.mult).then_inc(m_link, 1)
                    for s in range(G):
                        if base:
                            dve.compute_val(nth(mi, it, s))
                            dve.wait_ge(x_loaded, 16)
                            dve.wait_ge(m_prob, nth(mi, it, s))
                        else:
                            dve.compute_val(linked(k, s))
                            dve.wait_ge(x_loaded, 16)
                            dve.wait_ge(m_link, linked(k, s))
                        V.max(top8[s][:, :], prob[s][:, :]).then_inc(m_link, 1)
                    for s in range(G):
                        dve.compute_val(linked(k + 1, s))
                        dve.wait_ge(x_loaded, 16)
                        dve.wait_ge(m_link, linked(k + 1, s))
                        V.max_index(idx[s][:, :], top8[s][:, :], prob[s][:, :]).then_inc(m_link, 1)
                    for s in range(G):
                        dve.wait_ge(m_link, linked(k + 2, s))
                        V.tensor_copy(idxf[s][:, :], idx[s][:, :]).then_inc(m_link, 1)
                    for n, to in enumerate((rw, lg)):
                        for s in range(G):
                            dve.wait_ge(m_link, linked(k + 3, s))
                            V.scalar_tensor_tensor(to[s][:, :], iota[:, :], idxf[s][:, n:n + 1], prob[s][:, :],
                                                   ALU.is_equal, ALU.mult).then_inc(m_link, 1)
                    for s in range(G):
                        dve.wait_ge(m_link, linked(k + 5, s))
                        V.tensor_tensor(rw[s][:, :], rw[s][:, :], lg[s][:, :], ALU.add).then_inc(m_route if base else m_link, 1)
                    if not base:
                        for k, done_ in ((10, m_link), (14, m_route)):
                            r = 0 if k == 10 else 1
                            for s in range(G):
                                dve.wait_ge(m_link, linked(k, s))
                                V.tensor_reduce(col[s][:, r:r + 1], rw[s][:, :], AX.X, ALU.add).then_inc(m_link, 1)
                            for s in range(G):
                                dve.wait_ge(m_link, linked(k + 1, s))
                                V.tensor_scalar(col[s][:, r:r + 1], col[s][:, r:r + 1], 1e-9, None, ALU.add).then_inc(m_link, 1)
                            for s in range(G):
                                dve.wait_ge(m_link, linked(k + 2, s))
                                V.reciprocal(col[s][:, 2 + r:3 + r], col[s][:, r:r + 1]).then_inc(m_link, 1)
                            for s in range(G):
                                dve.wait_ge(m_link, linked(k + 3, s))
                                V.tensor_scalar(rw[s][:, :], rw[s][:, :], col[s][:, 2 + r:3 + r], None, ALU.mult).then_inc(done_, 1)
                    done = 0
                    for g, experts in enumerate(m["groups"]):
                        n = 512 if not base else 256 * len(experts)
                        for s in range(G):
                            dve.wait_ge(m_silu, nth_group(base, it, s, NG, g))
                            V.tensor_tensor(AT[s][:, 0:n], SG[s][:, 0:n], ps[s][:, 3, 0:n], ALU.mult).then_inc(m_act, 1)
                        for s in range(G):
                            if g == 0:
                                dve.wait_ge(m_route, nth(mi, it, s))
                        for k, e in enumerate(experts):
                            for s in range(G):
                                y = ps[s][:, g % 2, k * D:(k + 1) * D]
                                w = 1.0 if e < first else rw[s][:, e - first:e - first + 1]
                                sync = m_acc if k == len(experts) - 1 else m_part
                                if k == 0:
                                    dve.wait_ge(m_dn_ps, nth_group(base, it, s, NG, g))
                                if e == 0:
                                    op = V.tensor_scalar(acc[s], y, w, None, ALU.mult)
                                else:
                                    if k == 0:
                                        dve.wait_ge(m_acc, nth_group(base, it, s, NG, g - 1))
                                    else:
                                        dve.wait_ge(m_part, m["part0"] + it * (G * m["parts"]) + done + s + 1 - G)
                                    op = V.scalar_tensor_tensor(acc[s], y, w, acc[s], ALU.mult, ALU.add)
                                op.then_inc(sync, 1)
                            if k < len(experts) - 1:
                                done += G
                    for s in range(G):
                        dve.wait_ge(m_acc, nth_group(base, it, s, NG, NG - 1))
                        V.scalar_tensor_tensor(X[:, it * G + s, :], acc[s], m["gate"], xw[s][:, :], ALU.mult, ALU.add).then_inc(x_updated, 1)

            def linear_attention():
                with dve.Fori(0, IT) as it:
                    norm_steps(LN3, NO[LN3], it, normed)
                    for s in range(G):
                        dve.wait_ge(t_k, 2 + 2 * it + s + 1)
                        V.tensor_reduce(col[s][:, :], K3[s], AX.X, ALU.max).then_inc(t_klink, 1)
                    for s in range(G):
                        dve.wait_ge(t_klink, nth(0, it, s, 1))
                        V.tensor_tensor(K3E[s], K3[s], col[s][:, :, None].to_broadcast([128, 4, KEYS3]), ALU.subtract).then_inc(t_kshift, 1)
                    for s in range(G):
                        dve.wait_ge(q_ps, nth(48, it, s))
                        V.bn_stats(st[s][:, 0:6], ps[s][:, 1, :]).then_inc(t_qlink, 1)
                        dve.compute_val(nth(0, it, s, 2, 0))
                        dve.wait_ge(x_loaded, 16)
                        dve.wait_ge(t_qlink, nth(0, it, s, 2, 0))
                        V.bn_aggr(mv[s][:, :], st[s][:, 0:6]).then_inc(t_qlink, 1)
                    for s in range(G):
                        dve.wait_ge(t_kexp, nth(0, it, s))
                        V.tensor_reduce(rc[s][:, 0:4], K3E[s], AX.X, ALU.add).then_inc(o_recip, 1)
                    for s in range(G):
                        dve.wait_ge(o_recip, 48 + 4 * it + s + 1)
                        V.reciprocal(rc[s][:, 4:8], rc[s][:, 0:4]).then_inc(o_recip, 1)
                    for s in range(G):
                        dve.wait_ge(t_qrs, nth(0, it, s))
                        V.tensor_scalar(Q3[s], ps[s][:, 1, :], mv[s][:, 0:1], rs[s][:, 0:1], ALU.subtract, ALU.mult).then_inc(t_qg, 1)
                    for s in range(G):
                        dve.wait_ge(t_qg, it * 8 + s + 1)
                        V.tensor_tensor(Q3[s], Q3[s], qg, ALU.mult).then_inc(t_qg, 1)
                    for s in range(G):
                        dve.wait_ge(t_qg, it * 8 + 2 + s + 1)
                        V.tensor_tensor(Q3[s], Q3[s], qb, ALU.add).then_inc(t_qg, 1)
                    q8 = lambda s: Q3[s].rearrange("p (h d) -> p h d", d=D3)
                    for s in range(G):
                        dve.wait_ge(t_qg, it * 8 + 4 + s + 1)
                        V.tensor_reduce(mx[s][:, 0:8], q8(s), AX.X, ALU.max).then_inc(t_qg, 1)
                    for s in range(G):
                        dve.wait_ge(t_qg, it * 8 + 6 + s + 1)
                        V.tensor_tensor(q8(s), q8(s), mx[s][:, 0:8, None].to_broadcast([S, 8, D3]), ALU.subtract).then_inc(t_qshift, 1)
                    for s in range(G):
                        dve.wait_ge(o_recip, 48 + 4 * it + 2 + s + 1)
                        dve.wait_ge(t_c_ps, nth(0, it, s))
                        for c in range(4):
                            last = V.scalar_tensor_tensor(C3[s][:, c, :], ps[s][:, 3, c * 128:(c + 1) * 128], rc[s][:, 4 + c:5 + c],
                                                          blockpair[:, :], ALU.mult, ALU.mult)
                        last.then_inc(t_c, 1)
                    for s in range(G):
                        dve.wait_ge(t_qexp, nth(0, it, s))
                        V.tensor_reduce(mx[s][:, 0:8], q8(s), AX.X, ALU.add).then_inc(sc_max, 1)
                    for s in range(G):
                        dve.wait_ge(sc_max, 48 + 4 * it + s + 1)
                        V.reciprocal(mx[s][:, 8:16], mx[s][:, 0:8]).then_inc(sc_max, 1)
                    for s in range(G):
                        dve.wait_ge(sc_max, 48 + 4 * it + 2 + s + 1)
                        V.tensor_scalar(mx[s][:, 0:8], mx[s][:, 8:16], 8.0, None, ALU.mult).then_inc(sc_masked, 1)
                    for s in range(G):
                        dve.wait_ge(sc_masked, nth(32, it, s))
                        dve.wait_ge(t_o_ps, nth(0, it, s))
                        V.tensor_tensor(O3[s].rearrange("p (h e) -> p h e", e=D3), ps[s][:, 1, :].rearrange("p (h e) -> p h e", e=D3),
                                        mx[s][:, 0:8, None].to_broadcast([S, 8, D3]), ALU.mult).then_inc(o_ready, 1)
                    for s in range(G):
                        dve.wait_ge(o_ready, nth(48, it, s))
                        V.bn_stats(st[s][:, 0:6], O3[s]).then_inc(t_olink, 1)
                        dve.compute_val(nth(0, it, s, 2, 0))
                        dve.wait_ge(x_loaded, 16)
                        dve.wait_ge(t_olink, nth(0, it, s, 2, 0))
                        V.bn_aggr(mv[s][:, :], st[s][:, 0:6]).then_inc(t_olink, 1)
                    for s in range(G):
                        dve.wait_ge(t_ors, nth(0, it, s))
                        V.tensor_scalar(O3[s], O3[s], mv[s][:, 0:1], rs[s][:, 0:1], ALU.subtract, ALU.mult).then_inc(t_o, 1)
                    for s in range(G):
                        dve.wait_ge(t_y_ps, nth(0, it, s))
                        V.scalar_tensor_tensor(X[:, it * G + s, :], ps[s][:, 3, 0:D], gates[:, 0, 3:4], xw[s][:, :], ALU.mult, ALU.add).then_inc(x_updated, 1)

            def chosen_expert():
                with dve.Fori(0, IT) as it:
                    norm_steps(LN3F, NO[LN3F], it, normed)
                    for s in range(G):
                        dve.wait_ge(m_lg_ps, nth(32, it, s))
                        V.tensor_tensor(lg[s][0:1, :], ps[s][0:1, 1, 0:8], moe3_rb[0:1, :], ALU.add).then_inc(m_shift, 1)
                    for s in range(G):
                        dve.wait_ge(x_loaded, 16)
                        dve.wait_ge(m_shift, nth(32, it, s))
                        V.max(top8[s][0:1, :], lg[s][0:1, :]).then_inc(m_prob, 1)
                    for s in range(G):
                        dve.wait_ge(x_loaded, 16)
                        dve.wait_ge(m_prob, nth(32 + 0, it, s))
                        V.max_index(idx[s][0:1, :], top8[s][0:1, :], lg[s][0:1, :]).then_inc(m_route, 1)
                    for s in range(G):
                        dve.wait_ge(m_dn_ps, nth(16 * 7, it, s))
                        V.tensor_tensor(acc[s], ps[s][:, 3, 0:D], FB2[s], ALU.add).then_inc(m_acc, 1)
                    for s in range(G):
                        dve.wait_ge(m_acc, nth(16 * 7, it, s))
                        V.scalar_tensor_tensor(X[:, it * G + s, :], acc[s], gates[:, 1, 3:4], xw[s][:, :], ALU.mult, ALU.add).then_inc(x_updated, 1)

            V.memset(seed[:, :], 0.0).then_inc(x_updated, G)
            dve.wait_ge(x_updated, G)
            V.memset(seed[:, :], 0.0).then_inc(ffn_done, G)
            dve.wait_ge(x_loaded, 16)
            dve.wait_ge(w0_loaded, 96)
            dve.wait_ge(gates_ready, 1)
            attention(XA[0], 0)
            dve.wait_ge(w1_loaded, 176)
            V.tensor_copy(ident_b[:, :], ident[:, :]).then_inc(consts_cast, 1)
            V.tensor_copy(band_b[:, :], band_f[:, :]).then_inc(consts_cast, 1)
            with dve.Fori(0, IT) as it:
                def start(s):
                    V.tensor_scalar(Y[:, it * G + s, :], xw[s][:, :], mv[s][:, 0:1], rs[s][:, 0:1],
                                    ALU.subtract, ALU.mult).then_inc(x_updated, 1)
                norm_steps(LNY, None, it, start)
            dve.wait_ge(x_updated, G + LN1)
            with dve.Fori(0, DEPTH // 2) as lp:
                for p in range(2):
                    local_layer(p, lp)
            dve.wait_ge(ffn_done, G + DEPTH * B)
            allx = lambda t: t[:, :, :].rearrange("p b d -> p (b d)")
            V.scalar_tensor_tensor(allx(X), allx(Y), gates[:, 1, 0:1], allx(X), ALU.mult, ALU.add).then_inc(ffn_gated, 1)
            dve.wait_ge(ffn_gated, 1)
            attention(XA[1], 1)
            mixture(MOE[0])
            dve.wait_ge(late_loaded, 288)
            V.tensor_tensor(side[:, :], side[:, :], side[:, :], ALU.add).then_inc(late_prep, 1)
            V.tensor_scalar(bq_s, bqkv[:, 0:1], 8 ** -0.5, None, ALU.mult).then_inc(late_prep, 1)
            dve.wait_ge(late_prep, 2)
            attention(XA[2], 2)
            mixture(MOE[1])
            linear_attention()
            chosen_expert()


def inputs_of(a):
    c = np.ascontiguousarray
    f = {k: np.asarray(v) for k, v in a.items()}
    col = lambda v: v.reshape(-1, 1)
    row = lambda v: v.reshape(1, -1)
    d = dict(constants())
    d["x"] = c(f["x"].transpose(1, 0, 2))
    d["ctxT"] = c(f["ctx_1024"].transpose(2, 0, 1))
    d["g_xattn"], d["g_ffn"] = row(f["g_xattn"]), row(f["g_ffn"])
    d["side"] = f["fside_SxS2_0"]
    w0 = np.zeros((D, 2, D), np.float32)
    for h in range(16):
        w0[h * 8:h * 8 + 8, 0, h * 8:h * 8 + 8] = f["L0_xattn_W1"].T
    w0[:, 1, :] = f["L0_xattn_W2"].T
    d["w0"] = w0
    d["q_scale"], d["k_scale"] = f["L0_ffn_q_scale"], f["L0_ffn_k_scale"]
    d["wqkv"] = f["L0_ffn_Wqkv"]
    d["wout"] = c(f["L0_ffn_Wo"].reshape(DEPTH, 8, 128, D).transpose(0, 2, 1, 3))
    d["wff1"], d["wff2"], d["bff2"] = f["L0_ffn_W1"], f["L0_ffn_W2"], f["L0_ffn_b2"]
    lcol = np.zeros((DEPTH, D, 8), np.float32)
    lcol[:, :, 0], lcol[:, :, 1] = f["L0_ffn_ln_g"], f["L0_ffn_ln_b"]
    for i, (lo, hi) in enumerate(HC):
        lcol[:, 0:hi - lo, 2 + i] = f["L0_ffn_b1"][:, lo:hi]
        lcol[:, 0:hi - lo, 5 + i] = f["L0_ffn_b1"][:, HID + lo:HID + hi]
    d["lcol"] = lcol
    chunks = lambda w: w.reshape(4, 128, D).transpose(1, 0, 2)
    d["w1"] = c(np.stack([f["L1_xattn_Wq"], f["L1_xattn_Wkv"][:, :512], f["L1_xattn_Wkv"][:, 512:],
                          chunks(f["L1_xattn_Wo"]).reshape(128, 512)], 1))
    d["aff1"] = c(np.stack([f["L1_xattn_ln_scale"], f["L1_xattn_ln_bias"]], 1))
    d["moe1_r"] = c(f["L1_ffn_gate_w"].T)
    d["moe1_gu"] = c(f["L1_ffn_gate_up_proj"].transpose(1, 0, 2))
    d["moe1_d"] = c(f["L1_ffn_down_proj"].transpose(1, 0, 2))
    wqkv = f["L2_xattn_Wqkv"]
    d["w2"] = c(np.stack([wqkv[:D].T, wqkv[D:2 * D].T, wqkv[2 * D:].T, f["L2_xattn_Wo"].T], 1))
    d["bqkv"] = c(f["L2_xattn_bqkv"].reshape(3, D).T)
    d["bo2"] = row(f["L2_xattn_bo"])
    both = lambda s, e: np.concatenate([f[s][None], f[e]], 0)
    d["moe2_g"] = c(both("L2_ffn_Wg_s", "L2_ffn_Wg").transpose(2, 0, 1))
    d["moe2_u"] = c(both("L2_ffn_Wu_s", "L2_ffn_Wu").transpose(2, 0, 1))
    d["moe2_d"] = c(both("L2_ffn_Wd_s", "L2_ffn_Wd").transpose(2, 0, 1).reshape(2, 128, E2, D).transpose(1, 2, 0, 3))
    d["moe2_r"], d["moe2_rb"] = c(f["L2_ffn_Wr"].T), row(f["L2_ffn_rb"])
    d["w3"] = c(np.stack([f["L3_xattn_Wq"], f["L3_xattn_Wkv"][:, :512], f["L3_xattn_Wkv"][:, 512:]], 1))
    d["w3o"] = c(chunks(f["L3_xattn_Wout"]))
    d["nullk"] = c(col(np.tile(f["L3_xattn_null_kv"][0], 2)))
    d["nullv"] = row(np.tile(f["L3_xattn_null_kv"][1], 8))
    d["qg"], d["qb"] = row(f["L3_xattn_ln_q_g"]), row(f["L3_xattn_ln_q_b"])
    d["og"], d["ob"] = c(f["L3_xattn_ln_out_g"].reshape(4, 128).T), c(f["L3_xattn_ln_out_b"].reshape(4, 128).T)
    d["moe3_r"], d["moe3_rb"] = f["L3_ffn_Wr"], row(f["L3_ffn_br"])
    d["moe3_w1"] = f["L3_ffn_W1"]
    d["moe3_w2"] = c(f["L3_ffn_W2"].reshape(8, 4, 128, D).transpose(0, 2, 1, 3))
    d["moe3_b1"] = c(f["L3_ffn_b1"].reshape(8, 4, 128).transpose(0, 2, 1))
    d["moe3_b2"] = f["L3_ffn_b2"]
    return {k: c(v) for k, v in d.items()}


def kernel(**inputs):
    import concourse.bacc as bacc
    from concourse.bass_utils import run_bass_kernel_spmd

    arrays = inputs_of(inputs)
    nc = bacc.Bacc("TRN2", target_bir_lowering=False, num_devices=1)
    dram = {k: nc.dram_tensor(f"in_{k}", v.shape, mybir.dt.from_np(v.dtype), kind="ExternalInput").ap() for k, v in arrays.items()}
    out = nc.dram_tensor("out_x", (S, B, D), F32, kind="ExternalOutput").ap()
    program(nc, dram, out)
    r = run_bass_kernel_spmd(nc, [{f"in_{k}": v for k, v in arrays.items()}], core_ids=[0])
    return np.ascontiguousarray(r.results[0]["out_x"].transpose(1, 0, 2))
```

```python
from contextlib import ExitStack

import numpy as np

import concourse.bass as bass
from concourse import mybir

F32 = mybir.dt.float32
BF16 = mybir.dt.bfloat16
U32 = mybir.dt.uint32
ALU = mybir.AluOpType
ACT = mybir.ActivationFunctionType
AX = mybir.AxisListType

B, S, D, M = 16, 128, 128, 77
G = 2
IT = B // G
DEPTH, LH, LD = 6, 16, 64
QK_SCALE = 8.0
INNER = LH * LD
HID = int(D * 4 * 2 / 3)
HC = [(0, 128), (128, 256), (256, HID)]
WINDOW = 32
EPS = 1e-5
NEG = -1e25
E1, E2, E3 = 8, 9, 8
EH2 = 256
FF3 = 512
H3, D3 = 8, 64
ND = D // 128 * 4
KEYS3 = M + 1


def constants():
    t = np.arange(S)
    shift = np.zeros((S, S), np.float32)
    shift[t[:-1], t[1:]] = 1
    i, j = t[:, None], t[None, :]
    first = (i // WINDOW - 1) * WINDOW
    seen = (j <= i) & (j + WINDOW >= i) & (j >= first)
    half = np.arange(0, LD, 2, dtype=np.float32)
    inv = (np.float32(1) / np.float32(10000) ** (half / np.float32(LD))).astype(np.float32)
    f = t[:, None].astype(np.float32) * inv[None]
    base = ((half + np.float32(0.4 * LD)) / np.float32(1.4 * LD)).astype(np.float32)
    power = ((t.astype(np.float32) - S // 2) / np.float32(WINDOW // 2)).astype(np.float32)
    scale = (base[None] ** power[:, None]).astype(np.float32)
    two = lambda a: np.concatenate([a, a], 1)
    cos, sin, scale = two(np.cos(f)), two(np.sin(f)), two(scale)
    sin[:, :LD // 2] *= -1
    rot = np.stack([cos * scale, sin * scale, cos / scale, sin / scale], 1)
    d = np.arange(D)
    return {
        "ident": np.eye(S, dtype=np.float32),
        "shift": shift,
        "band": np.where(seen, 0, NEG).astype(np.float32),
        "causal": np.where(np.arange(M)[None] > t[:, None], NEG, 0).astype(np.float32),
        "heads16": (d[:, None] // 8 == np.arange(16)[None]).astype(np.float32),
        "heads2": (d[:, None] // 64 == np.arange(2)[None]).astype(np.float32),
        "pair": (d[:, None] // 64 == d[None] // 64).astype(np.float32),
        "rot": np.ascontiguousarray(rot, np.float32),
        "iota": np.tile(np.arange(8, dtype=np.float32)[None], (S, 1)),
    }


def program(nc, dram, out):
    ctx = ExitStack()
    with ctx:
        def sb(name, shape, dt=F32):
            return ctx.enter_context(nc.sbuf_tensor(name, list(shape), dt))

        def sem(name):
            return ctx.enter_context(nc.semaphore(name))

        def pair(name, shape, dt=F32):
            return [sb(f"{name}{s}", shape, dt) for s in range(G)]

        X = sb("X", [S, B, D])
        Y = sb("Y", [S, B, D])
        ident, shift = sb("ident", [S, S]), sb("shift", [S, S])
        band_f = sb("band_f", [S, S])
        ident_b, band_b = sb("ident_b", [S, S], BF16), sb("band_b", [S, S], BF16)
        causal = sb("causal", [S, M])
        heads16, heads2 = sb("heads16", [D, 16]), sb("heads2", [D, 2])
        blockpair = sb("blockpair", [D, D])
        iota = sb("iota", [S, 8])
        rot = sb("rot", [S, 4, LD])
        qk_scale = pair("qk_scale", [S, 2, LD])
        table = pair("table", [S, 2, 2, LD])
        gates = sb("gates", [S, 2, 4])
        eps_col, neghalf = sb("eps_col", [S, 1]), sb("neghalf", [S, 2 * LH])
        seed = sb("seed", [S, 1])
        w0 = sb("w0", [D, 2, D])
        w1 = sb("w1", [D, 4, 4 * D])
        aff1 = sb("aff1", [D, 2])
        moe1_r = sb("moe1_r", [D, E1])
        moe1_gu = sb("moe1_gu", [D, E1, 2 * D])
        moe1_d = sb("moe1_d", [D, E1, D])
        LW = 3 * INNER + INNER + 2 * HID + 3 * D + D
        lw = [sb(f"lw{p}", [D, LW]) for p in range(2)]
        lcol = [sb(f"lcol{p}", [D, 8]) for p in range(2)]
        wqkv = [t[:, 0:3 * INNER] for t in lw]
        o_ = 3 * INNER
        wout = [t[:, o_:o_ + INNER].rearrange("p (c n) -> p c n", n=D) for t in lw]
        o_ += INNER
        wff1 = [t[:, o_:o_ + 2 * HID] for t in lw]
        o_ += 2 * HID
        wff2 = [t[:, o_:o_ + 3 * D].rearrange("p (c n) -> p c n", n=D) for t in lw]
        o_ += 3 * D
        bff2 = [t[:, o_:o_ + D] for t in lw]
        moe2_g = lw[0][:, 0:E2 * EH2].rearrange("p (e n) -> p e n", n=EH2)
        moe2_u = lw[0][:, E2 * EH2:2 * E2 * EH2].rearrange("p (e n) -> p e n", n=EH2)
        o_ = 2 * E2 * EH2
        w2 = lw[0][:, o_:o_ + 4 * D].rearrange("p (k n) -> p k n", n=D)
        moe2_d = lw[1][:, 0:E2 * EH2].rearrange("p (e c n) -> p e c n", e=E2, n=D)
        o_ = E2 * EH2
        w3 = lw[1][:, o_:o_ + 3 * 512].rearrange("p (k n) -> p k n", n=512)
        o_ += 3 * 512
        w3o = lw[1][:, o_:o_ + 512].rearrange("p (c n) -> p c n", n=D)
        o_ += 512
        small = sb("small", [D, 1100])
        qg, qb = small[:, 0:512], small[:, 512:1024]
        og, ob = small[:, 1024:1028], small[:, 1028:1032]
        bqkv, bq_s = small[:, 1032:1035], small[:, 1035:1036]
        nullk = small[:, 1036:1037]
        moe2_r, moe2_rb = small[:, 1040:1048], small[:, 1048:1056]
        moe3_r, moe3_rb = small[:, 1056:1064], small[:, 1064:1072]
        bo2 = sb("bo2", [S, D])
        xw = pair("xw", [S, D])
        xn = pair("xn", [S, D])
        xnT = pair("xnT", [D, S])
        st, mv, ve, rs = (pair(n, [S, k]) for n, k in (("st", 12), ("mv", 2), ("ve", 1), ("rs", 1)))
        ctxT = pair("ctxT", [D, M])
        area = pair("area", [128, 5 * 2 * INNER + LH * (LD + 1) + 12 * 128])
        K2 = 2 * INNER

        def part(s, at, n, p=128):
            return area[s][0:p, at:at + n]

        bufs = range(G)
        KN = [part(s, INNER, INNER) for s in bufs]
        SQ = [part(s, K2, K2) for s in bufs]
        QR = [part(s, 2 * K2, K2) for s in bufs]
        RA = [part(s, 3 * K2, K2) for s in bufs]
        QKT = [part(s, 4 * K2, K2) for s in bufs]
        LV = [part(s, 5 * K2, LH * (LD + 1)).rearrange("p (h e) -> p h e", e=LD + 1) for s in bufs]
        at_ = 5 * K2 + LH * (LD + 1)
        hidT = [part(s, at_, 384).rearrange("p (c n) -> p c n", n=S) for s in bufs]
        geluT = [part(s, at_ + 384, 384).rearrange("p (c n) -> p c n", n=S) for s in bufs]
        xsT = [part(s, at_ + 768, S) for s in bufs]
        y1 = [part(s, at_ + 896, D) for s in bufs]
        yb = [part(s, at_ + 1024, D) for s in bufs]
        LP, LPT = SQ, RA
        LO = [part(s, 0, INNER) for s in bufs]
        LOT = [part(s, INNER, INNER).rearrange("p (c n) -> p c n", n=S) for s in bufs]
        XQT = [part(s, 0, 512) for s in bufs]
        XKT = [part(s, 512, 4 * M) for s in bufs]
        XKX = [part(s, 1024, 16 * M) for s in bufs]
        XP = [part(s, K2 + 512, 16 * M) for s in bufs]
        XPT = [part(s, 2 * K2, K2, M) for s in bufs]
        XV = [part(s, 3 * K2, 8 * 65, M) for s in bufs]
        XO = [part(s, 3 * K2 + 1024, 512) for s in bufs]
        XOT = [part(s, 4 * K2, 512) for s in bufs]
        xt = [part(s, 4 * K2 + 512, D) for s in bufs]
        SG = [part(s, 0, 512) for s in bufs]
        AT = [part(s, 512, 512) for s in bufs]
        acc = [part(s, 1024, D) for s in bufs]
        Q3 = [part(s, 0, 512) for s in bufs]
        Q3T = [part(s, 512, 512).rearrange("p (c n) -> p c n", n=S) for s in bufs]
        K3 = [part(s, 1024, 4 * KEYS3).rearrange("p (c n) -> p c n", n=KEYS3) for s in bufs]
        K3T = [part(s, 1536, 512, KEYS3) for s in bufs]
        V3 = [part(s, 2048, 512, KEYS3) for s in bufs]
        C3 = [part(s, 2560, 512).rearrange("p (c n) -> p c n", n=D) for s in bufs]
        O3 = [part(s, 3072, 512) for s in bufs]
        O3T = [part(s, 3584, 512).rearrange("p (c n) -> p c n", n=S) for s in bufs]
        K3E = [part(s, 4096, 4 * KEYS3).rearrange("p (c n) -> p c n", n=KEYS3) for s in bufs]
        F1 = [part(s, 5000, FF3) for s in bufs]
        F2 = [part(s, 5512, FF3).rearrange("p (c n) -> p c n", n=D) for s in bufs]
        FB1 = [part(s, 6024, 4) for s in bufs]
        FB2 = [part(s, 6028, D) for s in bufs]
        F1T = [part(s, 6200, FF3).rearrange("p (c n) -> p c n", n=S) for s in bufs]
        ssq, rnq = pair("ssq", [S, 2 * LH]), pair("rnq", [S, 2 * LH])
        mx, negmx = pair("mx", [S, 16]), pair("negmx", [S, 16])
        rc = pair("rc", [S, 16])
        lg, pr, top8 = pair("lg", [S, 8]), pair("pr", [S, 8]), pair("top8", [S, 8])
        idx, idxf = pair("idx", [S, 8], U32), pair("idxf", [S, 8])
        sel, rw, col = pair("sel", [S, 8]), pair("rw", [S, 8]), pair("col", [S, 4])
        tokmean = pair("tokmean", [D, 1])

        ps = [ctx.enter_context(nc.psum_tensor(f"ps{s}", [128, 4, 512], F32)) for s in range(G)]

        x_loaded, w0_loaded, w1_loaded = sem("x_loaded"), sem("w0_loaded"), sem("w1_loaded")
        lw_loaded = [sem("lw_loaded0"), sem("lw_loaded1")]
        late_loaded = sem("late_loaded")
        ctx_loaded = [sem("ctx_loaded0"), sem("ctx_loaded1")]
        expert_loaded = [sem("expert_loaded0"), sem("expert_loaded1")]
        stored = sem("stored")
        consts_cast, tables_ready, gates_ready = sem("consts_cast"), sem("tables_ready"), sem("gates_ready")
        table_link, late_prep = sem("table_link"), sem("late_prep")
        v_ones = sem("v_ones")
        x_updated, ffn_done, ffn_gated = sem("x_updated"), sem("ffn_done"), sem("ffn_gated")
        xw_ready, ln_stats, ln_mean, ln_var, ln_rstd = (sem(n) for n in ("xw_ready", "ln_stats", "ln_mean", "ln_var", "ln_rstd"))
        x_normed, xnT_ps, xnT_ready = sem("x_normed"), sem("xnT_ps"), sem("xnT_ready")
        ln2_stats, ln2_mean, ln2_var, ln2_rstd, x_normed2 = (sem(n) for n in ("ln2_stats", "ln2_mean", "ln2_var", "ln2_rstd", "x_normed2"))
        k_ps, v_ps, q_ps, kT_ready, v_ready, kx_ready, qT_ready = (sem(n) for n in ("k_ps", "v_ps", "q_ps", "kT_ready", "v_ready", "kx_ready", "qT_ready"))
        sc_ps, sc_masked, sc_max, sc_shifted, sc_exp = (sem(n) for n in ("sc_ps", "sc_masked", "sc_max", "sc_shifted", "sc_exp"))
        pT_ps, pT_act, pT_dve, o_ps, o_recip, o_ready, oT_ps, oT_ready, y_ps, y_biased = (
            sem(n) for n in ("pT_ps", "pT_act", "pT_dve", "o_ps", "o_recip", "o_ready", "oT_ps", "oT_ready", "y_ps", "y_biased"))
        l_y, l_xsT_ps, l_xsT, l_qk_ps, l_sq, l_ss, l_ssf, l_rn, l_kn, l_ra, l_rb, l_rot_q, l_rot_k = (
            sem("l_" + n) for n in ("y", "xsT_ps", "xsT", "qk_ps", "sq", "ss", "ssf", "rn", "kn", "ra", "rb", "rot_q", "rot_k"))
        l_qkT_ps, l_qkT, l_v_ps, l_v, l_sc_ps, l_max, l_shift, l_exp, l_pT_ps, l_pT, l_pv_ps, l_rc, l_o = (
            sem("l_" + n) for n in ("qkT_ps", "qkT", "v_ps", "v", "sc_ps", "max", "shift", "exp", "pT_ps", "pT", "pv_ps", "rc", "o"))
        l_oT_ps, l_oT, l_att_ps, l_y1, l_yb, l_sh_ps, l_st, l_mv, l_ve, l_rs, l_xn, l_xnT_ps, l_xnT = (
            sem("l_" + n) for n in ("oT_ps", "oT", "att_ps", "y1", "yb", "sh_ps", "st", "mv", "ve", "rs", "xn", "xnT_ps", "xnT"))
        l_gate_ps, l_gelu, l_hid, l_ff_ps = (sem("l_" + n) for n in ("gate_ps", "gelu", "hid", "ff_ps"))
        m_lg_ps, m_link, m_shift, m_prob, m_route, m_gu_ps, m_silu, m_act, m_dn_ps, m_part, m_acc = (
            sem("m_" + n) for n in ("lg_ps", "link", "shift", "prob", "route", "gu_ps", "silu", "act", "dn_ps", "part", "acc"))
        e_xT = sem("e_xT")
        t_v, t_k, t_klink, t_kshift, t_kexp, t_kT_ps, t_kT, t_c_ps, t_c = (
            sem("t_" + n) for n in ("v", "k", "klink", "kshift", "kexp", "kT_ps", "kT", "c_ps", "c"))
        t_qlink, t_qvar, t_qrs, t_qg, t_qshift, t_qexp, t_qT_ps, t_qT, t_o_ps, t_olink, t_ovar, t_ors, t_o, t_oT_ps, t_oT, t_y_ps = (
            sem("t_" + n) for n in ("qlink", "qvar", "qrs", "qg", "qshift", "qexp", "qT_ps", "qT", "o_ps", "olink", "ovar", "ors", "o", "oT_ps", "oT", "y_ps"))

        LN0, LNY, LN1, LN1F, LN2, LN2F, LN3, LN3F = (16 * i for i in range(8))
        NO = {LN0: 0, LN1: 16, LN1F: 32, LN2: 48, LN2F: 64, LN3: 80, LN3F: 96}

        def nth(base, it, s, per=1, k=0):
            return base * per + (it * G + s) * per + k + 1

        def nth_group(base, it, s, per, g):
            return base + it * (G * per) + g * G + s + 1

        def heads4(ap, m=M):
            return ap.rearrange("p (h m) -> p h m", m=m)

        XA = [
            dict(ln=LN0, H=16, dv=8, C=1, scale=8 ** -0.5, mask=causal, hm=heads16, wq=w0[:, 0, :], wk=w0[:, 0, :],
                 wv=w0[:, 0, :], wo=w0[:, 1:2, :], gate=gates[:, 0, 0:1]),
            dict(ln=LN1, H=8, dv=64, C=4, scale=64 ** -0.5, mask=None, hm=heads2, wq=w1[:, 0, :], wk=w1[:, 1, :],
                 wv=w1[:, 2, :], wo=w1[:, 3, :].rearrange("p (c n) -> p c n", n=D), gate=gates[:, 0, 1:2]),
            dict(ln=LN2, H=16, dv=8, C=1, scale=1.0, mask=None, hm=heads16, wq=w2[:, 0, :], wk=w2[:, 1, :],
                 wv=w2[:, 2, :], wo=w2[:, 3:4, :], gate=gates[:, 0, 2:3]),
        ]
        side = sb("side", [S, M])
        XA[2]["mask"] = side
        for a in XA:
            a["HB"] = a["H"] // 4
            a["OB"] = 4 if a["dv"] == 64 else 16

        def gu1(e):
            return [(moe1_gu[:, e, 0:D], moe1_gu[:, e, D:2 * D])]

        def gu2(e):
            return [(moe2_g[:, e, c * 128:(c + 1) * 128], moe2_u[:, e, c * 128:(c + 1) * 128]) for c in range(2)]

        MOE = [
            dict(ln=LN1F, groups=[[0, 1, 2, 3], [4, 5, 6, 7]], gu=gu1, down=lambda e: [moe1_d[:, e, :]], r=moe1_r[:, :],
                 base=0, part0=0, parts=6, link0=0, links=17, gate=gates[:, 1, 1:2]),
            dict(ln=LN2F, groups=[[0, 1], [2, 3], [4, 5], [6, 7], [8]], gu=gu2,
                 down=lambda e: [moe2_d[:, e, c, :] for c in range(2)], r=moe2_r, base=32, part0=96, parts=4, link0=16 * 17, links=5, gate=gates[:, 1, 2:3]),
        ]

        def keys_first(j):
            return (j + 2) % 4

        class At:

            def __init__(self, p, lp, pr):
                self.p, self.lp, self.pr = p, lp, pr
                self.l = lp * 2 + p
                self.it = lp * (2 * IT) + p * IT + pr

        def local_transformer(engine, halves, prepare=None):
            def layer(p, lp, last):
                with engine.Fori(0, IT - 1) as pr:
                    halves((1, At(p, lp, pr)), (0, At(p, lp, pr)))
                    halves((0, At(p, lp, pr + 1)), (1, At(p, lp, pr)))
                ahead = None if last else (0, At(1 - p, lp + p, 0))
                if prepare and not last:
                    prepare(1 - p, lp + p)
                halves((1, At(p, lp, IT - 1)), (0, At(p, lp, IT - 1)))
                halves(ahead, (1, At(p, lp, IT - 1)))

            if prepare:
                prepare(0, 0)
            halves((0, At(0, 0, 0)), None)
            with engine.Fori(0, DEPTH // 2 - 1) as lp:
                for p in range(2):
                    layer(p, lp, False)
            for p in range(2):
                layer(p, DEPTH // 2 - 1, p == 1)

        block = ctx.enter_context(nc.Block())

        @block.sync
        def _(sp):
            def load(dst, name, done):
                sp.dma_start(dst, dram[name]).then_inc(done, 16)

            def context(a, s, b):
                sp.dma_start(ctxT[s][:, :], dram["ctxT"][:, b, :]).then_inc(ctx_loaded[s], 16)

            load(X[:, :, :], "x", x_loaded)
            for dst, name in ((ident, "ident"), (heads16, "heads16"), (causal, "causal")):
                load(dst[:, :], name, w0_loaded)
            load(w0[:, :, :], "w0", w0_loaded)
            for s in range(G):
                context(0, s, s)
            for i, name in enumerate(("g_xattn", "g_ffn")):
                sp.dma_start(gates[:, i, :], dram[name].partition_broadcast(S)).then_inc(w0_loaded, 16)
            for dst, name in ((shift, "shift"), (band_f, "band")):
                load(dst[:, :], name, w1_loaded)
            load(rot[:, :, :], "rot", w1_loaded)
            for dst, name in ((heads2, "heads2"), (blockpair, "pair"), (iota, "iota"), (aff1, "aff1"), (moe1_r, "moe1_r")):
                load(dst[:, :], name, w1_loaded)
            for dst, name in ((w1, "w1"), (moe1_gu, "moe1_gu"), (moe1_d, "moe1_d")):
                load(dst[:, :, :], name, w1_loaded)

            def layer(p, l):
                for dst, src in (
                    (wqkv[p], dram["wqkv"][l, :, :]), (wout[p], dram["wout"][l, :, :, :]), (wff1[p], dram["wff1"][l, :, :]),
                    (wff2[p][:, 0:2, :], dram["wff2"][l, 0:256, :].rearrange("(c p) n -> p c n", p=128)),
                    (wff2[p][0:HID - 256, 2, :], dram["wff2"][l, 256:HID, :]),
                    (lcol[p][:, :], dram["lcol"][l, :, :]), (bff2[p], dram["bff2"][bass.ds(l, 1), :].partition_broadcast(S)),
                    (qk_scale[p][:, 0, :], dram["q_scale"][bass.ds(l, 1), :].partition_broadcast(S)),
                    (qk_scale[p][:, 1, :], dram["k_scale"][bass.ds(l, 1), :].partition_broadcast(S)),
                ):
                    sp.dma_start(dst, src).then_inc(lw_loaded[p], 16)

            for p in range(2):
                layer(p, p)

            def contexts(a):
                if a:
                    for s in range(G):
                        sp.wait_ge(v_ps, 16 * a)
                        context(a, s, s)
                with sp.Fori(0, IT - 1) as it:
                    for s in range(G):
                        sp.wait_ge(v_ps, nth(16 * a, it, s))
                        context(a, s, it * G + s + G)

            contexts(0)
            with sp.Fori(0, DEPTH // 2 - 1) as lp:
                for p in range(2):
                    sp.wait_ge(ffn_done, G + (lp * 2 + p + 1) * B)
                    layer(p, lp * 2 + p + 2)
            sp.wait_ge(ffn_done, G + DEPTH * B)
            for dst, name in ((moe2_g, "moe2_g"), (moe2_u, "moe2_u"), (w2, "w2"), (w3, "w3"), (w3o, "w3o")):
                load(dst, name, late_loaded)
            load(moe2_d, "moe2_d", late_loaded)
            load(side[:, :], "side", late_loaded)
            for dst, name in ((og, "og"), (ob, "ob"), (bqkv, "bqkv"), (nullk, "nullk"), (moe2_r, "moe2_r"), (moe3_r, "moe3_r")):
                load(dst, name, late_loaded)
            for dst, name in ((qg, "qg"), (qb, "qb"), (moe2_rb, "moe2_rb"), (moe3_rb, "moe3_rb"), (bo2[:, :], "bo2")):
                sp.dma_start(dst, dram[name].partition_broadcast(128)).then_inc(late_loaded, 16)
            contexts(1)
            contexts(2)
            for s in range(G):
                sp.wait_ge(x_updated, G + LN3)
                sp.dma_start(V3[s][M:KEYS3, :], dram["nullv"]).then_inc(expert_loaded[s], 16)
            for s in range(G):
                sp.wait_ge(v_ps, 48)
                context(3, s, s)
            with sp.Fori(0, IT - 1) as it:
                for s in range(G):
                    sp.wait_ge(v_ps, nth(48, it, s))
                    context(3, s, it * G + s + G)
            with sp.Fori(0, IT) as it:
                for s in range(G):
                    sp.compute_val(nth(32, it, s))
                    sp.wait_ge(x_loaded, 16)
                    sp.wait_ge(m_route, nth(32, it, s))
                    e = sp.value_load(idx[s][0:1, 0:1], min_val=0, max_val=E3 - 1)
                    for dst, src in (
                        (F1[s], dram["moe3_w1"][bass.ds(e, 1), :, :].rearrange("a p n -> (a p) n")),
                        (F2[s], dram["moe3_w2"][bass.ds(e, 1), :, :, :].rearrange("a p c n -> (a p) c n")),
                        (FB1[s], dram["moe3_b1"][bass.ds(e, 1), :, :].rearrange("a p n -> (a p) n")),
                        (FB2[s], dram["moe3_b2"][bass.ds(e, 1), :].partition_broadcast(S)),
                    ):
                        sp.dma_start(dst, src).then_inc(expert_loaded[s], 16)
            sp.wait_ge(x_updated, G + LN3F + 16)
            sp.wait_ge(ffn_gated, 1)
            sp.dma_start(out, X[:, :, :]).then_inc(stored, 16)
            sp.wait_ge(stored, 16)

        @block.tensor
        def _(pe):
            def transpose_x(k, it, s, ready, n):
                pe.wait_ge(ready, n)
                nc.tensor.transpose(ps[s][:, 0, 0:S], xn[s][:, :], ident[:, :]).then_inc(xnT_ps, 1)

            def attention(a, i):
                H, dv, C, HB, OB = a["H"], a["dv"], a["C"], a["HB"], a["OB"]
                no = NO[a["ln"]]
                with pe.Fori(0, IT) as it:
                    for s in range(G):
                        pe.wait_ge(ctx_loaded[s], 16 * (IT * i + it + 1))
                        pe.wait_ge(x_updated, nth(a["ln"], it, s))
                        for c in range(C):
                            last = nc.tensor.matmul(ps[s][:, 2, c * M:(c + 1) * M], a["wk"][:, c * 128:(c + 1) * 128],
                                                    ctxT[s][:, :], start=True, stop=True)
                        last.then_inc(k_ps, 1)
                        nc.tensor.matmul(ps[s][0:M, 3, 0:H * dv], ctxT[s][:, :], a["wv"],
                                         start=True, stop=True).then_inc(v_ps, 1)
                    for s in range(G):
                        if i == 1:
                            transpose_x(no, it, s, x_normed2, nth(0, it, s))
                        else:
                            transpose_x(no, it, s, x_normed, nth(no, it, s))
                    for s in range(G):
                        pe.wait_ge(xnT_ready, nth(no, it, s))
                        for c in range(C):
                            last = nc.tensor.matmul(ps[s][:, 1, c * S:(c + 1) * S], a["wq"][:, c * 128:(c + 1) * 128],
                                                    xnT[s][:, :], start=True, stop=True)
                        last.then_inc(q_ps, 1)
                    for s in range(G):
                        pe.wait_ge(kx_ready, nth(16 * i, it, s))
                        pe.wait_ge(v_ready, nth(16 * i, it, s))
                        pe.wait_ge(qT_ready, nth(16 * i, it, s))
                        for j in range(4):
                            c = j if C == 4 else 0
                            last = nc.tensor.matmul(ps[s][:, j, 0:HB * M], XQT[s][:, c * S:(c + 1) * S],
                                                    XKX[s][:, j * HB * M:(j + 1) * HB * M], start=True, stop=True)
                        last.then_inc(sc_ps, 1)
                    for s in range(G):
                        pe.wait_ge(sc_exp, nth(16 * i, it, s))
                        for h in range(H):
                            last = nc.tensor.transpose(ps[s][0:M, h // 4, (h % 4) * S:(h % 4 + 1) * S],
                                                       XP[s][:, h * M:(h + 1) * M], ident[:, :])
                        last.then_inc(pT_ps, 1)
                    for s in range(G):
                        pe.wait_ge(pT_act, nth(16 * i, it, s))
                        pe.wait_ge(pT_dve, nth(16 * i, it, s))
                        for h in range(H):
                            w = dv + 1
                            last = nc.tensor.matmul(ps[s][:, h // OB, (h % OB) * w:(h % OB + 1) * w],
                                                    XPT[s][:, h * S:(h + 1) * S], XV[s][:, h * w:(h + 1) * w],
                                                    start=True, stop=True)
                        last.then_inc(o_ps, 1)
                    for s in range(G):
                        pe.wait_ge(o_ready, nth(16 * i, it, s))
                        for c in range(C):
                            last = nc.tensor.transpose(ps[s][:, 2, c * S:(c + 1) * S], XO[s][:, c * 128:(c + 1) * 128],
                                                       ident[:, :])
                        last.then_inc(oT_ps, 1)
                    for s in range(G):
                        pe.wait_ge(oT_ready, nth(16 * i, it, s))
                        for c in range(C):
                            last = nc.tensor.matmul(ps[s][:, 3, 0:D], XOT[s][:, c * S:(c + 1) * S], a["wo"][:, c, :],
                                                    start=(c == 0), stop=(c == C - 1))
                        last.then_inc(y_ps, 1)

            def shifted(s, w):
                pe.wait_ge(l_y, nth(0, w.it, s))
                nc.tensor.matmul(ps[s][0:64, 0, 0:S], xw[s][:, 0:64], ident[:, :], start=True, stop=True)
                nc.tensor.matmul(ps[s][64:128, 0, 0:S], xw[s][:, 64:128], shift[:, :],
                                 start=True, stop=True).then_inc(l_xsT_ps, 1)

            def queries_keys(s, w, j):
                if j == 2:
                    pe.wait_ge(lw_loaded[w.p], 144 * (w.lp + 1))
                    pe.wait_ge(l_xsT, nth(0, w.it, s))
                nc.tensor.matmul(ps[s][:, j, :], xsT[s], wqkv[w.p][:, j * 512:(j + 1) * 512],
                                 start=True, stop=True).then_inc(l_qk_ps, 1)

            def queries_keys_T(s, w, j):
                pe.wait_ge(l_rot_q if j < 2 else l_rot_k, nth(0, w.it, s, 2, j % 2))
                for c in range(4):
                    last = nc.tensor.transpose(ps[s][:, j, c * S:(c + 1) * S],
                                               QR[s][:, j * 512 + c * 128:j * 512 + (c + 1) * 128], ident[:, :])
                last.then_inc(l_qkT_ps, 1)

            def values(s, w):
                pe.wait_ge(l_qkT, nth(0, w.it, s, 4, 3))
                for j in range(2):
                    nc.tensor.matmul(ps[s][:, 2 + j, :], xsT[s], wqkv[w.p][:, K2 + j * 512:K2 + (j + 1) * 512],
                                     start=True, stop=True).then_inc(l_v_ps, 1)

            def scores(s, w, g):
                if g < 2:
                    pe.wait_ge(l_qkT, nth(0, w.it, s, 4, g + 2))
                if g == 2:
                    pe.wait_ge(l_v, nth(0, w.it, s, 2, 1))
                odd, c0 = g // 2, (g % 2) * 4
                nc.tensor.matmul(ps[s][:, g, :].rearrange("p (c n) -> p c n", n=S), ident_b[:, :],
                                 band_b[:, None, :].to_broadcast([S, 4, S]), start=True, stop=False,
                                 skip_group_check=True)
                for c in range(4):
                    rows = slice(64 * odd, 64 * odd + 64)
                    cols = slice((c0 + c) * S, (c0 + c + 1) * S)
                    last = nc.tensor.matmul(ps[s][:, g, c * S:(c + 1) * S], QKT[s][rows, cols],
                                            QKT[s][rows, INNER + (c0 + c) * S:INNER + (c0 + c + 1) * S],
                                            start=False, stop=(c == 3), skip_group_check=True)
                last.then_inc(l_sc_ps, 1)

            def probs_T(s, w, g):
                pe.wait_ge(l_exp, nth(0, w.it, s, 4, g))
                for c in range(4):
                    last = nc.tensor.transpose(ps[s][:, g, c * S:(c + 1) * S],
                                               LP[s][:, g * 512 + c * S:g * 512 + (c + 1) * S], ident[:, :])
                last.then_inc(l_pT_ps, 1)

            def probs_values(s, w, g):
                pe.wait_ge(l_pT, nth(0, w.it, s, 4, g))
                for c in range(4):
                    h = 2 * ((g % 2) * 4 + c) + g // 2
                    last = nc.tensor.matmul(ps[s][:, g, c * 65:(c + 1) * 65],
                                            LPT[s][:, g * 512 + c * S:g * 512 + (c + 1) * S], LV[s][:, h, :],
                                            start=True, stop=True)
                last.then_inc(l_pv_ps, 1)

            def outputs_T(s, w):
                pe.wait_ge(l_o, nth(0, w.it, s, 4, 3))
                for j in range(2):
                    for c in range(4):
                        last = nc.tensor.transpose(ps[s][:, j, c * S:(c + 1) * S],
                                                   LO[s][:, (4 * j + c) * 128:(4 * j + c + 1) * 128], ident[:, :])
                    last.then_inc(l_oT_ps, 1)

            def project(s, w):
                for c in range(8):
                    if c % 4 == 0:
                        pe.wait_ge(l_oT, nth(0, w.it, s, 2, c // 4))
                    last = nc.tensor.matmul(ps[s][:, 2, 0:D], LOT[s][:, c, :], wout[w.p][:, c, :],
                                            start=(c == 0), stop=(c == 7))
                last.then_inc(l_att_ps, 1)

            def shift_back(s, w):
                pe.wait_ge(l_y1, nth(0, w.it, s))
                nc.tensor.matmul(ps[s][:, 3, 0:64], shift[:, :], y1[s][:, 64:128],
                                 start=True, stop=True).then_inc(l_sh_ps, 1)

            def normed_T(s, w):
                pe.wait_ge(l_xn, nth(0, w.it, s, 2, 1))
                nc.tensor.transpose(ps[s][:, 0, 0:S], xn[s][:, :], ident[:, :]).then_inc(l_xnT_ps, 1)

            def up(s, w):
                pe.wait_ge(l_xnT, nth(0, w.it, s))
                for bank, at in ((1, HID), (2, 0)):
                    for c, (lo, hi) in enumerate(HC):
                        last = nc.tensor.matmul(ps[s][0:hi - lo, bank, c * S:(c + 1) * S],
                                                wff1[w.p][:, at + lo:at + hi], xnT[s][:, :], start=True, stop=True)
                    last.then_inc(l_gate_ps, 1)

            def down(s, w):
                for c, (lo, hi) in enumerate(HC):
                    pe.wait_ge(l_hid, nth(0, w.it, s, 3, c))
                    last = nc.tensor.matmul(ps[s][:, 0, 128:256], hidT[s][0:hi - lo, c, :], wff2[w.p][0:hi - lo, c, :],
                                            start=(c == 0), stop=(c == 2))
                last.then_inc(l_ff_ps, 1)

            def halves(a, b):
                if b: probs_values(*b, 0)
                if a:
                    shifted(*a)
                    queries_keys(*a, 2)
                    queries_keys(*a, 3)
                if b: probs_T(*b, 1)
                if a:
                    queries_keys(*a, 0)
                    queries_keys(*a, 1)
                if b:
                    probs_values(*b, 1)
                    probs_T(*b, 2)
                    probs_T(*b, 3)
                    probs_values(*b, 2)
                    probs_values(*b, 3)
                if a: queries_keys_T(*a, 0)
                if b: outputs_T(*b)
                if a:
                    queries_keys_T(*a, 1)
                    queries_keys_T(*a, 2)
                if b: project(*b)
                if a: queries_keys_T(*a, 3)
                if b: shift_back(*b)
                if a:
                    scores(*a, 0)
                    values(*a)
                if b: normed_T(*b)
                if a: scores(*a, 1)
                if b: up(*b)
                if a:
                    probs_T(*a, 0)
                    scores(*a, 2)
                    scores(*a, 3)
                if b: down(*b)

            def mixture(m):
                no, base = NO[m["ln"]], m["base"]
                mi = 16 if base else 0
                NG = len(m["groups"])
                with pe.Fori(0, IT) as it:
                    for s in range(G):
                        transpose_x(no, it, s, x_normed, nth(no, it, s))
                    for s in range(G):
                        pe.wait_ge(xnT_ready, nth(no, it, s))
                        nc.tensor.matmul(ps[s][:, 1, 0:8], xnT[s][:, :], m["r"], start=True, stop=True).then_inc(m_lg_ps, 1)
                    for g, experts in enumerate(m["groups"]):
                        for s in range(G):
                            if g:
                                pe.wait_ge(m_act, nth_group(base, it, s, NG, g - 1))
                            u = 0
                            for e in experts:
                                for wg, wu in m["gu"](e):
                                    nc.tensor.matmul(ps[s][:, 2, u * S:(u + 1) * S], wg, xnT[s][:, :], start=True, stop=True)
                                    last = nc.tensor.matmul(ps[s][:, 3, u * S:(u + 1) * S], wu, xnT[s][:, :], start=True, stop=True)
                                    u += 1
                            last.then_inc(m_gu_ps, 1)
                        for s in range(G):
                            if g == 0:
                                pass
                            elif g == 1:
                                pe.wait_ge(m_shift, nth(mi, it, s))
                            else:
                                pe.wait_ge(m_acc, nth_group(base, it, s, NG, g - 2))
                            pe.wait_ge(m_act, nth_group(base, it, s, NG, g))
                            u = 0
                            for n, e in enumerate(experts):
                                wd = m["down"](e)
                                for c, w in enumerate(wd):
                                    last = nc.tensor.matmul(ps[s][:, g % 2, n * D:(n + 1) * D], AT[s][:, u * S:(u + 1) * S], w,
                                                            start=(c == 0), stop=(c == len(wd) - 1))
                                    u += 1
                            last.then_inc(m_dn_ps, 1)

            def linear_attention():
                no = NO[LN3]
                with pe.Fori(0, IT) as it:
                    for s in range(G):
                        pe.wait_ge(ctx_loaded[s], 16 * (IT * 3 + it + 1))
                        pe.wait_ge(x_updated, nth(LN3, it, s))
                        for c in range(4):
                            last = nc.tensor.matmul(ps[s][:, 2, c * M:(c + 1) * M], w3[:, 1, c * 128:(c + 1) * 128],
                                                    ctxT[s][:, :], start=True, stop=True)
                        last.then_inc(k_ps, 1)
                        nc.tensor.matmul(ps[s][0:M, 3, :], ctxT[s][:, :], w3[:, 2, :], start=True, stop=True).then_inc(v_ps, 1)
                    for s in range(G):
                        transpose_x(no, it, s, x_normed, nth(no, it, s))
                    for s in range(G):
                        pe.wait_ge(xnT_ready, nth(no, it, s))
                        nc.tensor.matmul(ps[s][:, 1, :], xnT[s][:, :], w3[:, 0, :], start=True, stop=True).then_inc(q_ps, 1)
                    for s in range(G):
                        pe.wait_ge(t_kexp, nth(0, it, s))
                        for c in range(4):
                            last = nc.tensor.transpose(ps[s][0:KEYS3, 2, c * 128:(c + 1) * 128], K3E[s][:, c, :], ident[:, :])
                        last.then_inc(t_kT_ps, 1)
                    for s in range(G):
                        pe.wait_ge(t_v, nth(0, it, s))
                        pe.wait_ge(t_kT, nth(0, it, s))
                        for c in range(4):
                            cols = slice(c * 128, (c + 1) * 128)
                            last = nc.tensor.matmul(ps[s][:, 3, cols], K3T[s][:, cols], V3[s][:, cols], start=True, stop=True)
                        last.then_inc(t_c_ps, 1)
                    for s in range(G):
                        pe.wait_ge(t_qexp, nth(0, it, s))
                        for c in range(4):
                            last = nc.tensor.transpose(ps[s][:, 0, c * S:(c + 1) * S], Q3[s][:, c * 128:(c + 1) * 128], ident[:, :])
                        last.then_inc(t_qT_ps, 1)
                    for s in range(G):
                        pe.wait_ge(t_c, nth(0, it, s))
                        pe.wait_ge(t_qT, nth(0, it, s))
                        for c in range(4):
                            last = nc.tensor.matmul(ps[s][:, 1, c * 128:(c + 1) * 128], Q3T[s][:, c, :], C3[s][:, c, :],
                                                    start=True, stop=True)
                        last.then_inc(t_o_ps, 1)
                    for s in range(G):
                        pe.wait_ge(t_o, nth(0, it, s))
                        for c in range(4):
                            last = nc.tensor.transpose(ps[s][:, 2, c * S:(c + 1) * S], O3[s][:, c * 128:(c + 1) * 128], ident[:, :])
                        last.then_inc(t_oT_ps, 1)
                    for s in range(G):
                        pe.wait_ge(t_oT, nth(0, it, s))
                        for c in range(4):
                            last = nc.tensor.matmul(ps[s][:, 3, 0:D], O3T[s][:, c, :], w3o[:, c, :],
                                                    start=(c == 0), stop=(c == 3))
                        last.then_inc(t_y_ps, 1)

            def chosen_expert():
                no = NO[LN3F]
                with pe.Fori(0, IT) as it:
                    for s in range(G):
                        transpose_x(no, it, s, x_normed, nth(no, it, s))
                    for s in range(G):
                        pe.wait_ge(xnT_ready, nth(no, it, s))
                        nc.tensor.matmul(ps[s][0:1, 1, 0:8], tokmean[s][:, :], moe3_r, start=True, stop=True).then_inc(m_lg_ps, 1)
                    for s in range(G):
                        pe.wait_ge(expert_loaded[s], 16 + 64 * (it + 1))
                        for c in range(4):
                            last = nc.tensor.matmul(ps[s][:, 2, c * S:(c + 1) * S], F1[s][:, c * 128:(c + 1) * 128], xnT[s][:, :],
                                                    start=True, stop=True)
                        last.then_inc(m_gu_ps, 1)
                    for s in range(G):
                        pe.wait_ge(m_silu, nth(16 * 7, it, s))
                        for c in range(4):
                            last = nc.tensor.matmul(ps[s][:, 3, 0:D], F1T[s][:, c, :], F2[s][:, c, :],
                                                    start=(c == 0), stop=(c == 3))
                        last.then_inc(m_dn_ps, 1)

            pe.wait_ge(w0_loaded, 96)
            attention(XA[0], 0)
            pe.wait_ge(consts_cast, 2)
            local_transformer(pe, halves)
            pe.wait_ge(ffn_gated, 1)
            pe.wait_ge(w1_loaded, 176)
            attention(XA[1], 1)
            mixture(MOE[0])
            pe.wait_ge(late_loaded, 288)
            attention(XA[2], 2)
            mixture(MOE[1])
            linear_attention()
            chosen_expert()

        @block.scalar
        def _(act):
            def copy(dst, src, **kw):
                return nc.scalar.activation(dst, src, ACT.Identity if kw else ACT.Copy, **kw)

            def attention(a, i):
                H, dv, C, no = a["H"], a["dv"], a["C"], NO[a["ln"]]
                with act.Fori(0, IT) as it:
                    for s in range(G):
                        act.wait_ge(k_ps, nth(16 * i, it, s))
                        kw = dict(bias=bqkv[:, 1:2]) if i == 2 else {}
                        copy(XKT[s][:, 0:C * M], ps[s][:, 2, 0:C * M], **kw).then_inc(kT_ready, 1)
                        act.wait_ge(v_ps, nth(16 * i, it, s))
                        copy(heads4(XV[s][:, 0:H * (dv + 1)], dv + 1)[:, :, 0:dv],
                             ps[s][0:M, 3, 0:H * dv].rearrange("p (h e) -> p h e", e=dv)).then_inc(v_ready, 1)
                    for s in range(G):
                        act.wait_ge(xnT_ps, nth(no, it, s))
                        kw = dict(scale=aff1[:, 0:1], bias=aff1[:, 1:2]) if i == 1 else {}
                        copy(xnT[s][:, :], ps[s][:, 0, 0:S], **kw).then_inc(xnT_ready, 1)
                    for s in range(G):
                        act.wait_ge(q_ps, nth(16 * i, it, s))
                        kw = dict(scale=8 ** -0.5, bias=bq_s) if i == 2 else {}
                        copy(XQT[s][:, 0:C * S], ps[s][:, 1, 0:C * S], **kw).then_inc(qT_ready, 1)
                    for s in range(G):
                        act.wait_ge(sc_shifted, nth(16 * i, it, s))
                        nc.scalar.activation(XP[s][:, 0:H * M], XP[s][:, 0:H * M], ACT.Exp, scale=a["scale"]).then_inc(sc_exp, 1)
                    for s in range(G):
                        act.wait_ge(pT_ps, nth(16 * i, it, s))
                        copy(XPT[s][:, 0:H * S // 2], ps[s][0:M, 0:H // 8, :].rearrange("p j n -> p (j n)")).then_inc(pT_act, 1)
                    for s in range(G):
                        act.wait_ge(oT_ps, nth(16 * i, it, s))
                        kw = dict(bias=bqkv[:, 2:3]) if i == 2 else {}
                        copy(XOT[s][:, 0:C * S], ps[s][:, 2, 0:C * S], **kw).then_inc(oT_ready, 1)

            def shifted(s, w):
                act.wait_ge(l_xsT_ps, nth(0, w.it, s))
                copy(xsT[s], ps[s][:, 0, 0:S]).then_inc(l_xsT, 1)

            def squares(s, w, j):
                act.wait_ge(l_qk_ps, nth(0, w.it, s, 4, keys_first(j)))
                nc.scalar.activation(SQ[s][:, j * 512:(j + 1) * 512], ps[s][:, j, :], ACT.Square).then_inc(l_sq, 1)

            def queries_keys_T(s, w, j):
                act.wait_ge(l_qkT_ps, nth(0, w.it, s, 4, j))
                copy(QKT[s][:, j * 512:(j + 1) * 512], ps[s][:, j, :]).then_inc(l_qkT, 1)

            def values(s, w):
                for j in range(2):
                    act.wait_ge(l_v_ps, nth(0, w.it, s, 2, j))
                    copy(LV[s][:, 8 * j:8 * j + 8, 0:LD], ps[s][:, 2 + j, :].rearrange("p (h e) -> p h e", e=LD)).then_inc(l_v, 1)

            def exponentials(s, w, g):
                act.wait_ge(l_shift, nth(0, w.it, s, 4, g))
                for c in range(4):
                    h = 2 * ((g % 2) * 4 + c) + g // 2
                    last = nc.scalar.activation(LP[s][:, g * 512 + c * S:g * 512 + (c + 1) * S], ps[s][:, g, c * S:(c + 1) * S],
                                                ACT.Exp, scale=rnq[s][:, h:h + 1], bias=negmx[s][:, 4 * g + c:4 * g + c + 1])
                last.then_inc(l_exp, 1)

            def probs_T(s, w, g):
                act.wait_ge(l_pT_ps, nth(0, w.it, s, 4, g))
                copy(LPT[s][:, g * 512:(g + 1) * 512], ps[s][:, g, :]).then_inc(l_pT, 1)

            def outputs_T(s, w):
                for j in range(2):
                    act.wait_ge(l_oT_ps, nth(0, w.it, s, 2, j))
                    copy(LOT[s][:, 4 * j:4 * j + 4, :].rearrange("p c n -> p (c n)"), ps[s][:, j, :]).then_inc(l_oT, 1)

            def normed_T(s, w):
                act.wait_ge(lw_loaded[w.p], 144 * (w.lp + 1))
                act.wait_ge(l_xnT_ps, nth(0, w.it, s))
                copy(xnT[s][:, :], ps[s][:, 0, 0:S], scale=lcol[w.p][:, 0:1], bias=lcol[w.p][:, 1:2]).then_inc(l_xnT, 1)

            def gelu(s, w):
                act.wait_ge(l_gate_ps, nth(0, w.it, s, 2, 0))
                for c, (lo, hi) in enumerate(HC):
                    nc.scalar.activation(geluT[s][0:hi - lo, c, :], ps[s][0:hi - lo, 1, c * S:(c + 1) * S], ACT.Gelu,
                                         bias=lcol[w.p][0:hi - lo, 5 + c:6 + c]).then_inc(l_gelu, 1)

            def halves(a, b):
                if b: exponentials(*b, 1)
                if a: shifted(*a)
                if b: exponentials(*b, 2)
                if a:
                    squares(*a, 2)
                    squares(*a, 3)
                if b: probs_T(*b, 1)
                if a: squares(*a, 0)
                if b: exponentials(*b, 3)
                if a: squares(*a, 1)
                if b:
                    probs_T(*b, 2)
                    probs_T(*b, 3)
                    outputs_T(*b)
                if a:
                    queries_keys_T(*a, 0)
                    queries_keys_T(*a, 1)
                    queries_keys_T(*a, 2)
                    queries_keys_T(*a, 3)
                    exponentials(*a, 0)
                if b: normed_T(*b)
                if a: values(*a)
                if b: gelu(*b)
                if a: probs_T(*a, 0)

            def mixture(m):
                no, base, NG = NO[m["ln"]], m["base"], len(m["groups"])
                mi = 16 if base else 0
                with act.Fori(0, IT) as it:
                    for s in range(G):
                        act.wait_ge(xnT_ps, nth(no, it, s))
                        copy(xnT[s][:, :], ps[s][:, 0, 0:S]).then_inc(xnT_ready, 1)
                    for s in range(G):
                        act.wait_ge(m_shift, nth(mi, it, s))
                        nc.scalar.activation(pr[s][:, :], lg[s][:, :], ACT.Sigmoid if base else ACT.Exp).then_inc(m_prob, 1)
                    for g, experts in enumerate(m["groups"]):
                        n = 512 if not base else 256 * len(experts)
                        for s in range(G):
                            act.wait_ge(m_gu_ps, nth_group(base, it, s, NG, g))
                            nc.scalar.activation(SG[s][:, 0:n], ps[s][:, 2, 0:n], ACT.Silu).then_inc(m_silu, 1)

            def linear_attention():
                no = NO[LN3]
                for s in range(G):
                    act.wait_ge(x_updated, LN3 + s + 1)
                    act.wait_ge(late_loaded, 288)
                    copy(K3[s][:, :, M], nullk.to_broadcast([128, 4])).then_inc(t_k, 1)
                with act.Fori(0, IT) as it:
                    for s in range(G):
                        act.wait_ge(k_ps, nth(48, it, s))
                        copy(K3[s][:, :, 0:M], ps[s][:, 2, 0:4 * M].rearrange("p (c n) -> p c n", n=M)).then_inc(t_k, 1)
                        act.wait_ge(v_ps, nth(48, it, s))
                        copy(V3[s][0:M, :], ps[s][0:M, 3, :]).then_inc(t_v, 1)
                    for s in range(G):
                        act.wait_ge(xnT_ps, nth(no, it, s))
                        copy(xnT[s][:, :], ps[s][:, 0, 0:S]).then_inc(xnT_ready, 1)
                    for s in range(G):
                        act.wait_ge(t_kshift, nth(0, it, s))
                        K = K3E[s].rearrange("p c n -> p (c n)")
                        nc.scalar.activation(K, K, ACT.Exp).then_inc(t_kexp, 1)
                    for s in range(G):
                        act.wait_ge(t_kT_ps, nth(0, it, s))
                        copy(K3T[s], ps[s][0:KEYS3, 2, :]).then_inc(t_kT, 1)
                    for s in range(G):
                        act.wait_ge(t_qshift, nth(0, it, s))
                        nc.scalar.activation(Q3[s], Q3[s], ACT.Exp).then_inc(t_qexp, 1)
                    for s in range(G):
                        act.wait_ge(t_qT_ps, nth(0, it, s))
                        copy(Q3T[s].rearrange("p c n -> p (c n)"), ps[s][:, 0, :]).then_inc(t_qT, 1)
                    for s in range(G):
                        act.wait_ge(t_oT_ps, nth(0, it, s))
                        for c in range(4):
                            last = copy(O3T[s][:, c, :], ps[s][:, 2, c * S:(c + 1) * S], scale=og[:, c:c + 1], bias=ob[:, c:c + 1])
                        last.then_inc(t_oT, 1)

            def chosen_expert():
                no = NO[LN3F]
                with act.Fori(0, IT) as it:
                    for s in range(G):
                        act.wait_ge(xnT_ps, nth(no, it, s))
                        copy(xnT[s][:, :], ps[s][:, 0, 0:S]).then_inc(e_xT, 1)
                        act.wait_ge(e_xT, nth(0, it, s))
                        nc.scalar.activation(F1T[s][:, 0, :], xnT[s][:, :], ACT.Copy, scale=1.0 / S,
                                             accum_out=tokmean[s][:, :]).then_inc(xnT_ready, 1)
                    for s in range(G):
                        act.wait_ge(m_gu_ps, nth(16 * 7, it, s))
                        for c in range(4):
                            last = nc.scalar.activation(F1T[s][:, c, :], ps[s][:, 2, c * S:(c + 1) * S], ACT.Relu, bias=FB1[s][:, c:c + 1])
                        last.then_inc(m_silu, 1)

            act.wait_ge(w0_loaded, 96)
            nc.scalar.activation(gates[:, :, :], gates[:, :, :], ACT.Tanh).then_inc(gates_ready, 1)
            act.wait_ge(v_ones, 2)
            attention(XA[0], 0)
            act.wait_ge(v_ones, 4)
            local_transformer(act, halves)
            act.wait_ge(w1_loaded, 176)
            act.wait_ge(v_ones, 6)
            attention(XA[1], 1)
            mixture(MOE[0])
            act.wait_ge(late_prep, 2)
            act.wait_ge(v_ones, 8)
            attention(XA[2], 2)
            mixture(MOE[1])
            linear_attention()
            chosen_expert()

        @block.gpsimd
        def _(pool):
            def layer_norms(base):
                with pool.Fori(0, IT) as it:
                    for s in range(G):
                        pool.wait_ge(ln_mean, nth(base, it, s))
                        pool.tensor_tensor(ve[s][:, :], mv[s][:, 1:2], eps_col[:, :], ALU.add).then_inc(ln_var, 1)
                        pool.wait_ge(ln_var, nth(base, it, s))
                        pool.tensor_tensor(rs[s][:, :], ve[s][:, :], neghalf[:, 0:1], ALU.pow).then_inc(ln_rstd, 1)

            def attention(a, i):
                H, C, hm = a["H"], a["C"], a["hm"]
                with pool.Fori(0, IT) as it:
                    for s in range(G):
                        pool.wait_ge(ln_mean, nth(a["ln"], it, s))
                        pool.tensor_tensor(ve[s][:, :], mv[s][:, 1:2], eps_col[:, :], ALU.add).then_inc(ln_var, 1)
                        pool.wait_ge(ln_var, nth(a["ln"], it, s))
                        pool.tensor_tensor(rs[s][:, :], ve[s][:, :], neghalf[:, 0:1], ALU.pow).then_inc(ln_rstd, 1)
                    if i == 1:
                        for s in range(G):
                            pool.wait_ge(ln2_mean, nth(0, it, s))
                            pool.tensor_tensor(ve[s][:, :], mv[s][:, 1:2], eps_col[:, :], ALU.add).then_inc(ln2_var, 1)
                            pool.wait_ge(ln2_var, nth(0, it, s))
                            pool.tensor_tensor(rs[s][:, :], ve[s][:, :], neghalf[:, 0:1], ALU.pow).then_inc(ln2_rstd, 1)
                    for s in range(G):
                        pool.wait_ge(kT_ready, nth(16 * i, it, s))
                        pool.wait_ge(x_updated, nth(a["ln"], it, s))
                        HQ = H // C
                        for c in range(C):
                            last = pool.tensor_tensor(heads4(XKX[s][:, c * HQ * M:(c + 1) * HQ * M]),
                                                      XKT[s][:, None, c * M:(c + 1) * M].to_broadcast([128, HQ, M]),
                                                      hm[:, :, None].to_broadcast([128, HQ, M]), ALU.mult)
                        last.then_inc(kx_ready, 1)

            def rotary_factors(p, lp):
                hd = LD // 2
                pool.wait_ge(lw_loaded[p], 144 * (lp + 1))
                for i in range(2):
                    pool.tensor_tensor(table[p][:, i, 0, :], qk_scale[p][:, i, :], rot[:, 2 * i, :], ALU.mult)
                    for lo, other in ((0, hd), (hd, 0)):
                        last = pool.tensor_tensor(table[p][:, i, 1, lo:lo + hd], qk_scale[p][:, i, other:other + hd],
                                                  rot[:, 2 * i + 1, lo:lo + hd], ALU.mult)
                last.then_inc(tables_ready, 1)

            def inverse_norms(s, w, i):
                pool.wait_ge(l_ssf, nth(0, w.it, s, 2, 1 - i))
                heads = slice(LH * i, LH * (i + 1))
                pool.tensor_tensor(rnq[s][:, heads], ssq[s][:, heads], neghalf[:, heads], ALU.pow).then_inc(l_rn, 1)

            def straight(s, w, j):
                pool.wait_ge(tables_ready, w.l + 1)
                pool.wait_ge(l_kn, nth(0, w.it, s, 2, j - 2))
                pool.tensor_tensor(RA[s][:, j * 512:(j + 1) * 512].rearrange("p (h d) -> p h d", d=LD),
                                   KN[s][:, (j - 2) * 512:(j - 1) * 512].rearrange("p (h d) -> p h d", d=LD),
                                   table[w.p][:, 1, 0:1, :].to_broadcast([S, 8, LD]), ALU.mult).then_inc(l_ra, 1)

            def rotary_sum(s, w, j):
                pool.wait_ge(l_rb, nth(0, w.it, s, 4, j))
                cols = slice(j * 512, (j + 1) * 512)
                pool.tensor_tensor(QR[s][:, cols], QR[s][:, cols], RA[s][:, cols], ALU.add).then_inc(l_rot_q, 1)

            def biased(s, w):
                pool.wait_ge(lw_loaded[w.p], 144 * (w.lp + 1))
                pool.wait_ge(l_y1, nth(0, w.it, s))
                pool.tensor_tensor(yb[s], y1[s], bff2[w.p], ALU.add).then_inc(l_yb, 1)

            def inverse_std(s, w):
                pool.wait_ge(l_mv, nth(0, w.it, s))
                pool.tensor_tensor(ve[s][:, :], mv[s][:, 1:2], eps_col[:, :], ALU.add).then_inc(l_ve, 1)
                pool.wait_ge(l_ve, nth(0, w.it, s))
                pool.tensor_tensor(rs[s][:, :], ve[s][:, :], neghalf[:, 0:1], ALU.pow).then_inc(l_rs, 1)

            def halves(a, b):
                if a:
                    inverse_norms(*a, 1)
                    rotary_sum(*a, 0)
                    straight(*a, 2)
                    rotary_sum(*a, 1)
                    straight(*a, 3)
                    inverse_norms(*a, 0)
                if b:
                    inverse_std(*b)
                    biased(*b)

            def linear_attention():
                with pool.Fori(0, IT) as it:
                    for s in range(G):
                        pool.wait_ge(ln_mean, nth(LN3, it, s))
                        pool.tensor_tensor(ve[s][:, :], mv[s][:, 1:2], eps_col[:, :], ALU.add).then_inc(ln_var, 1)
                        pool.wait_ge(ln_var, nth(LN3, it, s))
                        pool.tensor_tensor(rs[s][:, :], ve[s][:, :], neghalf[:, 0:1], ALU.pow).then_inc(ln_rstd, 1)
                    for link, var, done in ((t_qlink, t_qvar, t_qrs), (t_olink, t_ovar, t_ors)):
                        for s in range(G):
                            pool.wait_ge(link, nth(0, it, s, 2, 1))
                            pool.tensor_tensor(ve[s][:, :], mv[s][:, 1:2], eps_col[:, :], ALU.add).then_inc(var, 1)
                            pool.wait_ge(var, nth(0, it, s))
                            pool.tensor_tensor(rs[s][:, :], ve[s][:, :], neghalf[:, 0:1], ALU.pow).then_inc(done, 1)

            pool.memset(eps_col[:, :], EPS).then_inc(table_link, 1)
            pool.memset(neghalf[:, :], -0.5).then_inc(table_link, 1)
            for s in range(G):
                pool.memset(XV[s], 1.0).then_inc(v_ones, 1)
            pool.wait_ge(w0_loaded, 96)
            pool.wait_ge(table_link, 2)
            attention(XA[0], 0)
            pool.wait_ge(w1_loaded, 176)
            layer_norms(LNY)
            for s in range(G):
                pool.wait_ge(x_updated, G + LNY)
                pool.memset(LV[s], 1.0).then_inc(v_ones, 1)
            local_transformer(pool, halves, rotary_factors)
            for s in range(G):
                pool.wait_ge(ffn_gated, 1)
                pool.memset(XV[s], 1.0).then_inc(v_ones, 1)
            attention(XA[1], 1)
            layer_norms(LN1F)
            for s in range(G):
                pool.wait_ge(x_updated, G + LN2)
                pool.memset(XV[s], 1.0).then_inc(v_ones, 1)
            attention(XA[2], 2)
            layer_norms(LN2F)
            linear_attention()
            layer_norms(LN3F)

        @block.vector
        def _(dve):
            V = nc.vector

            def norm_steps(base, no, it, final):
                for s in range(G):
                    dve.wait_ge(x_updated, nth(base, it, s))
                    V.tensor_scalar(xw[s][:, :], X[:, it * G + s, :], 1.0, None, ALU.mult).then_inc(xw_ready, 1)
                for s in range(G):
                    dve.wait_ge(xw_ready, nth(base, it, s))
                    V.bn_stats(st[s][:, 0:6], xw[s][:, :]).then_inc(ln_stats, 1)
                for s in range(G):
                    dve.wait_ge(x_loaded, 16)
                    dve.wait_ge(ln_stats, nth(base, it, s))
                    V.bn_aggr(mv[s][:, :], st[s][:, 0:6]).then_inc(ln_mean, 1)
                for s in range(G):
                    dve.wait_ge(ln_rstd, nth(base, it, s))
                    final(s)

            def normed(s):
                V.tensor_scalar(xn[s][:, :], xw[s][:, :], mv[s][:, 0:1], rs[s][:, 0:1], ALU.subtract, ALU.mult).then_inc(x_normed, 1)

            def attention(a, i):
                H, dv, C, HB, OB = a["H"], a["dv"], a["C"], a["HB"], a["OB"]
                no = NO[a["ln"]]
                with dve.Fori(0, IT) as it:
                    norm_steps(a["ln"], no, it, normed)
                    if i == 1:
                        for s in range(G):
                            dve.wait_ge(x_normed, nth(no, it, s))
                            V.bn_stats(st[s][:, 0:6], xn[s][:, :]).then_inc(ln2_stats, 1)
                        for s in range(G):
                            dve.compute_val(nth(0, it, s))
                            dve.wait_ge(x_loaded, 16)
                            dve.wait_ge(ln2_stats, nth(0, it, s))
                            V.bn_aggr(mv[s][:, :], st[s][:, 0:6]).then_inc(ln2_mean, 1)
                        for s in range(G):
                            dve.wait_ge(ln2_rstd, nth(0, it, s))
                            V.tensor_scalar(xn[s][:, :], xn[s][:, :], mv[s][:, 0:1], rs[s][:, 0:1],
                                            ALU.subtract, ALU.mult).then_inc(x_normed2, 1)
                    four = lambda ap: ap.rearrange("p (j h m) -> p j h m", j=4, m=M)
                    score = lambda s: ps[s][:, :, 0:HB * M].rearrange("p j (h m) -> p j h m", m=M)
                    P = lambda s: XP[s][:, 0:H * M]
                    if a["mask"] is not None:
                        for s in range(G):
                            dve.wait_ge(sc_ps, nth(16 * i, it, s))
                            mask = a["mask"][:, None, :].to_broadcast([S, HB, M])
                            for j in range(4):
                                last = V.tensor_tensor(four(P(s))[:, j, :, :], score(s)[:, j, :, :], mask, ALU.add)
                            last.then_inc(sc_masked, 1)
                    for s in range(G):
                        if a["mask"] is not None:
                            dve.wait_ge(sc_masked, nth(16 * (i // 2), it, s))
                            V.tensor_reduce(mx[s][:, 0:H], heads4(P(s)), AX.X, ALU.max).then_inc(sc_max, 1)
                        else:
                            dve.wait_ge(sc_ps, nth(16 * i, it, s))
                            V.tensor_reduce(mx[s][:, 0:H].rearrange("p (j h) -> p j h", j=4), score(s), AX.X, ALU.max).then_inc(sc_max, 1)
                    for s in range(G):
                        dve.wait_ge(sc_max, nth(16 * i, it, s))
                        if a["mask"] is not None:
                            V.tensor_tensor(heads4(P(s)), heads4(P(s)), mx[s][:, 0:H, None].to_broadcast([S, H, M]),
                                            ALU.subtract).then_inc(sc_shifted, 1)
                        else:
                            for j in range(4):
                                last = V.tensor_tensor(four(P(s))[:, j, :, :], score(s)[:, j, :, :],
                                                       mx[s][:, j * HB:(j + 1) * HB, None].to_broadcast([S, HB, M]), ALU.subtract)
                            last.then_inc(sc_shifted, 1)
                    for s in range(G):
                        dve.wait_ge(pT_ps, nth(16 * i, it, s))
                        V.tensor_copy(XPT[s][:, H * S // 2:H * S],
                                      ps[s][0:M, H // 8:H // 4, :].rearrange("p j n -> p (j n)")).then_inc(pT_dve, 1)
                    NB = H // OB
                    ov = lambda s: ps[s][:, 0:NB, 0:OB * (dv + 1)].rearrange("p j (h e) -> p j h e", e=dv + 1)
                    for s in range(G):
                        dve.wait_ge(o_ps, nth(16 * i, it, s))
                        V.reciprocal(rc[s][:, 0:H].rearrange("p (j h) -> p j h", j=NB), ov(s)[:, :, :, dv]).then_inc(o_recip, 1)
                    for s in range(G):
                        dve.wait_ge(o_recip, nth(16 * i, it, s))
                        for j in range(NB):
                            last = V.tensor_tensor(XO[s][:, j * OB * dv:(j + 1) * OB * dv].rearrange("p (h e) -> p h e", e=dv),
                                                   ov(s)[:, j, :, 0:dv],
                                                   rc[s][:, j * OB:(j + 1) * OB, None].to_broadcast([S, OB, dv]), ALU.mult)
                        last.then_inc(o_ready, 1)
                    for s in range(G):
                        dve.wait_ge(y_ps, nth(16 * i, it, s))
                        y = ps[s][:, 3, 0:D]
                        if i == 2:
                            V.tensor_tensor(xt[s], y, bo2[:, :], ALU.add).then_inc(y_biased, 1)
                            dve.wait_ge(y_biased, nth(0, it, s))
                            y = xt[s]
                        V.scalar_tensor_tensor(X[:, it * G + s, :], y, a["gate"], xw[s][:, :], ALU.mult, ALU.add).then_inc(x_updated, 1)

            def blk(ap, j):
                return ap[:, j * 512:(j + 1) * 512].rearrange("p (h d) -> p h d", d=LD)

            def tokens(s, w):
                dve.wait_ge(ffn_done, nth(0, w.it, s))
                V.tensor_scalar(xw[s][:, :], Y[:, w.pr * G + s, :], 1.0, None, ALU.mult).then_inc(l_y, 1)

            def square_sums(s, w, j):
                dve.wait_ge(l_sq, nth(0, w.it, s, 4, keys_first(j)))
                V.tensor_reduce(ssq[s][:, 8 * j:8 * j + 8], blk(SQ[s], j), AX.X, ALU.add).then_inc(l_ss, 1)

            def floors(s, w, i):
                dve.wait_ge(l_ss, nth(0, w.it, s, 4, 3 - 2 * i))
                part_ = ssq[s][:, LH * i:LH * (i + 1)]
                V.tensor_scalar(part_, part_, 1e-24, 1.0 if i else QK_SCALE ** -2, ALU.max, ALU.mult).then_inc(l_ssf, 1)

            def normalised(s, w, j):
                if j == 2:
                    dve.wait_ge(l_rn, nth(0, w.it, s, 2, 0))
                V.tensor_tensor(blk(KN[s], j - 2), ps[s][:, j, :].rearrange("p (h d) -> p h d", d=LD),
                                rnq[s][:, 8 * j:8 * j + 8, None].to_broadcast([S, 8, LD]), ALU.mult).then_inc(l_kn, 1)

            def rotated(s, w, j):
                hd = LD // 2
                factors = table[w.p][:, j // 2, :, :]
                if j == 0:
                    dve.wait_ge(tables_ready, w.l + 1)
                if j < 2:
                    dve.wait_ge(l_sq, nth(0, w.it, s, 4, keys_first(j)))
                    src = blk(ps[s][:, :, :].rearrange("p j n -> p (j n)"), j)
                    V.tensor_tensor(blk(RA[s], j), src, factors[:, 0:1, :].to_broadcast([S, 8, LD]), ALU.mult)
                else:
                    dve.wait_ge(l_kn, nth(0, w.it, s, 2, j - 2))
                    src = blk(KN[s], j - 2)
                for lo, other in ((0, hd), (hd, 0)):
                    last = V.tensor_tensor(blk(QR[s], j)[:, :, lo:lo + hd], src[:, :, other:other + hd],
                                           factors[:, 1:2, lo:lo + hd].to_broadcast([S, 8, hd]), ALU.mult)
                last.then_inc(l_rb, 1)

            def rotary_sum(s, w, j):
                dve.wait_ge(l_rb, nth(0, w.it, s, 4, j))
                dve.wait_ge(l_ra, nth(0, w.it, s, 2, j - 2))
                V.tensor_tensor(blk(QR[s], j), blk(QR[s], j), blk(RA[s], j), ALU.add).then_inc(l_rot_k, 1)

            def maxima(s, w, g):
                dve.wait_ge(l_sc_ps, nth(0, w.it, s, 4, g))
                V.tensor_reduce(mx[s][:, 4 * g:4 * g + 4], ps[s][:, g, :].rearrange("p (c n) -> p c n", n=S),
                                AX.X, ALU.max).then_inc(l_max, 1)

            def exponent_biases(s, w, g):
                if g == 0:
                    dve.wait_ge(l_rn, nth(0, w.it, s, 2, 1))
                dve.wait_ge(l_max, nth(0, w.it, s, 4, g))
                rq = rnq[s][:, 0:LH].rearrange("p (c k) -> p c k", k=2)
                V.scalar_tensor_tensor(negmx[s][:, 4 * g:4 * g + 4], mx[s][:, 4 * g:4 * g + 4], -1.0,
                                       rq[:, (g % 2) * 4:(g % 2) * 4 + 4, g // 2], ALU.mult, ALU.mult).then_inc(l_shift, 1)

            def pv(s, g):
                return ps[s][:, g, 0:4 * 65].rearrange("p (c e) -> p c e", e=65)

            def inverse_sums(s, w, g):
                dve.wait_ge(l_pv_ps, nth(0, w.it, s, 4, g))
                V.reciprocal(rc[s][:, 4 * g:4 * g + 4], pv(s, g)[:, :, LD]).then_inc(l_rc, 1)

            def outputs(s, w, g):
                dve.wait_ge(l_rc, nth(0, w.it, s, 4, g))
                o = LO[s].rearrange("p (c k e) -> p c k e", k=2, e=LD)
                V.tensor_tensor(o[:, (g % 2) * 4:(g % 2) * 4 + 4, g // 2, :], pv(s, g)[:, :, 0:LD],
                                rc[s][:, 4 * g:4 * g + 4, None].to_broadcast([S, 4, LD]), ALU.mult).then_inc(l_o, 1)

            def first_residual(s, w):
                dve.wait_ge(l_att_ps, nth(0, w.it, s))
                V.tensor_tensor(y1[s], ps[s][:, 2, 0:D], xw[s][:, :], ALU.add).then_inc(l_y1, 1)

            def token_stats(s, w):
                dve.wait_ge(l_y1, nth(0, w.it, s))
                V.bn_stats(st[s][:, 0:6], y1[s][:, 0:64])

            def shift_stats(s, w):
                dve.wait_ge(l_sh_ps, nth(0, w.it, s))
                V.bn_stats(st[s][:, 6:12], ps[s][:, 3, 0:64]).then_inc(l_st, 1)

            def statistics(s, w):
                dve.wait_ge(x_loaded, 16)
                dve.wait_ge(l_st, nth(0, w.it, s))
                V.bn_aggr(mv[s][:, :], st[s][:, 0:12]).then_inc(l_mv, 1)

            def shifted_normed(s, w):
                dve.wait_ge(l_rs, nth(0, w.it, s))
                V.tensor_scalar(xn[s][:, 0:64], y1[s][:, 0:64], mv[s][:, 0:1], rs[s][:, 0:1],
                                ALU.subtract, ALU.mult).then_inc(l_xn, 1)
                V.tensor_scalar(xn[s][:, 64:128], ps[s][:, 3, 0:64], mv[s][:, 0:1], rs[s][:, 0:1],
                                ALU.subtract, ALU.mult).then_inc(l_xn, 1)

            def hidden(s, w):
                dve.wait_ge(lw_loaded[w.p], 144 * (w.lp + 1))
                dve.wait_ge(l_gate_ps, nth(0, w.it, s, 2, 1))
                for c, (lo, hi) in enumerate(HC):
                    dve.wait_ge(l_gelu, nth(0, w.it, s, 3, c))
                    V.scalar_tensor_tensor(hidT[s][0:hi - lo, c, :], ps[s][0:hi - lo, 2, c * S:(c + 1) * S],
                                           lcol[w.p][0:hi - lo, 2 + c:3 + c], geluT[s][0:hi - lo, c, :],
                                           ALU.add, ALU.mult).then_inc(l_hid, 1)

            def second_residual(s, w):
                dve.wait_ge(l_yb, nth(0, w.it, s))
                dve.wait_ge(l_ff_ps, nth(0, w.it, s))
                V.tensor_tensor(Y[:, w.pr * G + s, :], ps[s][:, 0, 128:256], yb[s], ALU.add).then_inc(ffn_done, 1)

            def halves(a, b):
                if a: tokens(*a)
                if b:
                    maxima(*b, 2)
                    exponent_biases(*b, 2)
                    maxima(*b, 3)
                    inverse_sums(*b, 0)
                    outputs(*b, 0)
                if a: square_sums(*a, 2)
                if b: exponent_biases(*b, 3)
                if a:
                    square_sums(*a, 3)
                    floors(*a, 1)
                    rotated(*a, 0)
                    square_sums(*a, 0)
                    rotated(*a, 1)
                    normalised(*a, 2)
                if b:
                    inverse_sums(*b, 1)
                    inverse_sums(*b, 2)
                    outputs(*b, 1)
                    inverse_sums(*b, 3)
                    outputs(*b, 2)
                    outputs(*b, 3)
                if a:
                    rotated(*a, 2)
                    rotary_sum(*a, 2)
                    normalised(*a, 3)
                    square_sums(*a, 1)
                    rotated(*a, 3)
                    floors(*a, 0)
                    rotary_sum(*a, 3)
                if b:
                    first_residual(*b)
                    token_stats(*b)
                    shift_stats(*b)
                    statistics(*b)
                if a:
                    maxima(*a, 0)
                    exponent_biases(*a, 0)
                if b: shifted_normed(*b)
                if a:
                    maxima(*a, 1)
                    exponent_biases(*a, 1)
                if b:
                    hidden(*b)
                    second_residual(*b)

            def mixture(m):
                no, base, NG = NO[m["ln"]], m["base"], len(m["groups"])
                mi = 16 if base else 0
                first = 1 if base else 0
                with dve.Fori(0, IT) as it:
                    norm_steps(m["ln"], no, it, normed)

                    def linked(k, s):
                        return m["link0"] + it * (G * m["links"]) + (k - 1) * G + s + 1

                    if base:
                        k, prob = 0, pr
                        for s in range(G):
                            dve.wait_ge(m_lg_ps, nth(mi, it, s))
                            V.tensor_tensor(lg[s][:, :], ps[s][:, 1, 0:8], moe2_rb, ALU.add).then_inc(m_shift, 1)
                    else:
                        k, prob = 4, sel
                        for s in range(G):
                            dve.wait_ge(m_lg_ps, nth(mi, it, s))
                            V.tensor_reduce(col[s][:, 0:1], ps[s][:, 1, 0:8], AX.X, ALU.max).then_inc(m_link, 1)
                        for s in range(G):
                            dve.wait_ge(m_link, linked(1, s))
                            V.tensor_scalar(lg[s][:, :], ps[s][:, 1, 0:8], col[s][:, 0:1], None, ALU.subtract).then_inc(m_shift, 1)
                        for s in range(G):
                            dve.wait_ge(m_prob, nth(mi, it, s))
                            V.tensor_reduce(col[s][:, 1:2], pr[s][:, :], AX.X, ALU.add).then_inc(m_link, 1)
                        for s in range(G):
                            dve.wait_ge(m_link, linked(2, s))
                            V.reciprocal(col[s][:, 2:3], col[s][:, 1:2]).then_inc(m_link, 1)
                        for s in range(G):
                            dve.wait_ge(m_link, linked(3, s))
                            V.tensor_scalar(sel[s][:, :], pr[s][:, :], col[s][:, 2:3], None, ALU.mult).then_inc(m_link, 1)
                    for s in range(G):
                        if base:
                            dve.compute_val(nth(mi, it, s))
                            dve.wait_ge(x_loaded, 16)
                            dve.wait_ge(m_prob, nth(mi, it, s))
                        else:
                            dve.compute_val(linked(k, s))
                            dve.wait_ge(x_loaded, 16)
                            dve.wait_ge(m_link, linked(k, s))
                        V.max(top8[s][:, :], prob[s][:, :]).then_inc(m_link, 1)
                    for s in range(G):
                        dve.compute_val(linked(k + 1, s))
                        dve.wait_ge(x_loaded, 16)
                        dve.wait_ge(m_link, linked(k + 1, s))
                        V.max_index(idx[s][:, :], top8[s][:, :], prob[s][:, :]).then_inc(m_link, 1)
                    for s in range(G):
                        dve.wait_ge(m_link, linked(k + 2, s))
                        V.tensor_copy(idxf[s][:, :], idx[s][:, :]).then_inc(m_link, 1)
                    for n, to in enumerate((rw, lg)):
                        for s in range(G):
                            dve.wait_ge(m_link, linked(k + 3, s))
                            V.scalar_tensor_tensor(to[s][:, :], iota[:, :], idxf[s][:, n:n + 1], prob[s][:, :],
                                                   ALU.is_equal, ALU.mult).then_inc(m_link, 1)
                    for s in range(G):
                        dve.wait_ge(m_link, linked(k + 5, s))
                        V.tensor_tensor(rw[s][:, :], rw[s][:, :], lg[s][:, :], ALU.add).then_inc(m_route if base else m_link, 1)
                    if not base:
                        for k, done_ in ((10, m_link), (14, m_route)):
                            r = 0 if k == 10 else 1
                            for s in range(G):
                                dve.wait_ge(m_link, linked(k, s))
                                V.tensor_reduce(col[s][:, r:r + 1], rw[s][:, :], AX.X, ALU.add).then_inc(m_link, 1)
                            for s in range(G):
                                dve.wait_ge(m_link, linked(k + 1, s))
                                V.tensor_scalar(col[s][:, r:r + 1], col[s][:, r:r + 1], 1e-9, None, ALU.add).then_inc(m_link, 1)
                            for s in range(G):
                                dve.wait_ge(m_link, linked(k + 2, s))
                                V.reciprocal(col[s][:, 2 + r:3 + r], col[s][:, r:r + 1]).then_inc(m_link, 1)
                            for s in range(G):
                                dve.wait_ge(m_link, linked(k + 3, s))
                                V.tensor_scalar(rw[s][:, :], rw[s][:, :], col[s][:, 2 + r:3 + r], None, ALU.mult).then_inc(done_, 1)
                    done = 0
                    for g, experts in enumerate(m["groups"]):
                        n = 512 if not base else 256 * len(experts)
                        for s in range(G):
                            dve.wait_ge(m_silu, nth_group(base, it, s, NG, g))
                            V.tensor_tensor(AT[s][:, 0:n], SG[s][:, 0:n], ps[s][:, 3, 0:n], ALU.mult).then_inc(m_act, 1)
                        for s in range(G):
                            if g == 0:
                                dve.wait_ge(m_route, nth(mi, it, s))
                        for k, e in enumerate(experts):
                            for s in range(G):
                                y = ps[s][:, g % 2, k * D:(k + 1) * D]
                                w = 1.0 if e < first else rw[s][:, e - first:e - first + 1]
                                sync = m_acc if k == len(experts) - 1 else m_part
                                if k == 0:
                                    dve.wait_ge(m_dn_ps, nth_group(base, it, s, NG, g))
                                if e == 0:
                                    op = V.tensor_scalar(acc[s], y, w, None, ALU.mult)
                                else:
                                    if k == 0:
                                        dve.wait_ge(m_acc, nth_group(base, it, s, NG, g - 1))
                                    else:
                                        dve.wait_ge(m_part, m["part0"] + it * (G * m["parts"]) + done + s + 1 - G)
                                    op = V.scalar_tensor_tensor(acc[s], y, w, acc[s], ALU.mult, ALU.add)
                                op.then_inc(sync, 1)
                            if k < len(experts) - 1:
                                done += G
                    for s in range(G):
                        dve.wait_ge(m_acc, nth_group(base, it, s, NG, NG - 1))
                        V.scalar_tensor_tensor(X[:, it * G + s, :], acc[s], m["gate"], xw[s][:, :], ALU.mult, ALU.add).then_inc(x_updated, 1)

            def linear_attention():
                with dve.Fori(0, IT) as it:
                    norm_steps(LN3, NO[LN3], it, normed)
                    for s in range(G):
                        dve.wait_ge(t_k, 2 + 2 * it + s + 1)
                        V.tensor_reduce(col[s][:, :], K3[s], AX.X, ALU.max).then_inc(t_klink, 1)
                    for s in range(G):
                        dve.wait_ge(t_klink, nth(0, it, s, 1))
                        V.tensor_tensor(K3E[s], K3[s], col[s][:, :, None].to_broadcast([128, 4, KEYS3]), ALU.subtract).then_inc(t_kshift, 1)
                    for s in range(G):
                        dve.wait_ge(q_ps, nth(48, it, s))
                        V.bn_stats(st[s][:, 0:6], ps[s][:, 1, :]).then_inc(t_qlink, 1)
                        dve.compute_val(nth(0, it, s, 2, 0))
                        dve.wait_ge(x_loaded, 16)
                        dve.wait_ge(t_qlink, nth(0, it, s, 2, 0))
                        V.bn_aggr(mv[s][:, :], st[s][:, 0:6]).then_inc(t_qlink, 1)
                    for s in range(G):
                        dve.wait_ge(t_kexp, nth(0, it, s))
                        V.tensor_reduce(rc[s][:, 0:4], K3E[s], AX.X, ALU.add).then_inc(o_recip, 1)
                    for s in range(G):
                        dve.wait_ge(o_recip, 48 + 4 * it + s + 1)
                        V.reciprocal(rc[s][:, 4:8], rc[s][:, 0:4]).then_inc(o_recip, 1)
                    for s in range(G):
                        dve.wait_ge(t_qrs, nth(0, it, s))
                        V.tensor_scalar(Q3[s], ps[s][:, 1, :], mv[s][:, 0:1], rs[s][:, 0:1], ALU.subtract, ALU.mult).then_inc(t_qg, 1)
                    for s in range(G):
                        dve.wait_ge(t_qg, it * 8 + s + 1)
                        V.tensor_tensor(Q3[s], Q3[s], qg, ALU.mult).then_inc(t_qg, 1)
                    for s in range(G):
                        dve.wait_ge(t_qg, it * 8 + 2 + s + 1)
                        V.tensor_tensor(Q3[s], Q3[s], qb, ALU.add).then_inc(t_qg, 1)
                    q8 = lambda s: Q3[s].rearrange("p (h d) -> p h d", d=D3)
                    for s in range(G):
                        dve.wait_ge(t_qg, it * 8 + 4 + s + 1)
                        V.tensor_reduce(mx[s][:, 0:8], q8(s), AX.X, ALU.max).then_inc(t_qg, 1)
                    for s in range(G):
                        dve.wait_ge(t_qg, it * 8 + 6 + s + 1)
                        V.tensor_tensor(q8(s), q8(s), mx[s][:, 0:8, None].to_broadcast([S, 8, D3]), ALU.subtract).then_inc(t_qshift, 1)
                    for s in range(G):
                        dve.wait_ge(o_recip, 48 + 4 * it + 2 + s + 1)
                        dve.wait_ge(t_c_ps, nth(0, it, s))
                        for c in range(4):
                            last = V.scalar_tensor_tensor(C3[s][:, c, :], ps[s][:, 3, c * 128:(c + 1) * 128], rc[s][:, 4 + c:5 + c],
                                                          blockpair[:, :], ALU.mult, ALU.mult)
                        last.then_inc(t_c, 1)
                    for s in range(G):
                        dve.wait_ge(t_qexp, nth(0, it, s))
                        V.tensor_reduce(mx[s][:, 0:8], q8(s), AX.X, ALU.add).then_inc(sc_max, 1)
                    for s in range(G):
                        dve.wait_ge(sc_max, 48 + 4 * it + s + 1)
                        V.reciprocal(mx[s][:, 8:16], mx[s][:, 0:8]).then_inc(sc_max, 1)
                    for s in range(G):
                        dve.wait_ge(sc_max, 48 + 4 * it + 2 + s + 1)
                        V.tensor_scalar(mx[s][:, 0:8], mx[s][:, 8:16], 8.0, None, ALU.mult).then_inc(sc_masked, 1)
                    for s in range(G):
                        dve.wait_ge(sc_masked, nth(32, it, s))
                        dve.wait_ge(t_o_ps, nth(0, it, s))
                        V.tensor_tensor(O3[s].rearrange("p (h e) -> p h e", e=D3), ps[s][:, 1, :].rearrange("p (h e) -> p h e", e=D3),
                                        mx[s][:, 0:8, None].to_broadcast([S, 8, D3]), ALU.mult).then_inc(o_ready, 1)
                    for s in range(G):
                        dve.wait_ge(o_ready, nth(48, it, s))
                        V.bn_stats(st[s][:, 0:6], O3[s]).then_inc(t_olink, 1)
                        dve.compute_val(nth(0, it, s, 2, 0))
                        dve.wait_ge(x_loaded, 16)
                        dve.wait_ge(t_olink, nth(0, it, s, 2, 0))
                        V.bn_aggr(mv[s][:, :], st[s][:, 0:6]).then_inc(t_olink, 1)
                    for s in range(G):
                        dve.wait_ge(t_ors, nth(0, it, s))
                        V.tensor_scalar(O3[s], O3[s], mv[s][:, 0:1], rs[s][:, 0:1], ALU.subtract, ALU.mult).then_inc(t_o, 1)
                    for s in range(G):
                        dve.wait_ge(t_y_ps, nth(0, it, s))
                        V.scalar_tensor_tensor(X[:, it * G + s, :], ps[s][:, 3, 0:D], gates[:, 0, 3:4], xw[s][:, :], ALU.mult, ALU.add).then_inc(x_updated, 1)

            def chosen_expert():
                with dve.Fori(0, IT) as it:
                    norm_steps(LN3F, NO[LN3F], it, normed)
                    for s in range(G):
                        dve.wait_ge(m_lg_ps, nth(32, it, s))
                        V.tensor_tensor(lg[s][0:1, :], ps[s][0:1, 1, 0:8], moe3_rb[0:1, :], ALU.add).then_inc(m_shift, 1)
                    for s in range(G):
                        dve.wait_ge(x_loaded, 16)
                        dve.wait_ge(m_shift, nth(32, it, s))
                        V.max(top8[s][0:1, :], lg[s][0:1, :]).then_inc(m_prob, 1)
                    for s in range(G):
                        dve.wait_ge(x_loaded, 16)
                        dve.wait_ge(m_prob, nth(32 + 0, it, s))
                        V.max_index(idx[s][0:1, :], top8[s][0:1, :], lg[s][0:1, :]).then_inc(m_route, 1)
                    for s in range(G):
                        dve.wait_ge(m_dn_ps, nth(16 * 7, it, s))
                        V.tensor_tensor(acc[s], ps[s][:, 3, 0:D], FB2[s], ALU.add).then_inc(m_acc, 1)
                    for s in range(G):
                        dve.wait_ge(m_acc, nth(16 * 7, it, s))
                        V.scalar_tensor_tensor(X[:, it * G + s, :], acc[s], gates[:, 1, 3:4], xw[s][:, :], ALU.mult, ALU.add).then_inc(x_updated, 1)

            V.memset(seed[:, :], 0.0).then_inc(x_updated, G)
            dve.wait_ge(x_updated, G)
            V.memset(seed[:, :], 0.0).then_inc(ffn_done, G)
            dve.wait_ge(x_loaded, 16)
            dve.wait_ge(w0_loaded, 96)
            dve.wait_ge(gates_ready, 1)
            attention(XA[0], 0)
            dve.wait_ge(w1_loaded, 176)
            V.tensor_copy(ident_b[:, :], ident[:, :]).then_inc(consts_cast, 1)
            V.tensor_copy(band_b[:, :], band_f[:, :]).then_inc(consts_cast, 1)
            with dve.Fori(0, IT) as it:
                def start(s):
                    V.tensor_scalar(Y[:, it * G + s, :], xw[s][:, :], mv[s][:, 0:1], rs[s][:, 0:1],
                                    ALU.subtract, ALU.mult).then_inc(x_updated, 1)
                norm_steps(LNY, None, it, start)
            dve.wait_ge(x_updated, G + LN1)
            local_transformer(dve, halves)
            dve.wait_ge(ffn_done, G + DEPTH * B)
            allx = lambda t: t[:, :, :].rearrange("p b d -> p (b d)")
            V.scalar_tensor_tensor(allx(X), allx(Y), gates[:, 1, 0:1], allx(X), ALU.mult, ALU.add).then_inc(ffn_gated, 1)
            dve.wait_ge(ffn_gated, 1)
            attention(XA[1], 1)
            mixture(MOE[0])
            dve.wait_ge(late_loaded, 288)
            V.tensor_tensor(side[:, :], side[:, :], side[:, :], ALU.add).then_inc(late_prep, 1)
            V.tensor_scalar(bq_s, bqkv[:, 0:1], 8 ** -0.5, None, ALU.mult).then_inc(late_prep, 1)
            dve.wait_ge(late_prep, 2)
            attention(XA[2], 2)
            mixture(MOE[1])
            linear_attention()
            chosen_expert()


def inputs_of(a):
    c = np.ascontiguousarray
    f = {k: np.asarray(v) for k, v in a.items()}
    col = lambda v: v.reshape(-1, 1)
    row = lambda v: v.reshape(1, -1)
    d = dict(constants())
    d["x"] = c(f["x"].transpose(1, 0, 2))
    d["ctxT"] = c(f["ctx_1024"].transpose(2, 0, 1))
    d["g_xattn"], d["g_ffn"] = row(f["g_xattn"]), row(f["g_ffn"])
    d["side"] = f["fside_SxS2_0"]
    w0 = np.zeros((D, 2, D), np.float32)
    for h in range(16):
        w0[h * 8:h * 8 + 8, 0, h * 8:h * 8 + 8] = f["L0_xattn_W1"].T
    w0[:, 1, :] = f["L0_xattn_W2"].T
    d["w0"] = w0
    d["q_scale"], d["k_scale"] = f["L0_ffn_q_scale"], f["L0_ffn_k_scale"]
    d["wqkv"] = f["L0_ffn_Wqkv"]
    d["wout"] = c(f["L0_ffn_Wo"].reshape(DEPTH, 8, 128, D).transpose(0, 2, 1, 3))
    d["wff1"], d["wff2"], d["bff2"] = f["L0_ffn_W1"], f["L0_ffn_W2"], f["L0_ffn_b2"]
    lcol = np.zeros((DEPTH, D, 8), np.float32)
    lcol[:, :, 0], lcol[:, :, 1] = f["L0_ffn_ln_g"], f["L0_ffn_ln_b"]
    for i, (lo, hi) in enumerate(HC):
        lcol[:, 0:hi - lo, 2 + i] = f["L0_ffn_b1"][:, lo:hi]
        lcol[:, 0:hi - lo, 5 + i] = f["L0_ffn_b1"][:, HID + lo:HID + hi]
    d["lcol"] = lcol
    chunks = lambda w: w.reshape(4, 128, D).transpose(1, 0, 2)
    d["w1"] = c(np.stack([f["L1_xattn_Wq"], f["L1_xattn_Wkv"][:, :512], f["L1_xattn_Wkv"][:, 512:],
                          chunks(f["L1_xattn_Wo"]).reshape(128, 512)], 1))
    d["aff1"] = c(np.stack([f["L1_xattn_ln_scale"], f["L1_xattn_ln_bias"]], 1))
    d["moe1_r"] = c(f["L1_ffn_gate_w"].T)
    d["moe1_gu"] = c(f["L1_ffn_gate_up_proj"].transpose(1, 0, 2))
    d["moe1_d"] = c(f["L1_ffn_down_proj"].transpose(1, 0, 2))
    wqkv = f["L2_xattn_Wqkv"]
    d["w2"] = c(np.stack([wqkv[:D].T, wqkv[D:2 * D].T, wqkv[2 * D:].T, f["L2_xattn_Wo"].T], 1))
    d["bqkv"] = c(f["L2_xattn_bqkv"].reshape(3, D).T)
    d["bo2"] = row(f["L2_xattn_bo"])
    both = lambda s, e: np.concatenate([f[s][None], f[e]], 0)
    d["moe2_g"] = c(both("L2_ffn_Wg_s", "L2_ffn_Wg").transpose(2, 0, 1))
    d["moe2_u"] = c(both("L2_ffn_Wu_s", "L2_ffn_Wu").transpose(2, 0, 1))
    d["moe2_d"] = c(both("L2_ffn_Wd_s", "L2_ffn_Wd").transpose(2, 0, 1).reshape(2, 128, E2, D).transpose(1, 2, 0, 3))
    d["moe2_r"], d["moe2_rb"] = c(f["L2_ffn_Wr"].T), row(f["L2_ffn_rb"])
    d["w3"] = c(np.stack([f["L3_xattn_Wq"], f["L3_xattn_Wkv"][:, :512], f["L3_xattn_Wkv"][:, 512:]], 1))
    d["w3o"] = c(chunks(f["L3_xattn_Wout"]))
    d["nullk"] = c(col(np.tile(f["L3_xattn_null_kv"][0], 2)))
    d["nullv"] = row(np.tile(f["L3_xattn_null_kv"][1], 8))
    d["qg"], d["qb"] = row(f["L3_xattn_ln_q_g"]), row(f["L3_xattn_ln_q_b"])
    d["og"], d["ob"] = c(f["L3_xattn_ln_out_g"].reshape(4, 128).T), c(f["L3_xattn_ln_out_b"].reshape(4, 128).T)
    d["moe3_r"], d["moe3_rb"] = f["L3_ffn_Wr"], row(f["L3_ffn_br"])
    d["moe3_w1"] = f["L3_ffn_W1"]
    d["moe3_w2"] = c(f["L3_ffn_W2"].reshape(8, 4, 128, D).transpose(0, 2, 1, 3))
    d["moe3_b1"] = c(f["L3_ffn_b1"].reshape(8, 4, 128).transpose(0, 2, 1))
    d["moe3_b2"] = f["L3_ffn_b2"]
    return {k: c(v) for k, v in d.items()}


def kernel(**inputs):
    import concourse.bacc as bacc
    from concourse.bass_utils import run_bass_kernel_spmd

    arrays = inputs_of(inputs)
    nc = bacc.Bacc("TRN2", target_bir_lowering=False, num_devices=1)
    dram = {k: nc.dram_tensor(f"in_{k}", v.shape, mybir.dt.from_np(v.dtype), kind="ExternalInput").ap() for k, v in arrays.items()}
    out = nc.dram_tensor("out_x", (S, B, D), F32, kind="ExternalOutput").ap()
    program(nc, dram, out)
    r = run_bass_kernel_spmd(nc, [{f"in_{k}": v for k, v in arrays.items()}], core_ids=[0])
    return np.ascontiguousarray(r.results[0]["out_x"].transpose(1, 0, 2))
```

```python
from contextlib import ExitStack

import numpy as np

import concourse.bass as bass
from concourse import mybir

F32 = mybir.dt.float32
BF16 = mybir.dt.bfloat16
U32 = mybir.dt.uint32
ALU = mybir.AluOpType
ACT = mybir.ActivationFunctionType
AX = mybir.AxisListType

B, S, D, M = 16, 128, 128, 77
G = 2
IT = B // G
DEPTH, LH, LD = 6, 16, 64
QK_SCALE = 8.0
INNER = LH * LD
HID = int(D * 4 * 2 / 3)
HC = [(0, 128), (128, 256), (256, HID)]
WINDOW = 32
EPS = 1e-5
NEG = -1e25
E1, E2, E3 = 8, 9, 8
EH2 = 256
FF3 = 512
H3, D3 = 8, 64
ND = D // 128 * 4
KEYS3 = M + 1


def constants():
    t = np.arange(S)
    shift = np.zeros((S, S), np.float32)
    shift[t[:-1], t[1:]] = 1
    i, j = t[:, None], t[None, :]
    first = (i // WINDOW - 1) * WINDOW
    seen = (j <= i) & (j + WINDOW >= i) & (j >= first)
    half = np.arange(0, LD, 2, dtype=np.float32)
    inv = (np.float32(1) / np.float32(10000) ** (half / np.float32(LD))).astype(np.float32)
    f = t[:, None].astype(np.float32) * inv[None]
    base = ((half + np.float32(0.4 * LD)) / np.float32(1.4 * LD)).astype(np.float32)
    power = ((t.astype(np.float32) - S // 2) / np.float32(WINDOW // 2)).astype(np.float32)
    scale = (base[None] ** power[:, None]).astype(np.float32)
    two = lambda a: np.concatenate([a, a], 1)
    cos, sin, scale = two(np.cos(f)), two(np.sin(f)), two(scale)
    sin[:, :LD // 2] *= -1
    rot = np.stack([cos * scale, sin * scale, cos / scale, sin / scale], 1)
    d = np.arange(D)
    return {
        "ident": np.eye(S, dtype=np.float32),
        "shift": shift,
        "band": np.where(seen, 0, NEG).astype(np.float32),
        "causal": np.where(np.arange(M)[None] > t[:, None], NEG, 0).astype(np.float32),
        "heads16": (d[:, None] // 8 == np.arange(16)[None]).astype(np.float32),
        "heads2": (d[:, None] // 64 == np.arange(2)[None]).astype(np.float32),
        "pair": (d[:, None] // 64 == d[None] // 64).astype(np.float32),
        "rot": np.ascontiguousarray(rot, np.float32),
        "rank": np.tile(8 - np.arange(8, dtype=np.float32)[None], (S, 1)),
    }


def program(nc, dram, out):
    ctx = ExitStack()
    with ctx:
        def sb(name, shape, dt=F32):
            return ctx.enter_context(nc.sbuf_tensor(name, list(shape), dt))

        def sem(name):
            return ctx.enter_context(nc.semaphore(name))

        def pair(name, shape, dt=F32):
            return [sb(f"{name}{s}", shape, dt) for s in range(G)]

        X = sb("X", [S, B, D])
        Y = sb("Y", [S, B, D])
        ident, shift = sb("ident", [S, S]), sb("shift", [S, S])
        band_f = sb("band_f", [S, S])
        ident_b, band_b = sb("ident_b", [S, S], BF16), sb("band_b", [S, S], BF16)
        causal, causal_b = sb("causal", [S, M]), sb("causal_b", [S, M], BF16)
        heads16, heads2 = sb("heads16", [D, 16]), sb("heads2", [D, 2])
        blockpair = sb("blockpair", [D, D])
        rank = sb("rank", [S, 8])
        rot = sb("rot", [S, 4, LD])
        qk_scale = pair("qk_scale", [S, 2, LD])
        table = pair("table", [S, 2, 2, LD])
        gates = sb("gates", [S, 2, 4])
        eps_col, neghalf = sb("eps_col", [S, 1]), sb("neghalf", [S, 2 * LH])
        seed = sb("seed", [S, 1])
        w0 = sb("w0", [D, 2, D])
        w1 = sb("w1", [D, 4, 4 * D])
        aff1 = sb("aff1", [D, 2])
        moe1_r = sb("moe1_r", [D, E1])
        moe1_gu = sb("moe1_gu", [D, E1, 2 * D])
        moe1_d = sb("moe1_d", [D, E1, D])
        LW = 3 * INNER + INNER + 2 * HID + 3 * D + D
        lw = [sb(f"lw{p}", [D, LW]) for p in range(2)]
        lcol = [sb(f"lcol{p}", [D, 8]) for p in range(2)]
        wqkv = [t[:, 0:3 * INNER] for t in lw]
        o_ = 3 * INNER
        wout = [t[:, o_:o_ + INNER].rearrange("p (c n) -> p c n", n=D) for t in lw]
        o_ += INNER
        wff1 = [t[:, o_:o_ + 2 * HID] for t in lw]
        o_ += 2 * HID
        wff2 = [t[:, o_:o_ + 3 * D].rearrange("p (c n) -> p c n", n=D) for t in lw]
        o_ += 3 * D
        bff2 = [t[:, o_:o_ + D] for t in lw]
        moe2_g = lw[0][:, 0:E2 * EH2].rearrange("p (e n) -> p e n", n=EH2)
        moe2_u = lw[0][:, E2 * EH2:2 * E2 * EH2].rearrange("p (e n) -> p e n", n=EH2)
        o_ = 2 * E2 * EH2
        w2 = lw[0][:, o_:o_ + 4 * D].rearrange("p (k n) -> p k n", n=D)
        moe2_d = lw[1][:, 0:E2 * EH2].rearrange("p (e c n) -> p e c n", e=E2, n=D)
        o_ = E2 * EH2
        w3 = lw[1][:, o_:o_ + 3 * 512].rearrange("p (k n) -> p k n", n=512)
        o_ += 3 * 512
        w3o = lw[1][:, o_:o_ + 512].rearrange("p (c n) -> p c n", n=D)
        o_ += 512
        small = sb("small", [D, 1100])
        qg, qb = small[:, 0:512], small[:, 512:1024]
        og, ob = small[:, 1024:1028], small[:, 1028:1032]
        bqkv, bq_s = small[:, 1032:1035], small[:, 1035:1036]
        nullk = small[:, 1036:1037]
        moe2_r, moe2_rb = small[:, 1040:1048], small[:, 1048:1056]
        moe3_r, moe3_rb = small[:, 1056:1064], small[:, 1064:1072]
        bo2 = sb("bo2", [S, D])
        xw = pair("xw", [S, D])
        xn = pair("xn", [S, D])
        xnT = pair("xnT", [D, S])
        st, mv, ve, rs = (pair(n, [S, k]) for n, k in (("st", 12), ("mv", 2), ("ve", 1), ("rs", 1)))
        ctxT = pair("ctxT", [D, M])
        area = pair("area", [128, 5 * 2 * INNER + LH * (LD + 1) + 12 * 128])
        K2 = 2 * INNER

        def part(s, at, n, p=128):
            return area[s][0:p, at:at + n]

        bufs = range(G)
        SQ = [part(s, K2, K2) for s in bufs]
        QR = [part(s, 2 * K2, K2) for s in bufs]
        RA = [part(s, 3 * K2, K2) for s in bufs]
        QKT = [part(s, 4 * K2, K2) for s in bufs]
        LV = [part(s, 5 * K2, LH * (LD + 1)).rearrange("p (h e) -> p h e", e=LD + 1) for s in bufs]
        at_ = 5 * K2 + LH * (LD + 1)
        hidT = [part(s, at_, 384).rearrange("p (c n) -> p c n", n=S) for s in bufs]
        geluT = [part(s, at_ + 384, 384).rearrange("p (c n) -> p c n", n=S) for s in bufs]
        xsT = [part(s, at_ + 768, S) for s in bufs]
        y1 = [part(s, at_ + 896, D) for s in bufs]
        yb = [part(s, at_ + 1024, D) for s in bufs]
        LP, LPT = SQ, RA
        LO = [part(s, 0, INNER) for s in bufs]
        LOT = [part(s, INNER, INNER).rearrange("p (c n) -> p c n", n=S) for s in bufs]
        XQT = [part(s, 0, 512) for s in bufs]
        XKT = [part(s, 512, 4 * M) for s in bufs]
        XKX = [part(s, 1024, 16 * M) for s in bufs]
        XP = [part(s, K2 + 512, 16 * M) for s in bufs]
        XPT = [part(s, 2 * K2, K2, M) for s in bufs]
        XV = [part(s, 3 * K2, 8 * 65, M) for s in bufs]
        XO = [part(s, 3 * K2 + 1024, 512) for s in bufs]
        XOT = [part(s, 4 * K2, 512) for s in bufs]
        xt = [part(s, 4 * K2 + 512, D) for s in bufs]
        SG = [[part(s, 256 * k, 256) for k in range(2)] for s in bufs]
        AT = [[part(s, 512 + 256 * k, 256) for k in range(2)] for s in bufs]
        acc = [part(s, 1024, D) for s in bufs]
        quad_at = [(q % G, 4096 + 2048 * (q // G)) for q in range(B // 4)]
        XQ, XNQ, XNTQ = ([part(s, at + 512 * k, 512) for s, at in quad_at] for k in range(3))
        STQ = [part(s, at + 1536, 24) for s, at in quad_at]
        MVQ = [part(s, at + 1568, 8).rearrange("p (c k) -> p c k", k=2) for s, at in quad_at]
        VEQ, RSQ = ([part(s, at + 1584 + 8 * k, 4) for s, at in quad_at] for k in range(2))
        XNT = part(0, 2048, B * D).rearrange("p (b d) -> p b d", d=D)
        LG, PR, LEFT, RW = (part(1, 2048 + 128 * k, B * 8).rearrange("p (b e) -> p b e", e=8) for k in range(4))
        BEST, PLACE = (part(1, 2560 + 16 * k, B) for k in range(2))
        Q3 = [part(s, 0, 512) for s in bufs]
        Q3T = [part(s, 512, 512).rearrange("p (c n) -> p c n", n=S) for s in bufs]
        K3 = [part(s, 1024, 4 * KEYS3).rearrange("p (c n) -> p c n", n=KEYS3) for s in bufs]
        K3T = [part(s, 1536, 512, KEYS3) for s in bufs]
        V3 = [part(s, 2048, 512, KEYS3) for s in bufs]
        C3 = [part(s, 2560, 512).rearrange("p (c n) -> p c n", n=D) for s in bufs]
        O3 = [part(s, 3072, 512) for s in bufs]
        O3T = [part(s, 3584, 512).rearrange("p (c n) -> p c n", n=S) for s in bufs]
        K3E = [part(s, 4096, 4 * KEYS3).rearrange("p (c n) -> p c n", n=KEYS3) for s in bufs]
        EW = 2 * FF3 + 4 + D
        place = [(j % G, 3 * K2 + (j // G) * EW) for j in range(4)]
        F1 = [part(s, at, FF3) for s, at in place]
        F2 = [part(s, at + FF3, FF3).rearrange("p (c n) -> p c n", n=D) for s, at in place]
        FB1 = [part(s, at + 2 * FF3, 4) for s, at in place]
        FB2 = [part(s, at + 2 * FF3 + 4, D) for s, at in place]
        F1T = [part(s, 3 * K2 + 2 * EW, FF3).rearrange("p (c n) -> p c n", n=S) for s in bufs]
        ssq, rnq = pair("ssq", [S, 2 * LH]), pair("rnq", [S, 2 * LH])
        mx, negmx = pair("mx", [S, 16]), pair("negmx", [S, 16])
        rc = pair("rc", [S, 16])
        rw, col = pair("rw", [S, 8]), pair("col", [S, 4])
        toksum, tokmean = (sb(n, [D, B]) for n in ("toksum", "tokmean"))
        best8, chosen = sb("best8", [1, B, 8]), sb("chosen", [1, B, 8], U32)

        ps = [ctx.enter_context(nc.psum_tensor(f"ps{s}", [128, 4, 512], F32)) for s in range(G)]

        x_loaded, w0_loaded, w1_loaded = sem("x_loaded"), sem("w0_loaded"), sem("w1_loaded")
        lw_loaded = [sem("lw_loaded0"), sem("lw_loaded1")]
        late_loaded = sem("late_loaded")
        ctx_loaded = [sem("ctx_loaded0"), sem("ctx_loaded1")]
        expert_loaded = [sem(f"expert_loaded{j}") for j in range(4)]
        stored = sem("stored")
        consts_cast, tables_ready, gates_ready = sem("consts_cast"), sem("tables_ready"), sem("gates_ready")
        table_link, late_prep = sem("table_link"), sem("late_prep")
        v_ones = sem("v_ones")
        x_updated, ffn_done, ffn_gated = sem("x_updated"), sem("ffn_done"), sem("ffn_gated")
        xw_ready, ln_stats, ln_mean, ln_var, ln_rstd = (sem(n) for n in ("xw_ready", "ln_stats", "ln_mean", "ln_var", "ln_rstd"))
        x_normed, xnT_ps, xnT_ready = sem("x_normed"), sem("xnT_ps"), sem("xnT_ready")
        ln2_stats, ln2_mean, ln2_var, ln2_rstd, x_normed2 = (sem(n) for n in ("ln2_stats", "ln2_mean", "ln2_var", "ln2_rstd", "x_normed2"))
        k_ps, v_ps, q_ps, kT_ready, v_ready, kx_ready, qT_ready = (sem(n) for n in ("k_ps", "v_ps", "q_ps", "kT_ready", "v_ready", "kx_ready", "qT_ready"))
        sc_ps, sc_masked, sc_max, sc_shifted, sc_exp = (sem(n) for n in ("sc_ps", "sc_masked", "sc_max", "sc_shifted", "sc_exp"))
        pT_ps, pT_act, pT_dve, o_ps, o_recip, o_ready, oT_ps, oT_ready, y_ps, y_biased = (
            sem(n) for n in ("pT_ps", "pT_act", "pT_dve", "o_ps", "o_recip", "o_ready", "oT_ps", "oT_ready", "y_ps", "y_biased"))
        l_y, l_xsT_ps, l_xsT, l_qk_ps, l_sq, l_ss, l_ssf, l_rn, l_kn, l_rb, l_rsum = (
            sem("l_" + n) for n in ("y", "xsT_ps", "xsT", "qk_ps", "sq", "ss", "ssf", "rn", "kn", "rb", "rsum"))
        l_qkT_ps, l_qkT, l_v_ps, l_v, l_sc_ps, l_max, l_shift, l_exp, l_pT_ps, l_pT, l_pv_ps, l_rc, l_o = (
            sem("l_" + n) for n in ("qkT_ps", "qkT", "v_ps", "v", "sc_ps", "max", "shift", "exp", "pT_ps", "pT", "pv_ps", "rc", "o"))
        l_oT_ps, l_oT, l_att_ps, l_y1, l_yb, l_sh_ps, l_st, l_mv, l_ve, l_rs, l_xn, l_xnT_ps, l_xnT = (
            sem("l_" + n) for n in ("oT_ps", "oT", "att_ps", "y1", "yb", "sh_ps", "st", "mv", "ve", "rs", "xn", "xnT_ps", "xnT"))
        l_gate_ps, l_gelu, l_hid, l_ff_ps = (sem("l_" + n) for n in ("gate_ps", "gelu", "hid", "ff_ps"))
        m_link, m_gu_ps, m_silu, m_act, m_dn_ps, m_acc = (
            sem("m_" + n) for n in ("link", "gu_ps", "silu", "act", "dn_ps", "acc"))
        m_rw = sem("m_rw")
        r_x, r_stats, r_mean, r_var, r_rstd, r_norm, r_T_ps, r_T, r_lg_ps, r_kept = (
            sem("r_" + n) for n in ("x", "stats", "mean", "var", "rstd", "norm", "T_ps", "T", "lg_ps", "kept"))
        e_sum, e_mean, e_best, e_chosen = (sem("e_" + n) for n in ("sum", "mean", "best", "chosen"))
        t_v, t_k, t_klink, t_kshift, t_kexp, t_knormed, t_kT_ps, t_kT, t_c_ps, t_c = (
            sem("t_" + n) for n in ("v", "k", "klink", "kshift", "kexp", "knormed", "kT_ps", "kT", "c_ps", "c"))
        t_qlink, t_qvar, t_qrs, t_qg, t_qshift, t_qexp, t_qT_ps, t_qT, t_o_ps, t_olink, t_ovar, t_ors, t_o, t_oT_ps, t_oT, t_y_ps = (
            sem("t_" + n) for n in ("qlink", "qvar", "qrs", "qg", "qshift", "qexp", "qT_ps", "qT", "o_ps", "olink", "ovar", "ors", "o", "oT_ps", "oT", "y_ps"))

        LN0, LNY, LN1, LN1F, LN2, LN2F, LN3, LN3F = (16 * i for i in range(8))
        NB = {LN0: 0, LN1: 16, LN2: 32, LN3: 48}

        def nth(base, it, s, per=1, k=0):
            return base * per + (it * G + s) * per + k + 1

        def heads4(ap, m=M):
            return ap.rearrange("p (h m) -> p h m", m=m)

        XA = [
            dict(ln=LN0, H=16, dv=8, C=1, scale=8 ** -0.5, hm=heads16, wq=w0[:, 0, :], wk=w0[:, 0, :],
                 wv=w0[:, 0, :], wo=w0[:, 1:2, :], gate=gates[:, 0, 0:1]),
            dict(ln=LN1, H=8, dv=64, C=4, scale=64 ** -0.5, hm=heads2, wq=w1[:, 0, :], wk=w1[:, 1, :],
                 wv=w1[:, 2, :], wo=w1[:, 3, :].rearrange("p (c n) -> p c n", n=D), gate=gates[:, 0, 1:2]),
            dict(ln=LN2, H=16, dv=8, C=1, scale=1.0, hm=heads16, wq=w2[:, 0, :], wk=w2[:, 1, :],
                 wv=w2[:, 2, :], wo=w2[:, 3:4, :], gate=gates[:, 0, 2:3]),
        ]
        side = sb("side", [S, M])
        for a in XA:
            a["HB"] = a["H"] // 4
            a["OB"] = 4 if a["dv"] == 64 else 16

        QUADS = B // 4

        def gu1(e):
            return [(moe1_gu[:, e, 0:D], moe1_gu[:, e, D:2 * D])]

        def gu2(e):
            return [(moe2_g[:, e, c * 128:(c + 1) * 128], moe2_u[:, e, c * 128:(c + 1) * 128]) for c in range(2)]

        CHOOSE = 14
        MOE = [
            dict(ln=LN1F, n=0, groups=[[0, 1], [2, 3], [4, 5], [6, 7]], experts=E1, shared=0, gu=gu1, down=lambda e: [moe1_d[:, e, :]],
                 r=moe1_r[:, :], prob=ACT.Exp, links=CHOOSE + 14, before=2, link0=0, group0=0, expert0=0, gate=gates[:, 1, 1:2]),
            dict(ln=LN2F, n=1, groups=[[e] for e in range(E2)], experts=E2, shared=1, gu=gu2,
                 down=lambda e: [moe2_d[:, e, c, :] for c in range(2)], r=moe2_r, prob=ACT.Sigmoid, links=CHOOSE + 2, before=1,
                 link0=CHOOSE + 14, group0=B * 4, expert0=B * E1, gate=gates[:, 1, 2:3]),
        ]
        GROUPS, EXPERTS = B * (4 + E2), B * (E1 + E2)

        def in_pairs(engine, halves):
            halves((0, 0), None)
            with engine.Fori(0, IT - 1) as it:
                halves((1, it), (0, it))
                halves((0, it + 1), (1, it))
            halves((1, IT - 1), (0, IT - 1))
            halves(None, (1, IT - 1))

        def keys_first(j):
            return (j + 2) % 4

        def in_quads(engine, halves):
            def quad(q, last):
                for j in range(3):
                    halves((j + 1, q), (j, q))
                halves(None if last else (0, q + 1), (3, q))

            halves((0, 0), None)
            with engine.Fori(0, QUADS - 1) as q:
                quad(q, False)
            quad(QUADS - 1, True)

        class At:

            def __init__(self, p, lp, pr):
                self.p, self.lp, self.pr = p, lp, pr
                self.l = lp * 2 + p
                self.it = lp * (2 * IT) + p * IT + pr

        def local_transformer(engine, halves, prepare=None):
            def layer(p, lp, last):
                with engine.Fori(0, IT - 1) as pr:
                    halves((1, At(p, lp, pr)), (0, At(p, lp, pr)))
                    halves((0, At(p, lp, pr + 1)), (1, At(p, lp, pr)))
                ahead = None if last else (0, At(1 - p, lp + p, 0))
                if prepare and not last:
                    prepare(1 - p, lp + p)
                halves((1, At(p, lp, IT - 1)), (0, At(p, lp, IT - 1)))
                halves(ahead, (1, At(p, lp, IT - 1)))

            if prepare:
                prepare(0, 0)
            halves((0, At(0, 0, 0)), None)
            with engine.Fori(0, DEPTH // 2 - 1) as lp:
                for p in range(2):
                    layer(p, lp, False)
            for p in range(2):
                layer(p, DEPTH // 2 - 1, p == 1)

        block = ctx.enter_context(nc.Block())

        @block.sync
        def _(sp):
            def load(dst, name, done):
                sp.dma_start(dst, dram[name]).then_inc(done, 16)

            def context(a, s, b):
                sp.dma_start(ctxT[s][:, :], dram["ctxT"][:, b, :]).then_inc(ctx_loaded[s], 16)

            load(X[:, :, :], "x", x_loaded)
            for dst, name in ((ident, "ident"), (heads16, "heads16"), (causal, "causal")):
                load(dst[:, :], name, w0_loaded)
            load(w0[:, :, :], "w0", w0_loaded)
            for s in range(G):
                context(0, s, s)
            for i, name in enumerate(("g_xattn", "g_ffn")):
                sp.dma_start(gates[:, i, :], dram[name].partition_broadcast(S)).then_inc(w0_loaded, 16)
            def layer_parts(p, l):
                return (
                    (wqkv[p], dram["wqkv"][l, :, :]), (wout[p], dram["wout"][l, :, :, :]), (wff1[p], dram["wff1"][l, :, :]),
                    (wff2[p][:, 0:2, :], dram["wff2"][l, 0:256, :].rearrange("(c p) n -> p c n", p=128)),
                    (wff2[p][0:HID - 256, 2, :], dram["wff2"][l, 256:HID, :]),
                    (lcol[p][:, :], dram["lcol"][l, :, :]), (bff2[p], dram["bff2"][bass.ds(l, 1), :].partition_broadcast(S)),
                    (qk_scale[p][:, 0, :], dram["q_scale"][bass.ds(l, 1), :].partition_broadcast(S)),
                    (qk_scale[p][:, 1, :], dram["k_scale"][bass.ds(l, 1), :].partition_broadcast(S)),
                )

            def load_layer(p, l):
                for dst, src in layer_parts(p, l):
                    sp.dma_start(dst, src).then_inc(lw_loaded[p], 16)

            def first_contexts(a):
                sp.wait_ge(v_ps, 16 * a)
                for s in range(G):
                    context(a, s, s)

            def contexts(a):
                with sp.Fori(0, IT - 1) as it:
                    for s in range(G):
                        sp.wait_ge(v_ps, nth(16 * a, it, s))
                        context(a, s, it * G + s + G)

            behind = [(dst[:, :], dram[name], w1_loaded) for dst, name in (
                (shift, "shift"), (band_f, "band"), (heads2, "heads2"), (blockpair, "pair"), (rank, "rank"), (aff1, "aff1"), (moe1_r, "moe1_r"))]
            behind += [(dst[:, :, :], dram[name], w1_loaded) for dst, name in ((rot, "rot"), (w1, "w1"), (moe1_gu, "moe1_gu"), (moe1_d, "moe1_d"))]
            behind[8:8] = [(dst, src, lw_loaded[p]) for p in range(2) for dst, src in layer_parts(p, p)]
            per = -(-len(behind) // (IT - 1))
            for it in range(IT - 1):
                for s in range(G):
                    sp.wait_ge(v_ps, nth(0, it, s))
                    context(0, s, it * G + s + G)
                for dst, src, done in behind[it * per:(it + 1) * per]:
                    sp.dma_start(dst, src).then_inc(done, 16)
            first_contexts(1)
            with sp.Fori(0, DEPTH // 2 - 1) as lp:
                for p in range(2):
                    sp.wait_ge(ffn_done, G + (lp * 2 + p + 1) * B)
                    load_layer(p, lp * 2 + p + 2)
            contexts(1)
            first_contexts(2)
            sp.wait_ge(ffn_done, G + DEPTH * B)
            for dst, name in ((moe2_g, "moe2_g"), (moe2_u, "moe2_u"), (w2, "w2"), (w3, "w3"), (w3o, "w3o")):
                load(dst, name, late_loaded)
            load(moe2_d, "moe2_d", late_loaded)
            load(side[:, :], "side", late_loaded)
            for dst, name in ((og, "og"), (ob, "ob"), (bqkv, "bqkv"), (nullk, "nullk"), (moe2_r, "moe2_r"), (moe3_r, "moe3_r")):
                load(dst, name, late_loaded)
            for dst, name in ((qg, "qg"), (qb, "qb"), (moe2_rb, "moe2_rb"), (moe3_rb, "moe3_rb"), (bo2[:, :], "bo2")):
                sp.dma_start(dst, dram[name].partition_broadcast(128)).then_inc(late_loaded, 16)
            contexts(2)
            first_contexts(3)
            sp.wait_ge(x_updated, G + LN3)
            for s in range(G):
                load(V3[s][M:KEYS3, :], "nullv", late_loaded)
            contexts(3)

            def expert(j, q):
                e = sp.value_load(chosen[0:1, q * 4 + j, 0:1], min_val=0, max_val=E3 - 1)
                for dst, src in (
                    (F1[j], dram["moe3_w1"][bass.ds(e, 1), :, :].rearrange("a p n -> (a p) n")),
                    (F2[j], dram["moe3_w2"][bass.ds(e, 1), :, :, :].rearrange("a p c n -> (a p) c n")),
                    (FB1[j], dram["moe3_b1"][bass.ds(e, 1), :, :].rearrange("a p n -> (a p) n")),
                    (FB2[j], dram["moe3_b2"][bass.ds(e, 1), :].partition_broadcast(S)),
                ):
                    sp.dma_start(dst, src).then_inc(expert_loaded[j], 16)

            def store(q):
                sp.wait_ge(x_updated, G + LN3F + 4 * (q + 1))
                sp.dma_start(out[:, bass.ds(q * 4, 4), :], X[:, bass.ds(q * 4, 4), :]).then_inc(stored, 16)

            sp.wait_ge(ffn_gated, 1)
            sp.wait_ge(e_chosen, B)
            for j in range(4):
                expert(j, 0)
            with sp.Fori(0, QUADS - 1) as q:
                for j in range(4):
                    sp.wait_ge(m_acc, EXPERTS + 4 * q + j + 1)
                    expert(j, q + 1)
                store(q)
            store(QUADS - 1)
            sp.wait_ge(stored, 16 * QUADS)

        @block.tensor
        def _(pe):
            def transpose_x(s, ready, n):
                pe.wait_ge(ready, n)
                nc.tensor.transpose(ps[s][:, 0, 0:S], xn[s][:, :], ident[:, :]).then_inc(xnT_ps, 1)

            def attention(a, i):
                H, dv, C, HB, OB = a["H"], a["dv"], a["C"], a["HB"], a["OB"]
                no = NB[a["ln"]]

                def keys(s, it):
                    pe.wait_ge(ctx_loaded[s], 16 * (IT * i + it + 1))
                    pe.wait_ge(x_updated, nth(a["ln"], it, s))
                    for c in range(C):
                        last = nc.tensor.matmul(ps[s][:, 2, c * M:(c + 1) * M], a["wk"][:, c * 128:(c + 1) * 128],
                                                ctxT[s][:, :], start=True, stop=True)
                    last.then_inc(k_ps, 1)

                def values(s, it):
                    nc.tensor.matmul(ps[s][0:M, 3, 0:H * dv], ctxT[s][:, :], a["wv"], start=True, stop=True).then_inc(v_ps, 1)

                def normed_T(s, it):
                    if i == 1:
                        transpose_x(s, x_normed2, nth(0, it, s))
                    else:
                        transpose_x(s, x_normed, nth(no, it, s))

                def queries(s, it):
                    pe.wait_ge(xnT_ready, nth(no, it, s))
                    for c in range(C):
                        last = nc.tensor.matmul(ps[s][:, 1, c * S:(c + 1) * S], a["wq"][:, c * 128:(c + 1) * 128],
                                                xnT[s][:, :], start=True, stop=True)
                    last.then_inc(q_ps, 1)

                def scores(s, it, j):
                    if j == 0:
                        pe.wait_ge(kx_ready, nth(16 * i, it, s))
                        pe.wait_ge(v_ready, nth(16 * i, it, s))
                        pe.wait_ge(qT_ready, nth(16 * i, it, s))
                    c = j if C == 4 else 0
                    if i == 0:
                        nc.tensor.matmul(heads4(ps[s][:, j, 0:HB * M]), ident_b[:, :], causal_b[:, None, :].to_broadcast([S, HB, M]),
                                         start=True, stop=False)
                    nc.tensor.matmul(ps[s][:, j, 0:HB * M], XQT[s][:, c * S:(c + 1) * S], XKX[s][:, j * HB * M:(j + 1) * HB * M],
                                     start=(i > 0), stop=True).then_inc(sc_ps, 1)

                def probs_T(s, it, j):
                    pe.wait_ge(sc_exp, nth(16 * i, it, s, 4, j))
                    for h in range(HB):
                        last = nc.tensor.transpose(ps[s][0:M, j, h * S:(h + 1) * S],
                                                   XP[s][:, (j * HB + h) * M:(j * HB + h + 1) * M], ident[:, :])
                    last.then_inc(pT_ps, 1)

                def probs_values(s, it, j):
                    pe.wait_ge(pT_act if j < 2 else pT_dve, nth(16 * i, it, s, 2, j % 2))
                    w = dv + 1
                    for h in range(j * HB, (j + 1) * HB):
                        last = nc.tensor.matmul(ps[s][:, h // OB, (h % OB) * w:(h % OB + 1) * w],
                                                XPT[s][:, h * S:(h + 1) * S], XV[s][:, h * w:(h + 1) * w], start=True, stop=True)
                    if j == 3:
                        last.then_inc(o_ps, 1)

                def outputs_T(s, it):
                    pe.wait_ge(o_ready, nth(16 * i, it, s))
                    for c in range(C):
                        last = nc.tensor.transpose(ps[s][:, 2, c * S:(c + 1) * S], XO[s][:, c * 128:(c + 1) * 128], ident[:, :])
                    last.then_inc(oT_ps, 1)

                def project(s, it):
                    pe.wait_ge(oT_ready, nth(16 * i, it, s))
                    for c in range(C):
                        last = nc.tensor.matmul(ps[s][:, 3, 0:D], XOT[s][:, c * S:(c + 1) * S], a["wo"][:, c, :],
                                                start=(c == 0), stop=(c == C - 1))
                    last.then_inc(y_ps, 1)

                if i == 1:
                    def halves(a, b):
                        if a: keys(*a)
                        if b:
                            probs_values(*b, 0)
                            probs_values(*b, 1)
                            probs_T(*b, 2)
                            probs_T(*b, 3)
                        if a: values(*a)
                        if b: probs_values(*b, 2)
                        if a: normed_T(*a)
                        if b: probs_values(*b, 3)
                        if a: queries(*a)
                        if b: outputs_T(*b)
                        if a:
                            scores(*a, 0)
                            scores(*a, 1)
                        if b: project(*b)
                        if a:
                            scores(*a, 2)
                            scores(*a, 3)
                            probs_T(*a, 0)
                            probs_T(*a, 1)
                else:
                    def halves(a, b):
                        if b:
                            probs_T(*b, 0)
                            probs_T(*b, 1)
                        if a: keys(*a)
                        if b:
                            probs_values(*b, 0)
                            probs_T(*b, 2)
                        if a: values(*a)
                        if b:
                            probs_values(*b, 1)
                            probs_T(*b, 3)
                        if a: normed_T(*a)
                        if b: probs_values(*b, 2)
                        if a: queries(*a)
                        if b: probs_values(*b, 3)
                        if a:
                            scores(*a, 0)
                            scores(*a, 1)
                            scores(*a, 2)
                        if b: outputs_T(*b)
                        if a: scores(*a, 3)
                        if b: project(*b)

                in_pairs(pe, halves)

            def tokens_T(s, w):
                pe.wait_ge(l_y, nth(0, w.it, s))
                nc.tensor.transpose(ps[s][:, 0, 0:S], xw[s][:, :], ident[:, :]).then_inc(l_xsT_ps, 1)

            def queries_keys(s, w, j):
                if j == 2:
                    pe.wait_ge(lw_loaded[w.p], 144 * (w.lp + 1))
                    pe.wait_ge(l_xsT, nth(0, w.it, s))
                nc.tensor.matmul(ps[s][:, j, :], xsT[s], wqkv[w.p][:, j * 512:(j + 1) * 512],
                                 start=True, stop=True).then_inc(l_qk_ps, 1)

            def queries_keys_T(s, w, j):
                if j < 2:
                    pe.wait_ge(l_rsum, nth(0, w.it, s, 4, keys_first(j)))
                else:
                    pe.wait_ge(l_kn, nth(0, w.it, s, 2, j - 2))
                for c in range(4):
                    last = nc.tensor.transpose(ps[s][:, j, c * S:(c + 1) * S],
                                               QR[s][:, j * 512 + c * 128:j * 512 + (c + 1) * 128], ident[:, :])
                last.then_inc(l_qkT_ps, 1)

            def values(s, w, j):
                pe.wait_ge(l_qkT, nth(0, w.it, s, 4, keys_first(2 + j)))
                nc.tensor.matmul(ps[s][:, 2 + j, :], xsT[s], wqkv[w.p][:, K2 + j * 512:K2 + (j + 1) * 512],
                                 start=True, stop=True).then_inc(l_v_ps, 1)

            def scores(s, w, g):
                if g < 2:
                    pe.wait_ge(l_qkT, nth(0, w.it, s, 4, keys_first(g)))
                else:
                    pe.wait_ge(l_v, nth(0, w.it, s, 2, g - 2))
                odd, c0 = g // 2, (g % 2) * 4
                nc.tensor.matmul(ps[s][:, g, :].rearrange("p (c n) -> p c n", n=S), ident_b[:, :],
                                 band_b[:, None, :].to_broadcast([S, 4, S]), start=True, stop=False,
                                 skip_group_check=True)
                for c in range(4):
                    rows = slice(64 * odd, 64 * odd + 64)
                    cols = slice((c0 + c) * S, (c0 + c + 1) * S)
                    last = nc.tensor.matmul(ps[s][:, g, c * S:(c + 1) * S], QKT[s][rows, cols],
                                            QKT[s][rows, INNER + (c0 + c) * S:INNER + (c0 + c + 1) * S],
                                            start=False, stop=(c == 3), skip_group_check=True)
                last.then_inc(l_sc_ps, 1)

            def probs_T(s, w, g):
                pe.wait_ge(l_exp, nth(0, w.it, s, 4, g))
                for c in range(4):
                    last = nc.tensor.transpose(ps[s][:, g, c * S:(c + 1) * S],
                                               LP[s][:, g * 512 + c * S:g * 512 + (c + 1) * S], ident[:, :])
                last.then_inc(l_pT_ps, 1)

            def probs_values(s, w, g):
                pe.wait_ge(l_v, nth(0, w.it, s, 2, g % 2))
                pe.wait_ge(l_pT, nth(0, w.it, s, 4, g))
                for c in range(4):
                    h = 2 * ((g % 2) * 4 + c) + g // 2
                    last = nc.tensor.matmul(ps[s][:, g, c * 65:(c + 1) * 65],
                                            LPT[s][:, g * 512 + c * S:g * 512 + (c + 1) * S], LV[s][:, h, :],
                                            start=True, stop=True)
                last.then_inc(l_pv_ps, 1)

            def outputs_T(s, w, j):
                pe.wait_ge(l_o, nth(0, w.it, s, 4, 2 + j))
                for c in range(4):
                    last = nc.tensor.transpose(ps[s][:, j, c * S:(c + 1) * S],
                                               LO[s][:, (4 * j + c) * 128:(4 * j + c + 1) * 128], ident[:, :])
                last.then_inc(l_oT_ps, 1)

            def project(s, w, j):
                pe.wait_ge(l_oT, nth(0, w.it, s, 2, j))
                for c in range(4 * j, 4 * j + 4):
                    last = nc.tensor.matmul(ps[s][:, 2, 0:D], LOT[s][:, c, :], wout[w.p][:, c, :],
                                            start=(c == 0), stop=(c == 7))
                if j:
                    last.then_inc(l_att_ps, 1)

            def shift_back(s, w):
                pe.wait_ge(l_y1, nth(0, w.it, s))
                nc.tensor.matmul(ps[s][:, 3, 0:64], shift[:, :], y1[s][:, 64:128],
                                 start=True, stop=True).then_inc(l_sh_ps, 1)

            def normed_T(s, w):
                pe.wait_ge(l_xn, nth(0, w.it, s, 2, 1))
                nc.tensor.transpose(ps[s][:, 0, 0:S], xn[s][:, :], ident[:, :]).then_inc(l_xnT_ps, 1)

            def up(s, w, value):
                if not value:
                    pe.wait_ge(l_xnT, nth(0, w.it, s))
                for c, (lo, hi) in enumerate(HC):
                    at = lo if value else HID + lo
                    last = nc.tensor.matmul(ps[s][0:hi - lo, 1 + value, c * S:(c + 1) * S],
                                            wff1[w.p][:, at:at + hi - lo], xnT[s][:, :], start=True, stop=True)
                last.then_inc(l_gate_ps, 1)

            def down(s, w):
                for c, (lo, hi) in enumerate(HC):
                    pe.wait_ge(l_hid, nth(0, w.it, s, 3, c))
                    last = nc.tensor.matmul(ps[s][:, 0, 128:256], hidT[s][0:hi - lo, c, :], wff2[w.p][0:hi - lo, c, :],
                                            start=(c == 0), stop=(c == 2))
                last.then_inc(l_ff_ps, 1)

            def halves(a, b):
                if b: scores(*b, 2)
                if a: tokens_T(*a)
                if b: scores(*b, 3)
                if a:
                    queries_keys(*a, 2)
                    queries_keys(*a, 3)
                    queries_keys(*a, 0)
                if b:
                    probs_T(*b, 0)
                    probs_T(*b, 1)
                if a: queries_keys(*a, 1)
                if b:
                    probs_T(*b, 2)
                    probs_values(*b, 0)
                    probs_T(*b, 3)
                    probs_values(*b, 1)
                    probs_values(*b, 2)
                    probs_values(*b, 3)
                    outputs_T(*b, 0)
                if a: queries_keys_T(*a, 2)
                if b:
                    outputs_T(*b, 1)
                    project(*b, 0)
                    project(*b, 1)
                if a: values(*a, 0)
                if b: shift_back(*b)
                if a:
                    queries_keys_T(*a, 3)
                    queries_keys_T(*a, 0)
                    queries_keys_T(*a, 1)
                    values(*a, 1)
                if b: normed_T(*b)
                if a: scores(*a, 0)
                if b:
                    up(*b, 0)
                    up(*b, 1)
                if a: scores(*a, 1)
                if b: down(*b)

            def quad_T(n, q):
                pe.wait_ge(r_norm, n * QUADS + q + 1)
                for c in range(4):
                    last = nc.tensor.transpose(ps[q % G][:, 2 * (q // G), c * S:(c + 1) * S], XNQ[q][:, c * D:(c + 1) * D], ident[:, :])
                last.then_inc(r_T_ps, 1)

            def mixture(m):
                groups = m["groups"]
                NG = len(groups)

                for q in range(QUADS):
                    quad_T(m["n"], q)
                for q in range(QUADS):
                    pe.wait_ge(r_T, m["n"] * QUADS + q + 1)
                    for c in range(4):
                        last = nc.tensor.matmul(ps[q % G][:, 1 + 2 * (q // G), c * 8:(c + 1) * 8], XNTQ[q][:, c * S:(c + 1) * S], m["r"],
                                                start=True, stop=True)
                    last.then_inc(r_lg_ps, 1)

                def gates_ups(s, it, g):
                    if g == 0:
                        pe.wait_ge(r_kept, 2 * QUADS * (m["n"] + 1))
                    if g > 1:
                        pe.wait_ge(m_act, m["group0"] + nth(0, it, s, NG, g - 2))
                    u = 0
                    for e in groups[g]:
                        for wg, wu in m["gu"](e):
                            nc.tensor.matmul(ps[s][:, 2 + g % 2, u * S:(u + 1) * S], wg, XNT[:, it * G + s, :], start=True, stop=True)
                            last = nc.tensor.matmul(ps[s][:, 2 + g % 2, (2 + u) * S:(3 + u) * S], wu, XNT[:, it * G + s, :], start=True, stop=True)
                            u += 1
                    last.then_inc(m_gu_ps, 1)

                def down(s, it, g):
                    if g > 1:
                        pe.wait_ge(m_acc, m["expert0"] + nth(0, it, s, m["experts"], groups[g - 2][-1]))
                    pe.wait_ge(m_act, m["group0"] + nth(0, it, s, NG, g))
                    u = 0
                    for n, e in enumerate(groups[g]):
                        wd = m["down"](e)
                        for c, w in enumerate(wd):
                            last = nc.tensor.matmul(ps[s][:, g % 2, n * D:(n + 1) * D], AT[s][g % 2][:, u * S:(u + 1) * S], w,
                                                    start=(c == 0), stop=(c == len(wd) - 1))
                            u += 1
                    last.then_inc(m_dn_ps, 1)

                def halves(a, b):
                    for g in range(NG):
                        if b: down(*b, g)
                        if b and g + 2 < NG: gates_ups(*b, g + 2)
                        if a and g + 2 >= NG: gates_ups(*a, g + 2 - NG)

                in_pairs(pe, halves)

            def linear_attention():
                def keys(s, it):
                    pe.wait_ge(ctx_loaded[s], 16 * (IT * 3 + it + 1))
                    pe.wait_ge(x_updated, nth(LN3, it, s))
                    for c in range(4):
                        last = nc.tensor.matmul(ps[s][:, 2, c * M:(c + 1) * M], w3[:, 1, c * 128:(c + 1) * 128],
                                                ctxT[s][:, :], start=True, stop=True)
                    last.then_inc(k_ps, 1)

                def values(s, it):
                    nc.tensor.matmul(ps[s][0:M, 3, :], ctxT[s][:, :], w3[:, 2, :], start=True, stop=True).then_inc(v_ps, 1)

                def normed_T(s, it):
                    transpose_x(s, x_normed, nth(NB[LN3], it, s))

                def queries(s, it):
                    pe.wait_ge(xnT_ready, nth(NB[LN3], it, s))
                    nc.tensor.matmul(ps[s][:, 1, :], xnT[s][:, :], w3[:, 0, :], start=True, stop=True).then_inc(q_ps, 1)

                def keys_T(s, it):
                    pe.wait_ge(t_knormed, nth(0, it, s))
                    for c in range(4):
                        last = nc.tensor.transpose(ps[s][0:KEYS3, 2, c * 128:(c + 1) * 128], K3E[s][:, c, :], ident[:, :])
                    last.then_inc(t_kT_ps, 1)

                def keys_values(s, it):
                    pe.wait_ge(t_v, nth(0, it, s))
                    pe.wait_ge(t_kT, nth(0, it, s))
                    for c in range(4):
                        cols = slice(c * 128, (c + 1) * 128)
                        last = nc.tensor.matmul(ps[s][:, 3, cols], K3T[s][:, cols], V3[s][:, cols], start=True, stop=True)
                    last.then_inc(t_c_ps, 1)

                def queries_T(s, it):
                    pe.wait_ge(t_qexp, nth(0, it, s))
                    for c in range(4):
                        last = nc.tensor.transpose(ps[s][:, 0, c * S:(c + 1) * S], Q3[s][:, c * 128:(c + 1) * 128], ident[:, :])
                    last.then_inc(t_qT_ps, 1)

                def outputs(s, it):
                    pe.wait_ge(t_c, nth(0, it, s))
                    pe.wait_ge(t_qT, nth(0, it, s))
                    for c in range(4):
                        last = nc.tensor.matmul(ps[s][:, 1, c * 128:(c + 1) * 128], Q3T[s][:, c, :], C3[s][:, c, :],
                                                start=True, stop=True)
                    last.then_inc(t_o_ps, 1)

                def outputs_T(s, it):
                    pe.wait_ge(t_o, nth(0, it, s))
                    for c in range(4):
                        last = nc.tensor.transpose(ps[s][:, 2, c * S:(c + 1) * S], O3[s][:, c * 128:(c + 1) * 128], ident[:, :])
                    last.then_inc(t_oT_ps, 1)

                def project(s, it):
                    pe.wait_ge(t_oT, nth(0, it, s))
                    for c in range(4):
                        last = nc.tensor.matmul(ps[s][:, 3, 0:D], O3T[s][:, c, :], w3o[:, c, :],
                                                start=(c == 0), stop=(c == 3))
                    last.then_inc(t_y_ps, 1)

                def halves(a, b):
                    if b:
                        keys_values(*b)
                        queries_T(*b)
                    if a: keys(*a)
                    if b: outputs(*b)
                    if a:
                        normed_T(*a)
                        queries(*a)
                        values(*a)
                    if b: outputs_T(*b)
                    if a: keys_T(*a)
                    if b: project(*b)

                in_pairs(pe, halves)

            def chosen_expert():
                for q in range(QUADS):
                    quad_T(2, q)
                for q in range(QUADS):
                    pe.wait_ge(e_mean, q + 1)
                    for c in range(4):
                        last = nc.tensor.matmul(ps[q % G][0:1, 1 + 2 * (q // G), c * 8:(c + 1) * 8], tokmean[:, q * 4 + c:q * 4 + c + 1], moe3_r,
                                                start=True, stop=True)
                    last.then_inc(r_lg_ps, 1)
                pe.wait_ge(r_kept, 6 * QUADS)

                def up(j, q):
                    pe.wait_ge(expert_loaded[j], 64 * (q + 1))
                    for c in range(4):
                        last = nc.tensor.matmul(ps[j % G][:, 2, c * S:(c + 1) * S], F1[j][:, c * 128:(c + 1) * 128],
                                                XNT[:, q * 4 + j, :], start=True, stop=True)
                    last.then_inc(m_gu_ps, 1)

                def down(j, q):
                    pe.wait_ge(m_silu, GROUPS + q * 4 + j + 1)
                    pe.wait_ge(m_acc, EXPERTS + q * 4 + j - 1)
                    for c in range(4):
                        last = nc.tensor.matmul(ps[j % G][:, 3, 0:D], F1T[j % G][:, c, :], F2[j][:, c, :],
                                                start=(c == 0), stop=(c == 3))
                    last.then_inc(m_dn_ps, 1)

                def halves(a, b):
                    if a: up(*a)
                    if b: down(*b)

                in_quads(pe, halves)

            pe.wait_ge(w0_loaded, 96)
            pe.wait_ge(consts_cast, 2)
            attention(XA[0], 0)
            pe.wait_ge(consts_cast, 3)
            local_transformer(pe, halves)
            pe.wait_ge(ffn_gated, 1)
            pe.wait_ge(w1_loaded, 176)
            attention(XA[1], 1)
            mixture(MOE[0])
            pe.wait_ge(late_loaded, 288)
            attention(XA[2], 2)
            mixture(MOE[1])
            pe.wait_ge(late_loaded, 320)
            linear_attention()
            chosen_expert()

        @block.scalar
        def _(act):
            def copy(dst, src, **kw):
                return nc.scalar.activation(dst, src, ACT.Identity if kw else ACT.Copy, **kw)

            def attention(a, i):
                H, dv, C, HB, no = a["H"], a["dv"], a["C"], a["HB"], NB[a["ln"]]

                def keys(s, it):
                    act.wait_ge(k_ps, nth(16 * i, it, s))
                    kw = dict(bias=bqkv[:, 1:2]) if i == 2 else {}
                    copy(XKT[s][:, 0:C * M], ps[s][:, 2, 0:C * M], **kw).then_inc(kT_ready, 1)

                def values(s, it):
                    act.wait_ge(v_ps, nth(16 * i, it, s))
                    copy(heads4(XV[s][:, 0:H * (dv + 1)], dv + 1)[:, :, 0:dv],
                         ps[s][0:M, 3, 0:H * dv].rearrange("p (h e) -> p h e", e=dv)).then_inc(v_ready, 1)

                def normed_T(s, it):
                    act.wait_ge(xnT_ps, nth(no, it, s))
                    kw = dict(scale=aff1[:, 0:1], bias=aff1[:, 1:2]) if i == 1 else {}
                    copy(xnT[s][:, :], ps[s][:, 0, 0:S], **kw).then_inc(xnT_ready, 1)

                def queries(s, it):
                    act.wait_ge(q_ps, nth(16 * i, it, s))
                    kw = dict(scale=8 ** -0.5, bias=bq_s) if i == 2 else {}
                    copy(XQT[s][:, 0:C * S], ps[s][:, 1, 0:C * S], **kw).then_inc(qT_ready, 1)

                def exponentials(s, it, j):
                    act.wait_ge(sc_shifted, nth(16 * i, it, s, 4, j))
                    P = XP[s][:, j * HB * M:(j + 1) * HB * M]
                    nc.scalar.activation(P, P, ACT.Exp, scale=a["scale"]).then_inc(sc_exp, 1)

                def probs_T(s, it, j):
                    act.wait_ge(pT_ps, nth(16 * i, it, s, 4, j))
                    copy(XPT[s][:, j * HB * S:(j + 1) * HB * S], ps[s][0:M, j, 0:HB * S]).then_inc(pT_act, 1)

                def outputs_T(s, it):
                    act.wait_ge(oT_ps, nth(16 * i, it, s))
                    kw = dict(bias=bqkv[:, 2:3]) if i == 2 else {}
                    copy(XOT[s][:, 0:C * S], ps[s][:, 2, 0:C * S], **kw).then_inc(oT_ready, 1)

                if i == 1:
                    def halves(a, b):
                        if b:
                            probs_T(*b, 0)
                            probs_T(*b, 1)
                            exponentials(*b, 2)
                            exponentials(*b, 3)
                        if a:
                            keys(*a)
                            values(*a)
                            normed_T(*a)
                            queries(*a)
                        if b: outputs_T(*b)
                        if a:
                            exponentials(*a, 0)
                            exponentials(*a, 1)
                else:
                    def halves(a, b):
                        if b:
                            exponentials(*b, 0)
                            exponentials(*b, 1)
                            probs_T(*b, 0)
                            exponentials(*b, 2)
                        if a: keys(*a)
                        if b:
                            probs_T(*b, 1)
                            exponentials(*b, 3)
                        if a:
                            normed_T(*a)
                            values(*a)
                            queries(*a)
                        if b: outputs_T(*b)

                in_pairs(act, halves)

            def shifted(s, w):
                act.wait_ge(l_xsT_ps, nth(0, w.it, s))
                copy(xsT[s][0:64, :], ps[s][0:64, 0, 0:S])
                copy(xsT[s][64:128, 1:S], ps[s][64:128, 0, 0:S - 1]).then_inc(l_xsT, 1)

            def squares(s, w, j):
                act.wait_ge(l_qk_ps, nth(0, w.it, s, 4, keys_first(j)))
                nc.scalar.activation(SQ[s][:, j * 512:(j + 1) * 512], ps[s][:, j, :], ACT.Square).then_inc(l_sq, 1)

            def queries_keys_T(s, w, j):
                act.wait_ge(l_qkT_ps, nth(0, w.it, s, 4, keys_first(j)))
                copy(QKT[s][:, j * 512:(j + 1) * 512], ps[s][:, j, :]).then_inc(l_qkT, 1)

            def values(s, w, j):
                act.wait_ge(l_v_ps, nth(0, w.it, s, 2, j))
                copy(LV[s][:, 8 * j:8 * j + 8, 0:LD], ps[s][:, 2 + j, :].rearrange("p (h e) -> p h e", e=LD)).then_inc(l_v, 1)

            def exponentials(s, w, g):
                act.wait_ge(l_shift, nth(0, w.it, s, 4, g))
                for c in range(4):
                    h = 2 * ((g % 2) * 4 + c) + g // 2
                    last = nc.scalar.activation(LP[s][:, g * 512 + c * S:g * 512 + (c + 1) * S], ps[s][:, g, c * S:(c + 1) * S],
                                                ACT.Exp, scale=rnq[s][:, h:h + 1], bias=negmx[s][:, 4 * g + c:4 * g + c + 1])
                last.then_inc(l_exp, 1)

            def probs_T(s, w, g):
                act.wait_ge(l_pT_ps, nth(0, w.it, s, 4, g))
                copy(LPT[s][:, g * 512:(g + 1) * 512], ps[s][:, g, :]).then_inc(l_pT, 1)

            def outputs_T(s, w, j):
                act.wait_ge(l_oT_ps, nth(0, w.it, s, 2, j))
                copy(LOT[s][:, 4 * j:4 * j + 4, :].rearrange("p c n -> p (c n)"), ps[s][:, j, :]).then_inc(l_oT, 1)

            def normed_T(s, w):
                act.wait_ge(lw_loaded[w.p], 144 * (w.lp + 1))
                act.wait_ge(l_xnT_ps, nth(0, w.it, s))
                copy(xnT[s][:, :], ps[s][:, 0, 0:S], scale=lcol[w.p][:, 0:1], bias=lcol[w.p][:, 1:2]).then_inc(l_xnT, 1)

            def gelu(s, w):
                act.wait_ge(l_gate_ps, nth(0, w.it, s, 2, 0))
                for c, (lo, hi) in enumerate(HC):
                    nc.scalar.activation(geluT[s][0:hi - lo, c, :], ps[s][0:hi - lo, 1, c * S:(c + 1) * S], ACT.Gelu,
                                         bias=lcol[w.p][0:hi - lo, 5 + c:6 + c]).then_inc(l_gelu, 1)

            def halves(a, b):
                if b:
                    values(*b, 1)
                    exponentials(*b, 0)
                if a: shifted(*a)
                if b: exponentials(*b, 1)
                if a: squares(*a, 2)
                if b: exponentials(*b, 2)
                if a: squares(*a, 3)
                if b:
                    probs_T(*b, 0)
                    exponentials(*b, 3)
                    probs_T(*b, 1)
                    probs_T(*b, 2)
                    probs_T(*b, 3)
                if a:
                    squares(*a, 0)
                    squares(*a, 1)
                if b:
                    outputs_T(*b, 0)
                    outputs_T(*b, 1)
                if a:
                    queries_keys_T(*a, 2)
                    queries_keys_T(*a, 3)
                    queries_keys_T(*a, 0)
                    queries_keys_T(*a, 1)
                    values(*a, 0)
                if b:
                    normed_T(*b)
                    gelu(*b)

            def quads_T(n):
                for q in range(QUADS):
                    act.wait_ge(r_T_ps, n * QUADS + q + 1)
                    copy(XNTQ[q], ps[q % G][:, 2 * (q // G), :]).then_inc(r_T, 1)

            def mixture(m):
                NG = len(m["groups"])

                quads_T(m["n"])
                act.wait_ge(m_link, m["link0"] + m["before"])
                nc.scalar.activation(PR[:, :, :], LG[:, :, :], m["prob"]).then_inc(m_link, 1)

                def silu(s, it, g):
                    act.wait_ge(m_gu_ps, m["group0"] + nth(0, it, s, NG, g))
                    nc.scalar.activation(SG[s][g % 2], ps[s][:, 2 + g % 2, 0:256], ACT.Silu).then_inc(m_silu, 1)

                def halves(a, b):
                    for g in range(NG):
                        if b and g + 2 < NG: silu(*b, g + 2)
                        if a and g + 2 >= NG: silu(*a, g + 2 - NG)

                in_pairs(act, halves)

            def linear_attention():
                for s in range(G):
                    act.wait_ge(x_updated, nth(LN3, 0, s))
                    copy(K3[s][:, :, M], nullk.to_broadcast([128, 4])).then_inc(t_k, 1)

                def keys(s, it):
                    act.wait_ge(k_ps, nth(48, it, s))
                    copy(K3[s][:, :, 0:M], ps[s][:, 2, 0:4 * M].rearrange("p (c n) -> p c n", n=M)).then_inc(t_k, 1)

                def values(s, it):
                    act.wait_ge(v_ps, nth(48, it, s))
                    copy(V3[s][0:M, :], ps[s][0:M, 3, :]).then_inc(t_v, 1)

                def normed_T(s, it):
                    act.wait_ge(xnT_ps, nth(NB[LN3], it, s))
                    copy(xnT[s][:, :], ps[s][:, 0, 0:S]).then_inc(xnT_ready, 1)

                def key_exponentials(s, it):
                    act.wait_ge(t_kshift, nth(0, it, s))
                    K = K3E[s].rearrange("p c n -> p (c n)")
                    nc.scalar.activation(K, K, ACT.Exp).then_inc(t_kexp, 1)

                def keys_T(s, it):
                    act.wait_ge(t_kT_ps, nth(0, it, s))
                    copy(K3T[s], ps[s][0:KEYS3, 2, :]).then_inc(t_kT, 1)

                def query_exponentials(s, it):
                    act.wait_ge(t_qshift, nth(0, it, s))
                    nc.scalar.activation(Q3[s], Q3[s], ACT.Exp).then_inc(t_qexp, 1)

                def queries_T(s, it):
                    act.wait_ge(t_qT_ps, nth(0, it, s))
                    copy(Q3T[s].rearrange("p c n -> p (c n)"), ps[s][:, 0, :]).then_inc(t_qT, 1)

                def outputs_T(s, it):
                    act.wait_ge(t_oT_ps, nth(0, it, s))
                    for c in range(4):
                        last = copy(O3T[s][:, c, :], ps[s][:, 2, c * S:(c + 1) * S], scale=og[:, c:c + 1], bias=ob[:, c:c + 1])
                    last.then_inc(t_oT, 1)

                def halves(a, b):
                    if b:
                        values(*b)
                        keys_T(*b)
                        query_exponentials(*b)
                        queries_T(*b)
                    if a:
                        keys(*a)
                        normed_T(*a)
                        key_exponentials(*a)
                    if b: outputs_T(*b)

                in_pairs(act, halves)

            def chosen_expert():
                quads_T(2)

                def hidden(j, q):
                    act.wait_ge(m_gu_ps, GROUPS + q * 4 + j + 1)
                    for c in range(4):
                        last = nc.scalar.activation(F1T[j % G][:, c, :], ps[j % G][:, 2, c * S:(c + 1) * S], ACT.Relu, bias=FB1[j][:, c:c + 1])
                    last.then_inc(m_silu, 1)

                def halves(a, b):
                    if a: hidden(*a)

                in_quads(act, halves)

            act.wait_ge(w0_loaded, 96)
            nc.scalar.activation(gates[:, :, :], gates[:, :, :], ACT.Tanh).then_inc(gates_ready, 1)
            act.wait_ge(v_ones, 2)
            attention(XA[0], 0)
            act.wait_ge(v_ones, 4)
            local_transformer(act, halves)
            act.wait_ge(w1_loaded, 176)
            act.wait_ge(v_ones, 6)
            attention(XA[1], 1)
            mixture(MOE[0])
            act.wait_ge(late_prep, 2)
            act.wait_ge(v_ones, 8)
            attention(XA[2], 2)
            mixture(MOE[1])
            linear_attention()
            chosen_expert()

        @block.gpsimd
        def _(pool):
            def quad_inverse_stds(n):
                for q in range(QUADS):
                    pool.wait_ge(r_mean, n * QUADS + q + 1)
                    pool.tensor_tensor(VEQ[q], MVQ[q][:, :, 1], eps_col[:, 0:1].to_broadcast([S, 4]), ALU.add).then_inc(r_var, 1)
                    pool.wait_ge(r_var, n * QUADS + q + 1)
                    pool.tensor_tensor(RSQ[q], VEQ[q], neghalf[:, 0:4], ALU.pow).then_inc(r_rstd, 1)

            def inverse_std(base, s, it):
                pool.wait_ge(ln_mean, nth(NB[base], it, s))
                pool.tensor_tensor(ve[s][:, :], mv[s][:, 1:2], eps_col[:, :], ALU.add).then_inc(ln_var, 1)
                pool.wait_ge(ln_var, nth(NB[base], it, s))
                pool.tensor_tensor(rs[s][:, :], ve[s][:, :], neghalf[:, 0:1], ALU.pow).then_inc(ln_rstd, 1)

            def attention(a, i):
                H, C, hm, ln = a["H"], a["C"], a["hm"], a["ln"]

                def second_inverse_std(s, it):
                    pool.wait_ge(ln2_mean, nth(0, it, s))
                    pool.tensor_tensor(ve[s][:, :], mv[s][:, 1:2], eps_col[:, :], ALU.add).then_inc(ln2_var, 1)
                    pool.wait_ge(ln2_var, nth(0, it, s))
                    pool.tensor_tensor(rs[s][:, :], ve[s][:, :], neghalf[:, 0:1], ALU.pow).then_inc(ln2_rstd, 1)

                def spread_keys(s, it):
                    pool.wait_ge(kT_ready, nth(16 * i, it, s))
                    pool.wait_ge(x_updated, nth(ln, it, s))
                    HQ = H // C
                    for c in range(C):
                        last = pool.tensor_tensor(heads4(XKX[s][:, c * HQ * M:(c + 1) * HQ * M]),
                                                  XKT[s][:, None, c * M:(c + 1) * M].to_broadcast([128, HQ, M]),
                                                  hm[:, :, None].to_broadcast([128, HQ, M]), ALU.mult)
                    last.then_inc(kx_ready, 1)

                if i == 1:
                    def halves(a, b):
                        if a:
                            inverse_std(ln, *a)
                            second_inverse_std(*a)
                            spread_keys(*a)
                else:
                    def halves(a, b):
                        if a:
                            inverse_std(ln, *a)
                            spread_keys(*a)

                in_pairs(pool, halves)

            def rotary_factors(p, lp):
                hd = LD // 2
                pool.wait_ge(lw_loaded[p], 144 * (lp + 1))
                for i in range(2):
                    pool.tensor_tensor(table[p][:, i, 0, :], qk_scale[p][:, i, :], rot[:, 2 * i, :], ALU.mult)
                    for lo, other in ((0, hd), (hd, 0)):
                        last = pool.tensor_tensor(table[p][:, i, 1, lo:lo + hd], qk_scale[p][:, i, other:other + hd],
                                                  rot[:, 2 * i + 1, lo:lo + hd], ALU.mult)
                last.then_inc(tables_ready, 1)

            def inverse_norms(s, w, j):
                pool.wait_ge(l_ssf, nth(0, w.it, s, 4, keys_first(j)))
                heads = slice(8 * j, 8 * j + 8)
                pool.tensor_tensor(rnq[s][:, heads], ssq[s][:, heads], neghalf[:, heads], ALU.pow).then_inc(l_rn, 1)

            def rotary_sum(s, w, j):
                pool.wait_ge(l_rb, nth(0, w.it, s, 4, keys_first(j)))
                cols = slice(j * 512, (j + 1) * 512)
                pool.tensor_tensor(QR[s][:, cols], QR[s][:, cols], RA[s][:, cols], ALU.add).then_inc(l_rsum, 1)

            def biased(s, w):
                pool.wait_ge(lw_loaded[w.p], 144 * (w.lp + 1))
                pool.wait_ge(l_y1, nth(0, w.it, s))
                pool.tensor_tensor(yb[s], y1[s], bff2[w.p], ALU.add).then_inc(l_yb, 1)

            def token_std(s, w):
                pool.wait_ge(l_mv, nth(0, w.it, s))
                pool.tensor_tensor(ve[s][:, :], mv[s][:, 1:2], eps_col[:, :], ALU.add).then_inc(l_ve, 1)
                pool.wait_ge(l_ve, nth(0, w.it, s))
                pool.tensor_tensor(rs[s][:, :], ve[s][:, :], neghalf[:, 0:1], ALU.pow).then_inc(l_rs, 1)

            def halves(a, b):
                if b: inverse_norms(*b, 1)
                if a:
                    inverse_norms(*a, 2)
                    rotary_sum(*a, 2)
                    rotary_sum(*a, 3)
                    inverse_norms(*a, 3)
                    rotary_sum(*a, 0)
                    rotary_sum(*a, 1)
                if b:
                    token_std(*b)
                    biased(*b)
                if a: inverse_norms(*a, 0)

            def linear_attention():
                def key_differences(s, it):
                    pool.wait_ge(t_klink, nth(0, it, s))
                    pool.tensor_tensor(K3E[s], K3[s], col[s][:, :, None].to_broadcast([128, 4, KEYS3]), ALU.subtract).then_inc(t_kshift, 1)

                def key_softmax(s, it):
                    pool.wait_ge(o_recip, nth(24, it, s, 2, 1))
                    pool.tensor_tensor(K3E[s], K3E[s], rc[s][:, 4:8, None].to_broadcast([128, 4, KEYS3]), ALU.mult).then_inc(t_knormed, 1)

                def query_std(s, it):
                    pool.wait_ge(t_qlink, nth(0, it, s, 2, 1))
                    pool.tensor_tensor(ve[s][:, :], mv[s][:, 1:2], eps_col[:, :], ALU.add).then_inc(t_qvar, 1)
                    pool.wait_ge(t_qvar, nth(0, it, s))
                    pool.tensor_tensor(rs[s][:, :], ve[s][:, :], neghalf[:, 0:1], ALU.pow).then_inc(t_qrs, 1)

                def output_std(s, it):
                    pool.wait_ge(t_olink, nth(0, it, s, 2, 1))
                    pool.tensor_tensor(ve[s][:, :], mv[s][:, 1:2], eps_col[:, :], ALU.add).then_inc(t_ovar, 1)
                    pool.wait_ge(t_ovar, nth(0, it, s))
                    pool.tensor_tensor(rs[s][:, :], ve[s][:, :], neghalf[:, 0:1], ALU.pow).then_inc(t_ors, 1)

                def halves(a, b):
                    if a:
                        inverse_std(LN3, *a)
                        key_differences(*a)
                    if b: output_std(*b)
                    if a:
                        query_std(*a)
                        key_softmax(*a)

                in_pairs(pool, halves)

            pool.memset(eps_col[:, :], EPS).then_inc(table_link, 1)
            pool.memset(neghalf[:, :], -0.5).then_inc(table_link, 1)
            for s in range(G):
                pool.memset(XV[s], 1.0).then_inc(v_ones, 1)
            pool.wait_ge(w0_loaded, 96)
            pool.wait_ge(table_link, 2)
            attention(XA[0], 0)
            pool.wait_ge(w1_loaded, 176)
            quad_inverse_stds(0)
            for s in range(G):
                pool.wait_ge(x_updated, G + LNY)
                pool.memset(xsT[s][:, 0:1], 0.0)
                pool.memset(LV[s], 1.0).then_inc(v_ones, 1)
            local_transformer(pool, halves, rotary_factors)
            for s in range(G):
                pool.wait_ge(ffn_gated, 1)
                pool.memset(XV[s], 1.0).then_inc(v_ones, 1)
            attention(XA[1], 1)
            quad_inverse_stds(1)
            for s in range(G):
                pool.wait_ge(x_updated, G + LN2)
                pool.memset(XV[s], 1.0).then_inc(v_ones, 1)
            attention(XA[2], 2)
            quad_inverse_stds(2)
            linear_attention()
            quad_inverse_stds(3)

        @block.vector
        def _(dve):
            V = nc.vector

            def quad_norms(n, normed_sequence, behind=None):
                def statistics(q):
                    V.tensor_scalar(XQ[q].rearrange("p (b d) -> p b d", d=D), X[:, q * 4:q * 4 + 4, :], 1.0, None, ALU.mult).then_inc(r_x, 1)
                    for c in range(4):
                        last = V.bn_stats(STQ[q][:, c * 6:(c + 1) * 6], X[:, q * 4 + c, :])
                    last.then_inc(r_stats, 1)

                def means(q):
                    dve.wait_ge(r_stats, n * QUADS + q + 1)
                    for c in range(4):
                        last = V.bn_aggr(MVQ[q][:, c, :], STQ[q][:, c * 6:(c + 1) * 6])
                    last.then_inc(r_mean, 1)

                statistics(0)
                for q in range(QUADS):
                    if q + 1 < QUADS:
                        statistics(q + 1)
                    means(q)
                for q in range(QUADS):
                    dve.wait_ge(r_x, n * QUADS + q + 1)
                    dve.wait_ge(r_rstd, n * QUADS + q + 1)
                    for c in range(4):
                        last = V.tensor_scalar(normed_sequence(q, c), XQ[q][:, c * D:(c + 1) * D], MVQ[q][:, c, 0:1], RSQ[q][:, c:c + 1],
                                               ALU.subtract, ALU.mult)
                    if behind:
                        last.then_inc(r_norm, 1)
                    else:
                        last.then_inc(x_updated, 4)
                if behind:
                    for q in range(QUADS):
                        behind(q)

            def normed_columns(q, c):
                return XNQ[q][:, c * D:(c + 1) * D]

            def keep_T(n, q):
                dve.wait_ge(r_T, n * QUADS + q + 1)
                V.tensor_scalar(XNT[:, q * 4:q * 4 + 4, :], XNTQ[q].rearrange("p (b d) -> p b d", d=S), 1.0, None, ALU.mult).then_inc(r_kept, 1)

            def normed(s):
                V.tensor_scalar(xn[s][:, :], xw[s][:, :], mv[s][:, 0:1], rs[s][:, 0:1], ALU.subtract, ALU.mult).then_inc(x_normed, 1)

            def copied(base, s, it):
                dve.wait_ge(x_updated, nth(base, it, s))
                V.tensor_scalar(xw[s][:, :], X[:, it * G + s, :], 1.0, None, ALU.mult).then_inc(xw_ready, 1)

            def statistics_x(base, s, it):
                dve.wait_ge(xw_ready, nth(NB[base], it, s))
                V.bn_stats(st[s][:, 0:6], xw[s][:, :]).then_inc(ln_stats, 1)

            def aggregated_x(base, s, it):
                dve.compute_val(nth(NB[base], it, s))
                dve.wait_ge(x_loaded, 16)
                dve.wait_ge(ln_stats, nth(NB[base], it, s))
                V.bn_aggr(mv[s][:, :], st[s][:, 0:6]).then_inc(ln_mean, 1)

            def attention(a, i):
                H, dv, C, HB, OB = a["H"], a["dv"], a["C"], a["HB"], a["OB"]
                no, ln = NB[a["ln"]], a["ln"]

                def normalised(s, it):
                    dve.wait_ge(ln_rstd, nth(NB[ln], it, s))
                    normed(s)

                def second_statistics(s, it):
                    dve.wait_ge(x_normed, nth(no, it, s))
                    V.bn_stats(st[s][:, 0:6], xn[s][:, :]).then_inc(ln2_stats, 1)
                    dve.compute_val(nth(0, it, s))
                    dve.wait_ge(x_loaded, 16)
                    dve.wait_ge(ln2_stats, nth(0, it, s))
                    V.bn_aggr(mv[s][:, :], st[s][:, 0:6]).then_inc(ln2_mean, 1)

                def normalised_again(s, it):
                    dve.wait_ge(ln2_rstd, nth(0, it, s))
                    V.tensor_scalar(xn[s][:, :], xn[s][:, :], mv[s][:, 0:1], rs[s][:, 0:1],
                                    ALU.subtract, ALU.mult).then_inc(x_normed2, 1)

                def quarter(s, j):
                    return heads4(XP[s][:, j * HB * M:(j + 1) * HB * M])

                def source(s, j):
                    return quarter(s, j) if i == 2 else heads4(ps[s][:, j, 0:HB * M])

                def masked(s, it, j):
                    if i == 2:
                        dve.wait_ge(sc_ps, nth(16 * i, it, s, 4, j))
                        V.tensor_tensor(quarter(s, j), heads4(ps[s][:, j, 0:HB * M]), side[:, None, :].to_broadcast([S, HB, M]),
                                        ALU.add).then_inc(sc_masked, 1)

                def maxima(s, it, j):
                    if i == 2:
                        dve.wait_ge(sc_masked, nth(0, it, s, 4, j))
                    else:
                        dve.wait_ge(sc_ps, nth(16 * i, it, s, 4, j))
                    V.tensor_reduce(mx[s][:, j * HB:(j + 1) * HB], source(s, j), AX.X, ALU.max).then_inc(sc_max, 1)

                def differences(s, it, j):
                    dve.wait_ge(sc_max, nth(16 * i, it, s, 4, j))
                    V.tensor_tensor(quarter(s, j), source(s, j), mx[s][:, j * HB:(j + 1) * HB, None].to_broadcast([S, HB, M]),
                                    ALU.subtract).then_inc(sc_shifted, 1)

                def probs_T(s, it, j):
                    dve.wait_ge(pT_ps, nth(16 * i, it, s, 4, j))
                    V.tensor_copy(XPT[s][:, j * HB * S:(j + 1) * HB * S], ps[s][0:M, j, 0:HB * S]).then_inc(pT_dve, 1)

                banks = H // OB

                def summed(s):
                    return ps[s][:, 0:banks, 0:OB * (dv + 1)].rearrange("p j (h e) -> p j h e", e=dv + 1)

                def inverse_sums(s, it):
                    dve.wait_ge(o_ps, nth(16 * i, it, s))
                    V.reciprocal(rc[s][:, 0:H].rearrange("p (j h) -> p j h", j=banks), summed(s)[:, :, :, dv]).then_inc(o_recip, 1)

                def outputs(s, it):
                    dve.wait_ge(o_recip, nth(16 * i, it, s))
                    for j in range(banks):
                        last = V.tensor_tensor(XO[s][:, j * OB * dv:(j + 1) * OB * dv].rearrange("p (h e) -> p h e", e=dv),
                                               summed(s)[:, j, :, 0:dv],
                                               rc[s][:, j * OB:(j + 1) * OB, None].to_broadcast([S, OB, dv]), ALU.mult)
                    last.then_inc(o_ready, 1)

                def residual(s, it):
                    dve.wait_ge(y_ps, nth(16 * i, it, s))
                    y = ps[s][:, 3, 0:D]
                    if i == 2:
                        V.tensor_tensor(xt[s], y, bo2[:, :], ALU.add).then_inc(y_biased, 1)
                        dve.wait_ge(y_biased, nth(0, it, s))
                        y = xt[s]
                    V.scalar_tensor_tensor(X[:, it * G + s, :], y, a["gate"], xw[s][:, :], ALU.mult, ALU.add).then_inc(x_updated, 1)

                if i == 1:
                    def halves(a, b):
                        if a: copied(ln, *a)
                        if b: maxima(*b, 2)
                        if a:
                            statistics_x(ln, *a)
                            aggregated_x(ln, *a)
                        if b:
                            maxima(*b, 3)
                            differences(*b, 2)
                            differences(*b, 3)
                        if a:
                            normalised(*a)
                            second_statistics(*a)
                        if b:
                            probs_T(*b, 2)
                            probs_T(*b, 3)
                        if a: normalised_again(*a)
                        if b:
                            inverse_sums(*b)
                            outputs(*b)
                        if a:
                            maxima(*a, 0)
                            maxima(*a, 1)
                            differences(*a, 0)
                            differences(*a, 1)
                        if b: residual(*b)
                else:
                    def halves(a, b):
                        if b: maxima(*b, 2)
                        if a: copied(ln, *a)
                        if b: differences(*b, 2)
                        if a: statistics_x(ln, *a)
                        if b: masked(*b, 3)
                        if a: aggregated_x(ln, *a)
                        if b:
                            maxima(*b, 3)
                            differences(*b, 3)
                        if a: normalised(*a)
                        if b:
                            probs_T(*b, 2)
                            probs_T(*b, 3)
                            inverse_sums(*b)
                            outputs(*b)
                        if a:
                            masked(*a, 0)
                            maxima(*a, 0)
                            masked(*a, 1)
                            differences(*a, 0)
                            maxima(*a, 1)
                            masked(*a, 2)
                            differences(*a, 1)
                        if b: residual(*b)

                in_pairs(dve, halves)

            def blk(ap, j):
                return ap[:, j * 512:(j + 1) * 512].rearrange("p (h d) -> p h d", d=LD)

            def tokens(s, w):
                dve.wait_ge(ffn_done, nth(0, w.it, s))
                V.tensor_scalar(xw[s][:, :], Y[:, w.pr * G + s, :], 1.0, None, ALU.mult).then_inc(l_y, 1)

            def square_sums(s, w, j):
                dve.wait_ge(l_sq, nth(0, w.it, s, 4, keys_first(j)))
                V.tensor_reduce(ssq[s][:, 8 * j:8 * j + 8], blk(SQ[s], j), AX.X, ALU.add).then_inc(l_ss, 1)

            def floors(s, w, j):
                dve.wait_ge(l_ss, nth(0, w.it, s, 4, keys_first(j)))
                part_ = ssq[s][:, 8 * j:8 * j + 8]
                V.tensor_scalar(part_, part_, 1e-24, QK_SCALE ** -2 if j < 2 else 1.0, ALU.max, ALU.mult).then_inc(l_ssf, 1)

            def rotated(s, w, j):
                hd = LD // 2
                factors = table[w.p][:, j // 2, :, :]
                if j == 2:
                    dve.wait_ge(tables_ready, w.l + 1)
                dve.wait_ge(l_sq, nth(0, w.it, s, 4, keys_first(j)))
                src = ps[s][:, j, :].rearrange("p (h d) -> p h d", d=LD)
                V.tensor_tensor(blk(RA[s], j), src, factors[:, 0:1, :].to_broadcast([S, 8, LD]), ALU.mult)
                for lo, other in ((0, hd), (hd, 0)):
                    last = V.tensor_tensor(blk(QR[s], j)[:, :, lo:lo + hd], src[:, :, other:other + hd],
                                           factors[:, 1:2, lo:lo + hd].to_broadcast([S, 8, hd]), ALU.mult)
                last.then_inc(l_rb, 1)

            def normalised(s, w, j):
                dve.wait_ge(l_rsum, nth(0, w.it, s, 4, keys_first(j)))
                dve.wait_ge(l_rn, nth(0, w.it, s, 4, keys_first(j)))
                V.tensor_tensor(blk(QR[s], j), blk(QR[s], j), rnq[s][:, 8 * j:8 * j + 8, None].to_broadcast([S, 8, LD]), ALU.mult).then_inc(l_kn, 1)

            def maxima(s, w, g):
                dve.wait_ge(l_sc_ps, nth(0, w.it, s, 4, g))
                V.tensor_reduce(mx[s][:, 4 * g:4 * g + 4], ps[s][:, g, :].rearrange("p (c n) -> p c n", n=S),
                                AX.X, ALU.max).then_inc(l_max, 1)

            def exponent_biases(s, w, g):
                dve.wait_ge(l_rn, nth(0, w.it, s, 4, keys_first(g % 2)))
                dve.wait_ge(l_max, nth(0, w.it, s, 4, g))
                rq = rnq[s][:, 0:LH].rearrange("p (c k) -> p c k", k=2)
                V.scalar_tensor_tensor(negmx[s][:, 4 * g:4 * g + 4], mx[s][:, 4 * g:4 * g + 4], -1.0,
                                       rq[:, (g % 2) * 4:(g % 2) * 4 + 4, g // 2], ALU.mult, ALU.mult).then_inc(l_shift, 1)

            def pv(s, g):
                return ps[s][:, g, 0:4 * 65].rearrange("p (c e) -> p c e", e=65)

            def inverse_sums(s, w, g):
                dve.wait_ge(l_pv_ps, nth(0, w.it, s, 4, g))
                V.reciprocal(rc[s][:, 4 * g:4 * g + 4], pv(s, g)[:, :, LD]).then_inc(l_rc, 1)

            def outputs(s, w, g):
                dve.wait_ge(l_rc, nth(0, w.it, s, 4, g))
                o = LO[s].rearrange("p (c k e) -> p c k e", k=2, e=LD)
                V.tensor_tensor(o[:, (g % 2) * 4:(g % 2) * 4 + 4, g // 2, :], pv(s, g)[:, :, 0:LD],
                                rc[s][:, 4 * g:4 * g + 4, None].to_broadcast([S, 4, LD]), ALU.mult).then_inc(l_o, 1)

            def first_residual(s, w):
                dve.wait_ge(l_att_ps, nth(0, w.it, s))
                V.tensor_tensor(y1[s], ps[s][:, 2, 0:D], xw[s][:, :], ALU.add).then_inc(l_y1, 1)

            def token_stats(s, w):
                dve.wait_ge(l_y1, nth(0, w.it, s))
                V.bn_stats(st[s][:, 0:6], y1[s][:, 0:64])

            def shift_stats(s, w):
                dve.wait_ge(l_sh_ps, nth(0, w.it, s))
                V.bn_stats(st[s][:, 6:12], ps[s][:, 3, 0:64]).then_inc(l_st, 1)

            def statistics(s, w):
                dve.wait_ge(x_loaded, 16)
                dve.wait_ge(l_st, nth(0, w.it, s))
                V.bn_aggr(mv[s][:, :], st[s][:, 0:12]).then_inc(l_mv, 1)

            def shifted_normed(s, w):
                dve.wait_ge(l_rs, nth(0, w.it, s))
                V.tensor_scalar(xn[s][:, 0:64], y1[s][:, 0:64], mv[s][:, 0:1], rs[s][:, 0:1],
                                ALU.subtract, ALU.mult).then_inc(l_xn, 1)
                V.tensor_scalar(xn[s][:, 64:128], ps[s][:, 3, 0:64], mv[s][:, 0:1], rs[s][:, 0:1],
                                ALU.subtract, ALU.mult).then_inc(l_xn, 1)

            def hidden(s, w):
                dve.wait_ge(lw_loaded[w.p], 144 * (w.lp + 1))
                dve.wait_ge(l_gate_ps, nth(0, w.it, s, 2, 1))
                for c, (lo, hi) in enumerate(HC):
                    dve.wait_ge(l_gelu, nth(0, w.it, s, 3, c))
                    V.scalar_tensor_tensor(hidT[s][0:hi - lo, c, :], ps[s][0:hi - lo, 2, c * S:(c + 1) * S],
                                           lcol[w.p][0:hi - lo, 2 + c:3 + c], geluT[s][0:hi - lo, c, :],
                                           ALU.add, ALU.mult).then_inc(l_hid, 1)

            def second_residual(s, w):
                dve.wait_ge(l_yb, nth(0, w.it, s))
                dve.wait_ge(l_ff_ps, nth(0, w.it, s))
                V.tensor_tensor(Y[:, w.pr * G + s, :], ps[s][:, 0, 128:256], yb[s], ALU.add).then_inc(ffn_done, 1)

            def halves(a, b):
                if a: tokens(*a)
                if b:
                    maxima(*b, 1)
                    exponent_biases(*b, 1)
                    maxima(*b, 2)
                    maxima(*b, 3)
                    exponent_biases(*b, 2)
                if a: square_sums(*a, 2)
                if b: exponent_biases(*b, 3)
                if a:
                    floors(*a, 2)
                    rotated(*a, 2)
                    rotated(*a, 3)
                    square_sums(*a, 3)
                    floors(*a, 3)
                if b:
                    inverse_sums(*b, 0)
                    outputs(*b, 0)
                if a: normalised(*a, 2)
                if b:
                    inverse_sums(*b, 1)
                    outputs(*b, 1)
                    inverse_sums(*b, 2)
                    outputs(*b, 2)
                    inverse_sums(*b, 3)
                    outputs(*b, 3)
                if a:
                    rotated(*a, 0)
                    rotated(*a, 1)
                if b: first_residual(*b)
                if a: normalised(*a, 3)
                if b:
                    token_stats(*b)
                    shift_stats(*b)
                    statistics(*b)
                    shifted_normed(*b)
                if a:
                    square_sums(*a, 0)
                    floors(*a, 0)
                    square_sums(*a, 1)
                    maxima(*a, 0)
                    floors(*a, 1)
                if b: hidden(*b)
                if a: exponent_biases(*a, 0)
                if b: second_residual(*b)

            def mixture(m):
                groups, quads = m["groups"], m["n"] * QUADS
                NG = len(groups)

                dve.wait_ge(x_updated, G + m["ln"])

                def behind(q):
                    keep_T(m["n"], q)
                    dve.wait_ge(r_lg_ps, quads + q + 1)
                    V.tensor_scalar(LG[:, q * 4:q * 4 + 4, :], ps[q % G][:, 1 + 2 * (q // G), 0:32].rearrange("p (b e) -> p b e", e=8),
                                    1.0, None, ALU.mult).then_inc(r_kept, 1)

                quad_norms(m["n"] + 1, normed_columns, behind)

                link = m["link0"]

                def over(t):
                    return t[:, :, None].to_broadcast([S, B, 8])

                ranks = rank[:, None, :].to_broadcast([S, B, 8])
                dve.wait_ge(r_kept, 2 * (quads + QUADS))
                if m["n"]:
                    V.tensor_tensor(LG[:, :, :], LG[:, :, :], moe2_rb[:, None, :].to_broadcast([S, B, 8]), ALU.add).then_inc(m_link, 1)
                    link += 2
                else:
                    V.tensor_reduce(BEST[:, :], LG[:, :, :], AX.X, ALU.max).then_inc(m_link, 1)
                    dve.wait_ge(m_link, link + 1)
                    V.tensor_tensor(LG[:, :, :], LG[:, :, :], over(BEST), ALU.subtract).then_inc(m_link, 1)
                    dve.wait_ge(m_link, link + 3)
                    V.tensor_reduce(BEST[:, :], PR[:, :, :], AX.X, ALU.add).then_inc(m_link, 1)
                    dve.wait_ge(m_link, link + 4)
                    V.reciprocal(PLACE[:, :], BEST[:, :]).then_inc(m_link, 1)
                    dve.wait_ge(m_link, link + 5)
                    V.tensor_tensor(PR[:, :, :], PR[:, :, :], over(PLACE), ALU.mult).then_inc(m_link, 1)
                    link += 6
                dve.wait_ge(m_link, link)
                for n, left in enumerate((PR, LEFT)):
                    V.tensor_reduce(BEST[:, :], left[:, :, :], AX.X, ALU.max).then_inc(m_link, 1)
                    dve.wait_ge(m_link, link + 1)
                    V.tensor_tensor(LG[:, :, :], left[:, :, :], over(BEST), ALU.is_equal).then_inc(m_link, 1)
                    dve.wait_ge(m_link, link + 2)
                    V.tensor_tensor(LG[:, :, :], LG[:, :, :], ranks, ALU.mult).then_inc(m_link, 1)
                    dve.wait_ge(m_link, link + 3)
                    V.tensor_reduce(PLACE[:, :], LG[:, :, :], AX.X, ALU.max).then_inc(m_link, 1)
                    dve.wait_ge(m_link, link + 4)
                    V.tensor_tensor(LG[:, :, :], LG[:, :, :], over(PLACE), ALU.is_equal).then_inc(m_link, 1)
                    dve.wait_ge(m_link, link + 5)
                    if n == 0:
                        V.tensor_tensor(RW[:, :, :], LG[:, :, :], PR[:, :, :], ALU.mult).then_inc(m_link, 1)
                        V.scalar_tensor_tensor(LEFT[:, :, :], LG[:, :, :], -4.0, PR[:, :, :], ALU.mult, ALU.add).then_inc(m_link, 1)
                        dve.wait_ge(m_link, link + 7)
                    else:
                        V.tensor_tensor(LG[:, :, :], LG[:, :, :], PR[:, :, :], ALU.mult).then_inc(m_link, 1)
                        dve.wait_ge(m_link, link + 6)
                        V.tensor_tensor(RW[:, :, :], RW[:, :, :], LG[:, :, :], ALU.add).then_inc(m_link, 1)
                        dve.wait_ge(m_link, link + 7)
                    link += 7
                if not m["n"]:
                    for _ in range(2):
                        V.tensor_reduce(BEST[:, :], RW[:, :, :], AX.X, ALU.add).then_inc(m_link, 1)
                        dve.wait_ge(m_link, link + 1)
                        V.tensor_scalar(BEST[:, :], BEST[:, :], 1e-9, None, ALU.add).then_inc(m_link, 1)
                        dve.wait_ge(m_link, link + 2)
                        V.reciprocal(PLACE[:, :], BEST[:, :]).then_inc(m_link, 1)
                        dve.wait_ge(m_link, link + 3)
                        V.tensor_tensor(RW[:, :, :], RW[:, :, :], over(PLACE), ALU.mult).then_inc(m_link, 1)
                        dve.wait_ge(m_link, link + 4)
                        link += 4

                def taken(s, it):
                    V.tensor_scalar(rw[s][:, :], RW[:, it * G + s, :], 1.0, None, ALU.mult).then_inc(m_rw, 1)

                def product(s, it, g):
                    dve.wait_ge(m_silu, m["group0"] + nth(0, it, s, NG, g))
                    V.tensor_tensor(AT[s][g % 2], SG[s][g % 2], ps[s][:, 2 + g % 2, 256:512], ALU.mult).then_inc(m_act, 1)

                def weighted(s, it, g):
                    if g == 0:
                        dve.wait_ge(m_rw, nth(m["n"] * B, it, s))
                    dve.wait_ge(m_dn_ps, m["group0"] + nth(0, it, s, NG, g))
                    for n, e in enumerate(groups[g]):
                        y = ps[s][:, g % 2, n * D:(n + 1) * D]
                        w = 1.0 if e < m["shared"] else rw[s][:, e - m["shared"]:e - m["shared"] + 1]
                        if e == 0:
                            op = V.tensor_scalar(acc[s], y, w, None, ALU.mult)
                        else:
                            dve.wait_ge(m_acc, m["expert0"] + nth(0, it, s, m["experts"], e - 1))
                            op = V.scalar_tensor_tensor(acc[s], y, w, acc[s], ALU.mult, ALU.add)
                        op.then_inc(m_acc, 1)

                def residual(s, it):
                    dve.wait_ge(m_acc, m["expert0"] + nth(0, it, s, m["experts"], m["experts"] - 1))
                    V.scalar_tensor_tensor(X[:, it * G + s, :], acc[s], m["gate"], X[:, it * G + s, :], ALU.mult, ALU.add).then_inc(x_updated, 1)

                def halves(a, b):
                    if a: taken(*a)
                    if b:
                        for g in range(NG):
                            product(*b, g)
                            if g: weighted(*b, g - 1)
                        weighted(*b, NG - 1)
                        residual(*b)

                in_pairs(dve, halves)

            def linear_attention():
                def q8(s):
                    return Q3[s].rearrange("p (h d) -> p h d", d=D3)

                def normalised(s, it):
                    dve.wait_ge(ln_rstd, nth(NB[LN3], it, s))
                    normed(s)

                def key_maxima(s, it):
                    dve.wait_ge(t_k, G + nth(0, it, s))
                    V.tensor_reduce(col[s][:, :], K3[s], AX.X, ALU.max).then_inc(t_klink, 1)

                def key_sums(s, it):
                    dve.wait_ge(t_kexp, nth(0, it, s))
                    V.tensor_reduce(rc[s][:, 0:4], K3E[s], AX.X, ALU.add).then_inc(o_recip, 1)
                    dve.wait_ge(o_recip, nth(24, it, s, 2, 0))
                    V.reciprocal(rc[s][:, 4:8], rc[s][:, 0:4]).then_inc(o_recip, 1)

                def query_stats(s, it):
                    dve.wait_ge(q_ps, nth(48, it, s))
                    V.bn_stats(st[s][:, 0:6], ps[s][:, 1, :]).then_inc(t_qlink, 1)
                    dve.compute_val(nth(0, it, s, 2, 0))
                    dve.wait_ge(x_loaded, 16)
                    dve.wait_ge(t_qlink, nth(0, it, s, 2, 0))
                    V.bn_aggr(mv[s][:, :], st[s][:, 0:6]).then_inc(t_qlink, 1)

                def query_gains(s, it):
                    dve.wait_ge(t_qlink, nth(0, it, s, 2, 1))
                    V.scalar_tensor_tensor(Q3[s], ps[s][:, 1, :], mv[s][:, 0:1], qg, ALU.subtract, ALU.mult).then_inc(t_qg, 1)

                def query_normed(s, it):
                    dve.wait_ge(t_qrs, nth(0, it, s))
                    dve.wait_ge(t_qg, nth(0, it, s, 3, 0))
                    V.scalar_tensor_tensor(Q3[s], Q3[s], rs[s][:, 0:1], qb, ALU.mult, ALU.add).then_inc(t_qg, 1)

                def query_maxima(s, it):
                    dve.wait_ge(t_qg, nth(0, it, s, 3, 1))
                    V.tensor_reduce(mx[s][:, 0:8], q8(s), AX.X, ALU.max).then_inc(t_qg, 1)

                def query_differences(s, it):
                    dve.wait_ge(t_qg, nth(0, it, s, 3, 2))
                    V.tensor_tensor(q8(s), q8(s), mx[s][:, 0:8, None].to_broadcast([S, 8, D3]), ALU.subtract).then_inc(t_qshift, 1)

                def query_sums(s, it):
                    dve.wait_ge(t_qexp, nth(0, it, s))
                    V.tensor_reduce(mx[s][:, 0:8], q8(s), AX.X, ALU.add).then_inc(sc_max, 1)
                    dve.wait_ge(sc_max, nth(96, it, s, 2, 0))
                    V.reciprocal(mx[s][:, 8:16], mx[s][:, 0:8]).then_inc(sc_max, 1)

                def cleared(s, it):
                    dve.wait_ge(t_c_ps, nth(0, it, s))
                    V.tensor_tensor(C3[s], ps[s][:, 3, :].rearrange("p (c n) -> p c n", n=D),
                                    blockpair[:, None, :].to_broadcast([D, 4, D]), ALU.mult).then_inc(t_c, 1)

                def outputs(s, it):
                    dve.wait_ge(sc_max, nth(96, it, s, 2, 1))
                    dve.wait_ge(t_o_ps, nth(0, it, s))
                    V.scalar_tensor_tensor(O3[s].rearrange("p (h e) -> p h e", e=D3), ps[s][:, 1, :].rearrange("p (h e) -> p h e", e=D3), 8.0,
                                           mx[s][:, 8:16, None].to_broadcast([S, 8, D3]), ALU.mult, ALU.mult).then_inc(o_ready, 1)

                def output_stats(s, it):
                    dve.wait_ge(o_ready, nth(48, it, s))
                    V.bn_stats(st[s][:, 0:6], O3[s]).then_inc(t_olink, 1)
                    dve.compute_val(nth(0, it, s, 2, 0))
                    dve.wait_ge(x_loaded, 16)
                    dve.wait_ge(t_olink, nth(0, it, s, 2, 0))
                    V.bn_aggr(mv[s][:, :], st[s][:, 0:6]).then_inc(t_olink, 1)

                def outputs_normed(s, it):
                    dve.wait_ge(t_ors, nth(0, it, s))
                    V.tensor_scalar(O3[s], O3[s], mv[s][:, 0:1], rs[s][:, 0:1], ALU.subtract, ALU.mult).then_inc(t_o, 1)

                def residual(s, it):
                    dve.wait_ge(t_y_ps, nth(0, it, s))
                    V.scalar_tensor_tensor(X[:, it * G + s, :], ps[s][:, 3, 0:D], gates[:, 0, 3:4], xw[s][:, :], ALU.mult, ALU.add).then_inc(x_updated, 1)

                def halves(a, b):
                    if a:
                        copied(LN3, *a)
                        statistics_x(LN3, *a)
                        aggregated_x(LN3, *a)
                    if b:
                        cleared(*b)
                        query_sums(*b)
                    if a:
                        normalised(*a)
                        key_maxima(*a)
                    if b:
                        outputs(*b)
                        output_stats(*b)
                    if a: query_stats(*a)
                    if b: outputs_normed(*b)
                    if a:
                        key_sums(*a)
                        query_gains(*a)
                        query_normed(*a)
                        query_maxima(*a)
                        query_differences(*a)
                    if b: residual(*b)

                in_pairs(dve, halves)

            def chosen_expert():
                def behind(q):
                    keep_T(2, q)
                    four = slice(q * 4, q * 4 + 4)
                    V.tensor_reduce(toksum[:, four], XNTQ[q].rearrange("p (b d) -> p b d", d=S), AX.X, ALU.add).then_inc(e_sum, 1)
                    dve.wait_ge(e_sum, q + 1)
                    V.tensor_scalar(tokmean[:, four], toksum[:, four], 1.0 / S, None, ALU.mult).then_inc(e_mean, 1)
                    dve.wait_ge(r_lg_ps, 2 * QUADS + q + 1)
                    V.tensor_tensor(LG[0:1, four, :], ps[q % G][0:1, 1 + 2 * (q // G), 0:32].rearrange("p (b e) -> p b e", e=8),
                                    moe3_rb[0:1, None, :].to_broadcast([1, 4, 8]), ALU.add).then_inc(r_kept, 1)

                dve.wait_ge(x_updated, G + LN3F)
                quad_norms(3, normed_columns, behind)
                dve.wait_ge(r_kept, 6 * QUADS)
                for n in range(B):
                    V.max(best8[0:1, n, :], LG[0:1, n, :]).then_inc(e_best, 1)
                dve.wait_ge(e_best, B)
                for n in range(B):
                    V.max_index(chosen[0:1, n, :], best8[0:1, n, :], LG[0:1, n, :]).then_inc(e_chosen, 1)

                def residual(j, q):
                    dve.wait_ge(m_dn_ps, GROUPS + q * 4 + j + 1)
                    V.tensor_tensor(acc[j % G], ps[j % G][:, 3, 0:D], FB2[j], ALU.add).then_inc(m_acc, 1)
                    dve.wait_ge(m_acc, EXPERTS + q * 4 + j + 1)
                    V.scalar_tensor_tensor(X[:, q * 4 + j, :], acc[j % G], gates[:, 1, 3:4], X[:, q * 4 + j, :], ALU.mult, ALU.add).then_inc(x_updated, 1)

                def halves(a, b):
                    if b: residual(*b)

                in_quads(dve, halves)

            V.memset(seed[:, :], 0.0).then_inc(x_updated, G)
            dve.wait_ge(x_updated, G)
            V.memset(seed[:, :], 0.0).then_inc(ffn_done, G)
            dve.wait_ge(x_loaded, 16)
            dve.wait_ge(w0_loaded, 96)
            dve.wait_ge(gates_ready, 1)
            V.tensor_copy(ident_b[:, :], ident[:, :]).then_inc(consts_cast, 1)
            V.tensor_copy(causal_b[:, :], causal[:, :]).then_inc(consts_cast, 1)
            attention(XA[0], 0)
            dve.wait_ge(w1_loaded, 176)
            V.tensor_copy(band_b[:, :], band_f[:, :]).then_inc(consts_cast, 1)
            dve.wait_ge(x_updated, G + LNY)
            quad_norms(0, lambda q, c: Y[:, q * 4 + c, :])
            dve.wait_ge(x_updated, G + LN1)
            local_transformer(dve, halves)
            dve.wait_ge(ffn_done, G + DEPTH * B)
            allx = lambda t: t[:, :, :].rearrange("p b d -> p (b d)")
            V.scalar_tensor_tensor(allx(X), allx(Y), gates[:, 1, 0:1], allx(X), ALU.mult, ALU.add).then_inc(ffn_gated, 1)
            dve.wait_ge(ffn_gated, 1)
            attention(XA[1], 1)
            mixture(MOE[0])
            dve.wait_ge(late_loaded, 288)
            V.tensor_tensor(side[:, :], side[:, :], side[:, :], ALU.add).then_inc(late_prep, 1)
            V.tensor_scalar(bq_s, bqkv[:, 0:1], 8 ** -0.5, None, ALU.mult).then_inc(late_prep, 1)
            dve.wait_ge(late_prep, 2)
            attention(XA[2], 2)
            mixture(MOE[1])
            linear_attention()
            chosen_expert()


def inputs_of(a):
    c = np.ascontiguousarray
    f = {k: np.asarray(v) for k, v in a.items()}
    col = lambda v: v.reshape(-1, 1)
    row = lambda v: v.reshape(1, -1)
    d = dict(constants())
    d["x"] = c(f["x"].transpose(1, 0, 2))
    d["ctxT"] = c(f["ctx_1024"].transpose(2, 0, 1))
    d["g_xattn"], d["g_ffn"] = row(f["g_xattn"]), row(f["g_ffn"])
    d["side"] = f["fside_SxS2_0"]
    w0 = np.zeros((D, 2, D), np.float32)
    for h in range(16):
        w0[h * 8:h * 8 + 8, 0, h * 8:h * 8 + 8] = f["L0_xattn_W1"].T
    w0[:, 1, :] = f["L0_xattn_W2"].T
    d["w0"] = w0
    d["q_scale"], d["k_scale"] = f["L0_ffn_q_scale"], f["L0_ffn_k_scale"]
    d["wqkv"] = f["L0_ffn_Wqkv"]
    d["wout"] = c(f["L0_ffn_Wo"].reshape(DEPTH, 8, 128, D).transpose(0, 2, 1, 3))
    d["wff1"], d["wff2"], d["bff2"] = f["L0_ffn_W1"], f["L0_ffn_W2"], f["L0_ffn_b2"]
    lcol = np.zeros((DEPTH, D, 8), np.float32)
    lcol[:, :, 0], lcol[:, :, 1] = f["L0_ffn_ln_g"], f["L0_ffn_ln_b"]
    for i, (lo, hi) in enumerate(HC):
        lcol[:, 0:hi - lo, 2 + i] = f["L0_ffn_b1"][:, lo:hi]
        lcol[:, 0:hi - lo, 5 + i] = f["L0_ffn_b1"][:, HID + lo:HID + hi]
    d["lcol"] = lcol
    chunks = lambda w: w.reshape(4, 128, D).transpose(1, 0, 2)
    d["w1"] = c(np.stack([f["L1_xattn_Wq"], f["L1_xattn_Wkv"][:, :512], f["L1_xattn_Wkv"][:, 512:],
                          chunks(f["L1_xattn_Wo"]).reshape(128, 512)], 1))
    d["aff1"] = c(np.stack([f["L1_xattn_ln_scale"], f["L1_xattn_ln_bias"]], 1))
    d["moe1_r"] = c(f["L1_ffn_gate_w"].T)
    d["moe1_gu"] = c(f["L1_ffn_gate_up_proj"].transpose(1, 0, 2))
    d["moe1_d"] = c(f["L1_ffn_down_proj"].transpose(1, 0, 2))
    wqkv = f["L2_xattn_Wqkv"]
    d["w2"] = c(np.stack([wqkv[:D].T, wqkv[D:2 * D].T, wqkv[2 * D:].T, f["L2_xattn_Wo"].T], 1))
    d["bqkv"] = c(f["L2_xattn_bqkv"].reshape(3, D).T)
    d["bo2"] = row(f["L2_xattn_bo"])
    both = lambda s, e: np.concatenate([f[s][None], f[e]], 0)
    d["moe2_g"] = c(both("L2_ffn_Wg_s", "L2_ffn_Wg").transpose(2, 0, 1))
    d["moe2_u"] = c(both("L2_ffn_Wu_s", "L2_ffn_Wu").transpose(2, 0, 1))
    d["moe2_d"] = c(both("L2_ffn_Wd_s", "L2_ffn_Wd").transpose(2, 0, 1).reshape(2, 128, E2, D).transpose(1, 2, 0, 3))
    d["moe2_r"], d["moe2_rb"] = c(f["L2_ffn_Wr"].T), row(f["L2_ffn_rb"])
    d["w3"] = c(np.stack([f["L3_xattn_Wq"], f["L3_xattn_Wkv"][:, :512], f["L3_xattn_Wkv"][:, 512:]], 1))
    d["w3o"] = c(chunks(f["L3_xattn_Wout"]))
    d["nullk"] = c(col(np.tile(f["L3_xattn_null_kv"][0], 2)))
    d["nullv"] = row(np.tile(f["L3_xattn_null_kv"][1], 8))
    d["qg"], d["qb"] = row(f["L3_xattn_ln_q_g"]), row(f["L3_xattn_ln_q_b"])
    d["og"], d["ob"] = c(f["L3_xattn_ln_out_g"].reshape(4, 128).T), c(f["L3_xattn_ln_out_b"].reshape(4, 128).T)
    d["moe3_r"], d["moe3_rb"] = f["L3_ffn_Wr"], row(f["L3_ffn_br"])
    d["moe3_w1"] = f["L3_ffn_W1"]
    d["moe3_w2"] = c(f["L3_ffn_W2"].reshape(8, 4, 128, D).transpose(0, 2, 1, 3))
    d["moe3_b1"] = c(f["L3_ffn_b1"].reshape(8, 4, 128).transpose(0, 2, 1))
    d["moe3_b2"] = f["L3_ffn_b2"]
    return {k: c(v) for k, v in d.items()}


def kernel(**inputs):
    import concourse.bacc as bacc
    from concourse.bass_utils import run_bass_kernel_spmd

    arrays = inputs_of(inputs)
    nc = bacc.Bacc("TRN2", target_bir_lowering=False, num_devices=1)
    dram = {k: nc.dram_tensor(f"in_{k}", v.shape, mybir.dt.from_np(v.dtype), kind="ExternalInput").ap() for k, v in arrays.items()}
    out = nc.dram_tensor("out_x", (S, B, D), F32, kind="ExternalOutput").ap()
    program(nc, dram, out)
    r = run_bass_kernel_spmd(nc, [{f"in_{k}": v for k, v in arrays.items()}], core_ids=[0])
    return np.ascontiguousarray(r.results[0]["out_x"].transpose(1, 0, 2))
```
